# Optimizing a Trainium2 kernel written in Bass

```python
import numpy as np
import jax
import jax.numpy as jnp

def _softmax(x, axis=-1):
    return jax.nn.softmax(x, axis=axis)

def _gelu(x):
    return jax.nn.gelu(x, approximate=True)

def _silu(x):
    return jax.nn.silu(x)

def _sigmoid(x):
    return jax.nn.sigmoid(x)

def _layernorm(x, axis=-1, eps=1e-05):
    m = jnp.mean(x, axis=axis, keepdims=True)
    v = jnp.var(x, axis=axis, keepdims=True)
    return (x - m) / jnp.sqrt(v + eps)

def _scatter_add(tgt, idx, src, axis=0):
    return tgt.at[idx].add(src)

def _segment_sum(src, seg, n):
    return jax.ops.segment_sum(src, seg, n)
kernel_name = 'mk_sandwich_d2_jaxref_r8_a717bb'

def setup_inputs(seed: int=0):
    np.random.seed(seed)
    _w = jnp.asarray

    def _L0_attn_setup():
        import jax, jax.numpy as jnp
        import numpy as np
        D_MODEL = 128
        N_HEADS = 16
        HEAD_DIM = D_MODEL // N_HEADS
        N_EXPERTS = 4
        HIDDEN = 4 * D_MODEL
        B, T = (1, 256)

        def _apply_rope(x, sin, cos):
            x1, x2 = (x[..., ::2], x[..., 1::2])
            r1 = x1 * cos - x2 * sin
            r2 = x1 * sin + x2 * cos
            return jnp.stack((r1, r2), axis=-1).reshape(x.shape)
        key = jax.random.key(seed)
        ks = jax.random.split(key, 16)
        s = 0.02
        d, E, Hd = (D_MODEL, N_EXPERTS, HIDDEN)
        return {'x': jax.random.normal(ks[0], (B, T, d), dtype=jnp.float32), 'w_dw': jax.random.normal(ks[1], (d, 3), dtype=jnp.float32) * s, 'w_pw': jax.random.normal(ks[2], (d, d), dtype=jnp.float32) * s, 'w_qkv': jax.random.normal(ks[3], (3 * d, d), dtype=jnp.float32) * s, 'w_o': jax.random.normal(ks[4], (d, d), dtype=jnp.float32) * s, 'w_gate': jax.random.normal(ks[5], (d, d), dtype=jnp.float32) * s, 'b_gate': jnp.zeros((d,), dtype=jnp.float32), 'ln_g': jnp.ones((d,), dtype=jnp.float32), 'ln_b': jnp.zeros((d,), dtype=jnp.float32), 'w_moe_gate': jax.random.normal(ks[6], (E, d), dtype=jnp.float32) * s, 'w1': jax.random.normal(ks[7], (E, Hd, d), dtype=jnp.float32) * s, 'b1': jnp.zeros((E, Hd), dtype=jnp.float32), 'w2': jax.random.normal(ks[8], (E, d, Hd), dtype=jnp.float32) * s, 'b2': jnp.zeros((E, d), dtype=jnp.float32)}
    _L0_attn_in = _L0_attn_setup()

    def _L0_ffn_setup():
        import jax, jax.numpy as jnp
        import numpy as np
        FP4_LUT = jnp.array([0.0, 0.5, 1.0, 1.5, 2.0, 3.0, 4.0, 6.0, -0.0, -0.5, -1.0, -1.5, -2.0, -3.0, -4.0, -6.0], dtype=jnp.float32)
        BLOCK = 32
        TOP_K = 2

        def dequant_mxfp4(blocks, scales):
            b = blocks.astype(jnp.int32)
            lo = b & 15
            hi = b >> 4 & 15
            nib = jnp.stack([lo, hi], axis=-1).reshape(blocks.shape[:-1] + (blocks.shape[-1] * 2,))
            vals = FP4_LUT[nib]
            s = jnp.exp2(scales.astype(jnp.float32) - 127.0)
            s = jnp.repeat(s, BLOCK, axis=-1)
            return vals * s
        key = jax.random.key(seed)
        ks = jax.random.split(key, 8)
        E, H, F, B, S = (16, 128, 256, 1, 128)
        hidden_states = jax.random.normal(ks[0], (B, S, H), dtype=jnp.float32)
        router_w = jax.random.normal(ks[1], (E, H), dtype=jnp.float32) * 0.05
        blocks_gu = jax.random.randint(ks[2], (E, 2 * F, H // 2), 0, 32, dtype=jnp.int32)
        scales_gu = jax.random.randint(ks[3], (E, 2 * F, H // BLOCK), 118, 130, dtype=jnp.int32)
        bias_gu = jax.random.normal(ks[4], (E, 2 * F), dtype=jnp.float32) * 0.02
        blocks_down = jax.random.randint(ks[5], (E, H, F // 2), 0, 32, dtype=jnp.int32)
        scales_down = jax.random.randint(ks[6], (E, H, F // BLOCK), 118, 130, dtype=jnp.int32)
        bias_down = jax.random.normal(ks[7], (E, H), dtype=jnp.float32) * 0.02
        return {'hidden_states': hidden_states, 'router_w': router_w, 'bias_gu': bias_gu, 'bias_down': bias_down, 'blocks_gu': blocks_gu, 'scales_gu': scales_gu, 'blocks_down': blocks_down, 'scales_down': scales_down}
    _L0_ffn_in = _L0_ffn_setup()

    def _L1_attn_setup():
        import jax, jax.numpy as jnp
        import numpy as np
        import math
        HIDDEN = 128
        NUM_LAYERS = 24
        INIT_RANGE = 0.02
        key = jax.random.key(seed)
        k1, k2 = jax.random.split(key)
        B, S, H = (4, 512, HIDDEN)
        hidden_states = jax.random.normal(k1, (B, S, H), dtype=jnp.float32)
        std = INIT_RANGE / math.sqrt(2.0 * NUM_LAYERS * H)
        W_q = jax.random.normal(k2, (H, H), dtype=jnp.float32) * std
        return {'hidden_states': hidden_states, 'W_q': W_q}
    _L1_attn_in = _L1_attn_setup()

    def _L1_ffn_setup():
        import jax, jax.numpy as jnp
        import numpy as np
        DIM = 128
        DEPTH = 6
        HEADS = 16
        DIM_HEAD = 64
        WINDOW = 32
        INNER = HEADS * DIM_HEAD
        DIM_INNER = int(DIM * 4 * 2 / 3)
        QK_SCALE = 8.0

        def shift_tokens(t):
            a, s = jnp.split(t, 2, -1)
            s = jnp.pad(s, ((0, 0), (1, 0), (0, 0)))[:, :-1]
            return jnp.concatenate([a, s], -1)

        def l2norm(t):
            return t / jnp.maximum(jnp.linalg.norm(t, axis=-1, keepdims=True), 1e-12)

        def rotate_half(x):
            x1, x2 = jnp.split(x, 2, -1)
            return jnp.concatenate([-x2, x1], -1)

        def rotary_tables(n):
            half = jnp.arange(0, DIM_HEAD, 2, dtype=jnp.float32)
            inv_freq = 1.0 / 10000.0 ** (half / DIM_HEAD)
            t = jnp.arange(n, dtype=jnp.float32)
            freqs = t[:, None] * inv_freq[None, :]
            freqs = jnp.concatenate([freqs, freqs], -1)
            base_scale = (half + 0.4 * DIM_HEAD) / (1.4 * DIM_HEAD)
            power = (t - n // 2) / (WINDOW // 2)
            scale = base_scale[None, :] ** power[:, None]
            scale = jnp.concatenate([scale, scale], -1)
            return (freqs, scale)

        def local_attention(q, k, v):
            b, h, n, d = q.shape
            w = WINDOW
            nw = n // w
            bq = q.reshape(b, h, nw, w, d)
            bk = k.reshape(b, h, nw, w, d)
            bv = v.reshape(b, h, nw, w, d)

            def look(t):
                p = jnp.pad(t, ((0, 0), (0, 0), (1, 0), (0, 0), (0, 0)))
                return jnp.concatenate([p[:, :, :nw], p[:, :, 1:]], axis=3)
            bk2, bv2 = (look(bk), look(bv))
            seq = jnp.arange(n).reshape(nw, w)
            seq_p = jnp.pad(seq, ((1, 0), (0, 0)), constant_values=-1)
            jt = jnp.concatenate([seq_p[:nw], seq_p[1:]], axis=1)
            it = seq[:, :, None]
            jb = jt[:, None, :]
            mask = (it < jb) | (it > jb + w) | (jb == -1)
            sim = jnp.einsum('bhwie,bhwje->bhwij', bq, bk2) * QK_SCALE
            sim = jnp.where(mask, -jnp.finfo(sim.dtype).max, sim)
            attn = jax.nn.softmax(sim, -1)
            out = jnp.einsum('bhwij,bhwje->bhwie', attn, bv2)
            return out.reshape(b, h, n, d)

        def attn_layer(x, Wqkv, qs, ksc, Wo):
            b, n, _ = x.shape
            qkv = x @ Wqkv
            q, k, v = jnp.split(qkv, 3, -1)
            sh = lambda t: t.reshape(b, n, HEADS, DIM_HEAD).transpose(0, 2, 1, 3)
            q, k, v = (sh(q), sh(k), sh(v))
            q = l2norm(q) * qs
            k = l2norm(k) * ksc
            freqs, scale = rotary_tables(n)
            cos, sin = (jnp.cos(freqs), jnp.sin(freqs))
            q = q * cos * scale + rotate_half(q) * sin * scale
            inv = 1.0 / scale
            k = k * cos * inv + rotate_half(k) * sin * inv
            out = local_attention(q, k, v)
            out = out.transpose(0, 2, 1, 3).reshape(b, n, INNER)
            return out @ Wo

        def ffn_layer(x, g, bln, W1, b1, W2, b2):
            mu = x.mean(-1, keepdims=True)
            var = ((x - mu) ** 2).mean(-1, keepdims=True)
            xn = (x - mu) / jnp.sqrt(var + 1e-05) * g + bln
            hg = xn @ W1 + b1
            a, gate = jnp.split(hg, 2, -1)
            return a * jax.nn.gelu(gate, approximate=False) @ W2 + b2
        key = jax.random.key(seed)
        ks = jax.random.split(key, 8)
        B, N = (2, 256)
        init = lambda k, shape: jax.random.normal(k, shape, jnp.float32) * 0.02
        return {'x': jax.random.normal(ks[0], (B, N, DIM), jnp.float32), 'Wqkv': init(ks[1], (DEPTH, DIM, 3 * INNER)), 'q_scale': jnp.ones((DEPTH, DIM_HEAD), jnp.float32), 'k_scale': jnp.ones((DEPTH, DIM_HEAD), jnp.float32), 'Wo': init(ks[2], (DEPTH, INNER, DIM)), 'ln_g': jnp.ones((DEPTH, DIM), jnp.float32), 'ln_b': jnp.zeros((DEPTH, DIM), jnp.float32), 'W1': init(ks[3], (DEPTH, DIM, 2 * DIM_INNER)), 'b1': jnp.zeros((DEPTH, 2 * DIM_INNER), jnp.float32), 'W2': init(ks[4], (DEPTH, DIM_INNER, DIM)), 'b2': jnp.zeros((DEPTH, DIM), jnp.float32)}
    _L1_ffn_in = _L1_ffn_setup()
    _d = {'L0_attn_x': _L0_attn_in['x'], 'L0_attn_w_dw': _L0_attn_in['w_dw'], 'L0_attn_w_pw': _L0_attn_in['w_pw'], 'L0_attn_w_qkv': _L0_attn_in['w_qkv'], 'L0_attn_w_o': _L0_attn_in['w_o'], 'L0_attn_w_gate': _L0_attn_in['w_gate'], 'L0_attn_b_gate': _L0_attn_in['b_gate'], 'L0_attn_ln_g': _L0_attn_in['ln_g'], 'L0_attn_ln_b': _L0_attn_in['ln_b'], 'L0_attn_w_moe_gate': _L0_attn_in['w_moe_gate'], 'L0_attn_w1': _L0_attn_in['w1'], 'L0_attn_b1': _L0_attn_in['b1'], 'L0_attn_w2': _L0_attn_in['w2'], 'L0_attn_b2': _L0_attn_in['b2'], 'L0_ffn_router_w': _L0_ffn_in['router_w'], 'L0_ffn_bias_gu': _L0_ffn_in['bias_gu'], 'L0_ffn_bias_down': _L0_ffn_in['bias_down'], 'L0_ffn_blocks_gu': _L0_ffn_in['blocks_gu'], 'L0_ffn_scales_gu': _L0_ffn_in['scales_gu'], 'L0_ffn_blocks_down': _L0_ffn_in['blocks_down'], 'L0_ffn_scales_down': _L0_ffn_in['scales_down'], 'L1_attn_W_q': _L1_attn_in['W_q'], 'L1_ffn_Wqkv': _L1_ffn_in['Wqkv'], 'L1_ffn_q_scale': _L1_ffn_in['q_scale'], 'L1_ffn_k_scale': _L1_ffn_in['k_scale'], 'L1_ffn_Wo': _L1_ffn_in['Wo'], 'L1_ffn_ln_g': _L1_ffn_in['ln_g'], 'L1_ffn_ln_b': _L1_ffn_in['ln_b'], 'L1_ffn_W1': _L1_ffn_in['W1'], 'L1_ffn_b1': _L1_ffn_in['b1'], 'L1_ffn_W2': _L1_ffn_in['W2'], 'L1_ffn_b2': _L1_ffn_in['b2']}
    _x0 = _d['L0_attn_x']
    _d['L0_attn_x'] = jax.random.normal(jax.random.fold_in(jax.random.key(seed), 1), (2, 2048, 128), dtype=_x0.dtype)
    del _x0
    return _d

def reference(L0_attn_x, L0_attn_w_dw, L0_attn_w_pw, L0_attn_w_qkv, L0_attn_w_o, L0_attn_w_gate, L0_attn_b_gate, L0_attn_ln_g, L0_attn_ln_b, L0_attn_w_moe_gate, L0_attn_w1, L0_attn_b1, L0_attn_w2, L0_attn_b2, L0_ffn_router_w, L0_ffn_bias_gu, L0_ffn_bias_down, L0_ffn_blocks_gu, L0_ffn_scales_gu, L0_ffn_blocks_down, L0_ffn_scales_down, L1_attn_W_q, L1_ffn_Wqkv, L1_ffn_q_scale, L1_ffn_k_scale, L1_ffn_Wo, L1_ffn_ln_g, L1_ffn_ln_b, L1_ffn_W1, L1_ffn_b1, L1_ffn_W2, L1_ffn_b2):

    def _L0_attn_ref(x, w_dw, w_pw, w_qkv, w_o, w_gate, b_gate, ln_g, ln_b, w_moe_gate, w1, b1, w2, b2):
        import jax, jax.numpy as jnp
        import numpy as np
        D_MODEL = 128
        N_HEADS = 16
        HEAD_DIM = D_MODEL // N_HEADS
        N_EXPERTS = 4
        HIDDEN = 4 * D_MODEL
        B, T = (1, 256)

        def _apply_rope(x, sin, cos):
            x1, x2 = (x[..., ::2], x[..., 1::2])
            r1 = x1 * cos - x2 * sin
            r2 = x1 * sin + x2 * cos
            return jnp.stack((r1, r2), axis=-1).reshape(x.shape)
        Bv, Tv, d = x.shape
        H, Dh = (N_HEADS, HEAD_DIM)
        dt = x.dtype
        xp = jnp.pad(x, ((0, 0), (2, 0), (0, 0)))
        y = xp[:, 0:Tv] * w_dw[:, 0] + xp[:, 1:Tv + 1] * w_dw[:, 1] + xp[:, 2:Tv + 2] * w_dw[:, 2]
        y = jnp.einsum('btd,ed->bte', y, w_pw)
        x = x + y
        qkv = jnp.einsum('btd,ed->bte', x, w_qkv).reshape(Bv, Tv, 3, H, Dh)
        q, k, v = (qkv[:, :, 0], qkv[:, :, 1], qkv[:, :, 2])
        inv_freq = 1.0 / 10000.0 ** (jnp.arange(0, Dh, 2, dtype=dt) / Dh)
        pos = jnp.arange(Tv, dtype=dt)
        theta = pos[:, None] * inv_freq[None, :]
        sin = jnp.sin(theta)[None, :, None, :]
        cos = jnp.cos(theta)[None, :, None, :]
        q = _apply_rope(q, sin, cos)
        k = _apply_rope(k, sin, cos)
        q_phi = jax.nn.elu(q) + 1.0
        k_phi = jax.nn.elu(k) + 1.0
        kv = k_phi[..., :, None] * v[..., None, :]
        kv_prefix = jnp.cumsum(kv, axis=1)
        k_prefix = jnp.cumsum(k_phi, axis=1)
        num = jnp.einsum('bthd,bthdm->bthm', q_phi, kv_prefix)
        denom = jnp.sum(q_phi * k_prefix, axis=-1, keepdims=True)
        attn = num / (denom + 1e-06)
        attn = attn.reshape(Bv, Tv, d)
        attn = jnp.einsum('btd,ed->bte', attn, w_o)
        delta = x - jnp.concatenate([x[:, :1], x[:, :-1]], axis=1)
        gate = jax.nn.sigmoid(jnp.einsum('btd,ed->bte', delta, w_gate) + b_gate)
        x = x + gate * attn
        mu = jnp.mean(x, axis=-1, keepdims=True)
        var = jnp.mean((x - mu) ** 2, axis=-1, keepdims=True)
        h = (x - mu) / jnp.sqrt(var + 1e-05) * ln_g + ln_b
        gw = jax.nn.softmax(jnp.einsum('btd,ed->bte', h, w_moe_gate), axis=-1)
        hid = jax.nn.silu(jnp.einsum('btd,efd->btef', h, w1) + b1)
        eo = jnp.einsum('btef,edf->bted', hid, w2) + b2
        ffn = jnp.einsum('bte,bted->btd', gw, eo)
        return x + ffn

    def _L0_ffn_ref(hidden_states, router_w, bias_gu, bias_down, blocks_gu, scales_gu, blocks_down, scales_down):
        import jax, jax.numpy as jnp
        import numpy as np
        FP4_LUT = jnp.array([0.0, 0.5, 1.0, 1.5, 2.0, 3.0, 4.0, 6.0, -0.0, -0.5, -1.0, -1.5, -2.0, -3.0, -4.0, -6.0], dtype=jnp.float32)
        BLOCK = 32
        TOP_K = 2

        def dequant_mxfp4(blocks, scales):
            b = blocks.astype(jnp.int32)
            lo = b & 15
            hi = b >> 4 & 15
            nib = jnp.stack([lo, hi], axis=-1).reshape(blocks.shape[:-1] + (blocks.shape[-1] * 2,))
            vals = FP4_LUT[nib]
            s = jnp.exp2(scales.astype(jnp.float32) - 127.0)
            s = jnp.repeat(s, BLOCK, axis=-1)
            return vals * s
        B, S, H = hidden_states.shape
        flat = hidden_states.reshape(-1, H)
        T = flat.shape[0]
        E = router_w.shape[0]
        logits = flat @ router_w.T
        top_vals, top_idx = jax.lax.top_k(logits, TOP_K)
        weights = jax.nn.softmax(top_vals, axis=-1).astype(flat.dtype)
        combine = jnp.zeros((T, E), flat.dtype).at[jnp.arange(T)[:, None], top_idx].set(weights)
        w_gu = dequant_mxfp4(blocks_gu, scales_gu)
        w_down = dequant_mxfp4(blocks_down, scales_down)
        gu = jnp.einsum('th,eoh->eto', flat, w_gu) + bias_gu[:, None, :]
        gate, up = jnp.split(gu, 2, axis=-1)
        h = jax.nn.silu(gate) * up
        y = jnp.einsum('etf,ehf->eth', h, w_down) + bias_down[:, None, :]
        out = jnp.einsum('eth,te->th', y, combine)
        return out.reshape(B, S, H)

    def _L1_attn_ref(hidden_states, W_q):
        import jax, jax.numpy as jnp
        import numpy as np
        import math
        HIDDEN = 128
        NUM_LAYERS = 24
        INIT_RANGE = 0.02
        q = jnp.einsum('bsh,oh->bso', hidden_states, W_q)
        pre_attn = jnp.einsum('bso,bto->bst', q, hidden_states)
        attention = jnp.einsum('bst,bth->bsh', pre_attn, hidden_states)
        return attention

    def _L1_ffn_ref(x, Wqkv, q_scale, k_scale, Wo, ln_g, ln_b, W1, b1, W2, b2):
        import jax, jax.numpy as jnp
        import numpy as np
        DIM = 128
        DEPTH = 6
        HEADS = 16
        DIM_HEAD = 64
        WINDOW = 32
        INNER = HEADS * DIM_HEAD
        DIM_INNER = int(DIM * 4 * 2 / 3)
        QK_SCALE = 8.0

        def shift_tokens(t):
            a, s = jnp.split(t, 2, -1)
            s = jnp.pad(s, ((0, 0), (1, 0), (0, 0)))[:, :-1]
            return jnp.concatenate([a, s], -1)

        def l2norm(t):
            return t / jnp.maximum(jnp.linalg.norm(t, axis=-1, keepdims=True), 1e-12)

        def rotate_half(x):
            x1, x2 = jnp.split(x, 2, -1)
            return jnp.concatenate([-x2, x1], -1)

        def rotary_tables(n):
            half = jnp.arange(0, DIM_HEAD, 2, dtype=jnp.float32)
            inv_freq = 1.0 / 10000.0 ** (half / DIM_HEAD)
            t = jnp.arange(n, dtype=jnp.float32)
            freqs = t[:, None] * inv_freq[None, :]
            freqs = jnp.concatenate([freqs, freqs], -1)
            base_scale = (half + 0.4 * DIM_HEAD) / (1.4 * DIM_HEAD)
            power = (t - n // 2) / (WINDOW // 2)
            scale = base_scale[None, :] ** power[:, None]
            scale = jnp.concatenate([scale, scale], -1)
            return (freqs, scale)

        def local_attention(q, k, v):
            b, h, n, d = q.shape
            w = WINDOW
            nw = n // w
            bq = q.reshape(b, h, nw, w, d)
            bk = k.reshape(b, h, nw, w, d)
            bv = v.reshape(b, h, nw, w, d)

            def look(t):
                p = jnp.pad(t, ((0, 0), (0, 0), (1, 0), (0, 0), (0, 0)))
                return jnp.concatenate([p[:, :, :nw], p[:, :, 1:]], axis=3)
            bk2, bv2 = (look(bk), look(bv))
            seq = jnp.arange(n).reshape(nw, w)
            seq_p = jnp.pad(seq, ((1, 0), (0, 0)), constant_values=-1)
            jt = jnp.concatenate([seq_p[:nw], seq_p[1:]], axis=1)
            it = seq[:, :, None]
            jb = jt[:, None, :]
            mask = (it < jb) | (it > jb + w) | (jb == -1)
            sim = jnp.einsum('bhwie,bhwje->bhwij', bq, bk2) * QK_SCALE
            sim = jnp.where(mask, -jnp.finfo(sim.dtype).max, sim)
            attn = jax.nn.softmax(sim, -1)
            out = jnp.einsum('bhwij,bhwje->bhwie', attn, bv2)
            return out.reshape(b, h, n, d)

        def attn_layer(x, Wqkv, qs, ksc, Wo):
            b, n, _ = x.shape
            qkv = x @ Wqkv
            q, k, v = jnp.split(qkv, 3, -1)
            sh = lambda t: t.reshape(b, n, HEADS, DIM_HEAD).transpose(0, 2, 1, 3)
            q, k, v = (sh(q), sh(k), sh(v))
            q = l2norm(q) * qs
            k = l2norm(k) * ksc
            freqs, scale = rotary_tables(n)
            cos, sin = (jnp.cos(freqs), jnp.sin(freqs))
            q = q * cos * scale + rotate_half(q) * sin * scale
            inv = 1.0 / scale
            k = k * cos * inv + rotate_half(k) * sin * inv
            out = local_attention(q, k, v)
            out = out.transpose(0, 2, 1, 3).reshape(b, n, INNER)
            return out @ Wo

        def ffn_layer(x, g, bln, W1, b1, W2, b2):
            mu = x.mean(-1, keepdims=True)
            var = ((x - mu) ** 2).mean(-1, keepdims=True)
            xn = (x - mu) / jnp.sqrt(var + 1e-05) * g + bln
            hg = xn @ W1 + b1
            a, gate = jnp.split(hg, 2, -1)
            return a * jax.nn.gelu(gate, approximate=False) @ W2 + b2
        for i in range(DEPTH):
            x = attn_layer(shift_tokens(x), Wqkv[i], q_scale[i], k_scale[i], Wo[i]) + x
            x = ffn_layer(shift_tokens(x), ln_g[i], ln_b[i], W1[i], b1[i], W2[i], b2[i]) + x
        return x
    x = L0_attn_x
    x = x + _layernorm(_L0_attn_ref(_layernorm(x, axis=-1), L0_attn_w_dw, L0_attn_w_pw, L0_attn_w_qkv, L0_attn_w_o, L0_attn_w_gate, L0_attn_b_gate, L0_attn_ln_g, L0_attn_ln_b, L0_attn_w_moe_gate, L0_attn_w1, L0_attn_b1, L0_attn_w2, L0_attn_b2), axis=-1)
    x = x + _layernorm(_L0_ffn_ref(_layernorm(x, axis=-1), L0_ffn_router_w, L0_ffn_bias_gu, L0_ffn_bias_down, L0_ffn_blocks_gu, L0_ffn_scales_gu, L0_ffn_blocks_down, L0_ffn_scales_down), axis=-1)
    x = x + _layernorm(_L1_attn_ref(_layernorm(x, axis=-1), L1_attn_W_q), axis=-1)
    x = x + _layernorm(_L1_ffn_ref(_layernorm(x, axis=-1), L1_ffn_Wqkv, L1_ffn_q_scale, L1_ffn_k_scale, L1_ffn_Wo, L1_ffn_ln_g, L1_ffn_ln_b, L1_ffn_W1, L1_ffn_b1, L1_ffn_W2, L1_ffn_b2), axis=-1)
    return x

_drawn_inputs = setup_inputs


def setup_inputs(seed=0):
    import zlib

    import numpy as np

    out = dict(_drawn_inputs(seed))
    spreads = {'L0_attn_b_gate': (0.0, 0.8),
     'L0_attn_ln_g': (1.0, 0.578),
     'L0_attn_ln_b': (0.0, 0.355),
     'L0_attn_b1': (0.0, 0.1),
     'L0_attn_b2': (0.0, 0.1),
     'L1_ffn_q_scale': (1.0, 0.6),
     'L1_ffn_k_scale': (1.0, 0.6),
     'L1_ffn_ln_g': (1.0, 0.6),
     'L1_ffn_ln_b': (0.0, 0.8),
     'L1_ffn_b1': (0.0, 0.8),
     'L1_ffn_b2': (0.0, 0.8)}
    factors = {'L0_attn_w_qkv': 5.867,
     'L0_attn_w_o': 6.977,
     'L0_attn_w_gate': 8.0,
     'L0_ffn_bias_gu': 64.0,
     'L0_ffn_bias_down': 64.0,
     'L1_ffn_W1': 6.444,
     'L1_ffn_W2': 6.323}
    for name, (base, spread) in spreads.items():
        noise = np.random.default_rng([zlib.crc32(name.encode()), seed]).standard_normal(out[name].shape)
        drawn = base * np.exp(spread * noise) if base else spread * noise
        out[name] = jnp.asarray(drawn.astype(out[name].dtype))
    for name, factor in factors.items():
        out[name] = (out[name] * factor).astype(out[name].dtype)
    return out
```

```python
from contextlib import ExitStack

import concourse.bass as bass
import numpy as np
from concourse import mybir

ALU = mybir.AluOpType
ACT = mybir.ActivationFunctionType
AX = mybir.AxisListType
F32 = mybir.dt.float32
F32R = mybir.dt.float32r
BF16 = mybir.dt.bfloat16
I32 = mybir.dt.int32

P = 128
D = 128
B = 2
T = 2048
J = T // P
N_TILES = B * J
G4 = 4
GROUPS = N_TILES // G4
LN_EPS = 1e-5
RSQRT_MAGIC = 0x5F3759DF
DMA = 16


class Memory:

    taken = []

    def __init__(self, nc, ctx, tag):
        self.nc, self.ctx, self.tag = nc, ctx, tag

    def sb(self, name, shape, dtype=F32):
        return self.ctx.enter_context(self.nc.sbuf_tensor(f"{self.tag}_{name}", list(shape), dtype))

    def bank(self, name, dtype=F32):
        return self.ctx.enter_context(self.nc.psum_tensor(f"{self.tag}_{name}_ps", [P, 512], dtype))

    def sem(self, name):
        semaphore = self.nc.alloc_semaphore(f"{self.tag}_{name}")
        self.taken.append(semaphore)
        return semaphore


def release_semaphores(nc):
    nc.clear_and_free_semaphores(Memory.taken)
    Memory.taken.clear()
    nc.all_engine_barrier()


def upto(index, per=1, k=0):
    return index * per + (k + 1)


RSQRT_STEPS = 11


def rsqrt_steps(nc, vec, x, y, t, magic, steps, done, waits_met):
    nc.vector.tensor_scalar(y.bitcast(I32), x.bitcast(I32), 1, -1, ALU.logical_shift_right,
                            ALU.bitwise_xor).then_inc(steps, 1)
    vec.wait_ge(steps, done + 1)
    vec.sem_inc(waits_met)
    nc.vector.tensor_tensor(t.bitcast(I32), y.bitcast(I32), magic, ALU.add).then_inc(steps, 1)
    a, b = t, y
    for k in (2, 5, 8):
        vec.wait_ge(steps, done + k)
        nc.vector.tensor_tensor(b, a, a, ALU.mult).then_inc(steps, 1)
        vec.wait_ge(steps, done + (k + 1))
        nc.vector.scalar_tensor_tensor(b, b, -0.5, x, ALU.mult, ALU.mult).then_inc(steps, 1)
        vec.wait_ge(steps, done + (k + 2))
        nc.vector.scalar_tensor_tensor(b, b, 1.5, a, ALU.add, ALU.mult).then_inc(steps, 1)
        a, b = b, a



def normalise_rows(nc, ctx, tag, x, xn, xT, ident, even_first=False, scale=None, bias=None):
    m = Memory(nc, ctx, tag)
    stats = m.sb("stats", [P, N_TILES, 6])
    mv = m.sb("mv", [P, N_TILES, 2])
    ve = m.sb("var_eps", [P, N_TILES])
    rstd = m.sb("rstd", [P, N_TILES])
    tmp = m.sb("tmp", [P, N_TILES])
    magic = m.sb("magic", [P, N_TILES], I32)
    banks = [m.bank(f"T{i}") for i in range(4)]
    magic_set, stat, steps, waits_met, rows_ready, T_ps, T_out = (
        m.sem(s) for s in ("magic_set", "stat", "steps", "waits_met", "rows_ready", "T_ps", "T_out"))

    with nc.Block() as block:
        @block.vector
        def _(v):
            nc.vector.memset(magic[:], RSQRT_MAGIC + 1).then_inc(magic_set, 1)
            for n in range(N_TILES):
                nc.vector.bn_stats(stats[:, n, :], x[:, n, :]).then_inc(stat, 1)
            v.wait_ge(stat, N_TILES)
            for n in range(N_TILES):
                nc.vector.bn_aggr(mv[:, n, :], stats[:, n, :]).then_inc(stat, 1)
            v.wait_ge(stat, 2 * N_TILES)
            nc.vector.tensor_scalar(ve[:], mv[:, :, 1], LN_EPS, None, ALU.add).then_inc(stat, 1)
            v.wait_ge(stat, 2 * N_TILES + 1)
            v.wait_ge(magic_set, 1)
            rsqrt_steps(nc, v, ve[:], rstd[:], tmp[:], magic[:], steps, 0, waits_met)
            v.wait_ge(steps, RSQRT_STEPS)
            for n in range(N_TILES):
                dst, src = xn[:, n, :], x[:, n, :]
                if even_first:
                    dst = dst.rearrange("p (two k) -> p k two", two=2)
                    src = src.rearrange("p (k two) -> p k two", two=2)
                nc.vector.tensor_scalar(dst, src, mv[:, n, 0:1], rstd[:, n:n + 1], ALU.subtract, ALU.mult
                                        ).then_inc(rows_ready, 1)

        @block.tensor
        def _(pe):
            for g in range(GROUPS):
                pe.wait_ge(rows_ready, G4 * (g + 1))
                if g >= 4:
                    pe.wait_ge(T_out, G4 * (g - 3))
                for t in range(G4):
                    last = nc.tensor.transpose(banks[g % 4][:, t * P:(t + 1) * P], xn[:, G4 * g + t, :], ident[:])
                last.then_inc(T_ps, 1)

        @block.scalar
        def _(act):
            for g in range(GROUPS):
                act.wait_ge(T_ps, g + 1)
                for t in range(G4):
                    src = banks[g % 4][:, t * P:(t + 1) * P]
                    if scale is None:
                        ins = nc.scalar.activation(xT(G4 * g + t), src, ACT.Copy)
                    else:
                        ins = nc.scalar.activation(xT(G4 * g + t), src, ACT.Identity, scale=scale, bias=bias)
                    ins.then_inc(T_out, 1)


def add_normalised(nc, ctx, tag, x, y):
    m = Memory(nc, ctx, tag)
    stats = m.sb("stats", [P, N_TILES, 6])
    mv = m.sb("mv", [P, N_TILES, 2])
    ve = m.sb("var_eps", [P, N_TILES])
    rstd = m.sb("rstd", [P, N_TILES])
    tmp = m.sb("tmp", [P, N_TILES])
    magic = m.sb("magic", [P, N_TILES], I32)
    magic_set, stat, steps, waits_met, scaled, summed = (
        m.sem(s) for s in ("magic_set", "stat", "steps", "waits_met", "scaled", "summed"))

    with nc.Block() as block:
        @block.vector
        def _(v):
            nc.vector.memset(magic[:], RSQRT_MAGIC + 1).then_inc(magic_set, 1)
            for n in range(N_TILES):
                nc.vector.bn_stats(stats[:, n, :], y[:, n, :]).then_inc(stat, 1)
            v.wait_ge(stat, N_TILES)
            for n in range(N_TILES):
                nc.vector.bn_aggr(mv[:, n, :], stats[:, n, :]).then_inc(stat, 1)
            v.wait_ge(stat, 2 * N_TILES)
            nc.vector.tensor_scalar(ve[:], mv[:, :, 1], LN_EPS, None, ALU.add).then_inc(stat, 1)
            v.wait_ge(stat, 2 * N_TILES + 1)
            v.wait_ge(magic_set, 1)
            rsqrt_steps(nc, v, ve[:], rstd[:], tmp[:], magic[:], steps, 0, waits_met)
            v.wait_ge(steps, RSQRT_STEPS)
            for n in range(N_TILES):
                nc.vector.tensor_scalar(y[:, n, :], y[:, n, :], mv[:, n, 0:1], rstd[:, n:n + 1], ALU.subtract, ALU.mult
                                        ).then_inc(scaled, 1)
            for g in range(GROUPS):
                if g % 2:
                    continue
                v.wait_ge(scaled, G4 * (g + 2))
                sl = slice(G4 * g, G4 * (g + 2))
                nc.vector.tensor_tensor(x[:, sl, :], x[:, sl, :], y[:, sl, :], ALU.add).then_inc(summed, 1)


AH = 16
AD = D // AH
VW = AD + 1
AE = 4
AF = 4 * D
AC = AF // P


def rope_constants():
    f = np.float32
    inv_freq = (f(1.0) / f(10000.0) ** (np.arange(0, AD, 2, dtype=f) / f(AD))).astype(f)
    theta = (np.arange(T, dtype=f)[:, None] * inv_freq[None, :]).astype(f)
    cos, sin = np.cos(theta), np.sin(theta)
    tabs = np.stack([np.stack([cos, cos], -1).reshape(T, AD), np.stack([-sin, sin], -1).reshape(T, AD)])
    return np.ascontiguousarray(tabs.reshape(2, J, P, AD).transpose(2, 0, 1, 3).astype(f))


def head_constants():
    p = np.arange(P)
    head4 = (((p[:, None] % 32) // AD) == np.arange(4)[None, :]).astype(np.float32)
    causal = (p[:, None] <= p[None, :]).astype(np.float32)
    blocks = np.repeat(((p[:, None] // AD) == np.arange(AH)[None, :]).astype(np.float32), VW, axis=1)
    return head4, causal, np.ascontiguousarray(blocks)


def conv_attention_mixture(nc, w, x, ident):
    with ExitStack() as ctx:
        m = Memory(nc, ctx, "a")
        x1 = m.sb("x1", [P, N_TILES, D])
        with ExitStack() as c1:
            m1 = Memory(nc, c1, "a1")
            xc = m1.sb("xT", [P, B, 2 + T])
            x1T = m1.sb("x1T", [P, B, 1 + T])
            wpw = m1.sb("w_pw", [P, D])
            wdw = m1.sb("w_dw", [P, 3])
            wqkv = m1.sb("w_qkv", [P, 3 * D])
            wg = m1.sb("w_gate", [P, D])
            wo = m1.sb("w_o", [P, D])
            bg = m1.sb("b_gate", [1, D])
            ones1 = m1.sb("ones1", [1, P])
            rope = m1.sb("rope", [P, 2, J, AD])
            head4 = m1.sb("head4", [P, 4])
            causal = m1.sb("causal", [P, P])
            blocks = m1.sb("blocks", [P, AH * VW])
            with ExitStack() as c2:
                normalise_rows(nc, c2, "an", x, x1,
                               lambda n: xc[:, n % B, 2 + (n // B) * P:2 + (n // B + 1) * P], ident)

            with ExitStack() as c2, nc.Block() as block:
                m2 = Memory(nc, c2, "av")
                cv = m2.sb("conv", [P, 2, B, 2 * P])
                db = [m2.bank("x1T0"), m2.bank("x1T1")]
                tb = [m2.bank("x1_0"), m2.bank("x1_1")]
                loaded, zeroed, conv, d_ps, t_ps, d_out, t_out, first = (
                    m2.sem(s) for s in ("loaded", "zeroed", "conv", "d_ps", "t_ps", "d_out", "t_out", "first"))

                @block.sync
                def _(sp):
                    for dst, name in ((wpw[:], "w_pw"), (wdw[:], "w_dw"), (wqkv[:], "w_qkv"), (wg[:], "w_gate"),
                                      (wo[:], "w_o"), (bg[:], "b_gate"), (rope[:], "rope"), (head4[:], "head4"),
                                      (causal[:], "causal"), (blocks[:], "blocks")):
                        sp.dma_start(dst, w[name]).then_inc(loaded, DMA)
                    sp.wait_ge(loaded, 10 * DMA)

                @block.vector
                def _(v):
                    nc.vector.memset(xc[:, :, 0:2], 0.0).then_inc(zeroed, 1)
                    nc.vector.memset(ones1[:], 1.0).then_inc(zeroed, 1)
                    v.wait_ge(loaded, 10 * DMA)
                    v.wait_ge(zeroed, 2)
                    with v.Fori(0, GROUPS // 2) as i:
                        for par in range(2):
                            g = i * 2 + par
                            v.wait_ge(t_ps, g + 1)
                            src = lambda k: xc[:, :, bass.ds(g * (2 * P) + k, 2 * P)]
                            nc.vector.tensor_scalar(cv[:, par], src(0), wdw[:, 0:1], None, ALU.mult).then_inc(conv, 1)
                            for k in (1, 2):
                                v.wait_ge(conv, g * 3 + k)
                                nc.vector.scalar_tensor_tensor(cv[:, par], src(k), wdw[:, k:k + 1], cv[:, par], ALU.mult, ALU.add
                                                               ).then_inc(conv, 1)
                            v.wait_ge(d_ps, g + 1)
                            nc.vector.tensor_tensor(x1T[:, :, bass.ds(g * (2 * P) + 1, 2 * P)],
                                                    db[par][:].rearrange("p (b t) -> p b t", b=B), src(2), ALU.add).then_inc(d_out, 1)
                            v.wait_ge(t_ps, g + 3)
                            rows = x1[:, bass.ds(g * G4, G4), :]
                            nc.vector.tensor_tensor(rows, tb[par][:].rearrange("p (t d) -> p t d", t=G4), rows, ALU.add).then_inc(t_out, 1)
                    v.wait_ge(d_out, GROUPS)
                    nc.vector.tensor_copy(x1T[:, :, 0:1], x1T[:, :, 1:2]).then_inc(first, 1)

                @block.tensor
                def _(pe):
                    nc.tensor.nop().then_inc(t_ps, 2)
                    with pe.Fori(0, GROUPS // 2) as i:
                        for par in range(2):
                            g = i * 2 + par
                            pe.wait_ge(conv, g * 3 + 3)
                            nc.tensor.matmul(db[par][:], wpw[:], cv[:, par].rearrange("p b t -> p (b t)"), start=True, stop=True
                                             ).then_inc(d_ps, 1)
                            for t in range(G4):
                                last = nc.tensor.matmul(tb[par][:, t * D:(t + 1) * D], cv[:, par, t % B, (t // B) * P:(t // B + 1) * P],
                                                        wpw[:], start=True, stop=True)
                            last.then_inc(t_ps, 1)

            with ExitStack() as c2, nc.Block() as block:
                m2 = Memory(nc, c2, "al")
                W = AH * VW
                xt = m2.sb("x_tile", [P, B, P])
                dt = m2.sb("delta_tile", [P, B, P])
                rc = m2.sb("cos_terms", [P, B, 2 * D])
                rs = m2.sb("sin_terms", [P, B, 2 * D])
                neg = m2.sb("negative", [P, B, 2 * D])
                phi = m2.sb("phi", [P, B, 2 * D])
                va = m2.sb("v_and_1", [P, B, W])
                qT = m2.sb("qT", [P, B, P])
                qx = m2.sb("q_heads", [P, B, 4, P])
                kx = m2.sb("k_groups", [P, B, 4, P])
                pr = m2.sb("products", [P, 4, 4, P])
                state = m2.sb("state", [P, B, W])
                upd = m2.sb("state_update", [P, W])
                den = m2.sb("den", [P, AH])
                rden = m2.sb("inv_den", [P, AH])
                at = m2.sb("attn", [P, D])
                aT = m2.sb("attnT", [P, P])
                th = m2.sb("gate_tanh", [P, B, D])
                gt = m2.sb("gated", [P, D])
                qk_b = m2.bank("qk")
                vg_b = m2.bank("v_gate")
                T_b = m2.bank("T")
                s_b = [m2.bank("s0"), m2.bank("s1")]
                num_b = m2.bank("num")
                upd_b = m2.bank("upd")
                o_b = m2.bank("o")
                names = ("zeroed tile_ready delta_ready qkv_ps gate_ps tanh_done cos_done sin_done roped floored exped "
                         "phi_ready v_ready qkT_ps qT_ready qx_ready kx_ready s_ps masked num_ps upd_ps upd_masked "
                         "state_ready den_ready rden_ready at_ready aT_ps aT_ready o_ps gated x2_ready waits_met")
                (zeroed, tile_ready, delta_ready, qkv_ps, gate_ps, tanh_done, cos_done, sin_done, roped, floored, exped,
                 phi_ready, v_ready, qkT_ps, qT_ready, qx_ready, kx_ready, s_ps, masked, num_ps, upd_ps, upd_masked,
                 state_ready, den_ready, rden_ready, at_ready, aT_ps, aT_ready, o_ps, gated, x2_ready, waits_met) = (
                    m2.sem(s) for s in names.split())

                @block.gpsimd
                def _(pool):
                    nc.gpsimd.memset(kx[:], 0.0).then_inc(zeroed, 1)
                    nc.gpsimd.memset(va[:], 1.0).then_inc(zeroed, 1)
                    nc.gpsimd.memset(state[:], 0.0).then_inc(zeroed, 1)
                    with pool.Fori(0, J) as j:
                        for b in range(B):
                            u = j * 2 + b
                            pool.wait_ge(qkv_ps, u + 1)
                            pool.wait_ge(gate_ps, u + 1)
                            now, before = x1T[:, b, bass.ds(j * P + 1, P)], x1T[:, b, bass.ds(j * P, P)]
                            nc.gpsimd.tensor_copy(xt[:, b, :], now).then_inc(tile_ready, 1)
                            nc.gpsimd.tensor_tensor(dt[:, b, :], now, before, ALU.subtract).then_inc(delta_ready, 1)

                @block.tensor
                def _(pe):
                    nc.tensor.nop().then_inc(qkv_ps, 2)
                    nc.tensor.nop().then_inc(gate_ps, 2)
                    pe.wait_ge(zeroed, 3)

                    def project(u, b):
                        pe.wait_ge(tile_ready, u + 1)
                        pe.wait_ge(sin_done, u * 2 + 2)
                        nc.tensor.matmul(qk_b[:, 0:2 * D], xt[:, b, :], wqkv[:, 0:2 * D], start=True, stop=True
                                         ).then_inc(qkv_ps, 1)
                        pe.wait_ge(v_ready, u + 1)
                        pe.wait_ge(tanh_done, u + 1)
                        nc.tensor.matmul(vg_b[:, D:2 * D], xt[:, b, :], wqkv[:, 2 * D:3 * D], start=True, stop=True)
                        pe.wait_ge(delta_ready, u + 1)
                        nc.tensor.matmul(vg_b[:, 0:D], dt[:, b, :], wg[:], start=True, stop=False)
                        nc.tensor.matmul(vg_b[:, 0:D], ones1[:], bg[:], start=False, stop=True).then_inc(gate_ps, 1)

                    project(0, 0)
                    def tile(j, b, more=True):
                        u = j * 2 + b
                        pe.wait_ge(phi_ready, u + 1)
                        for k in range(2):
                            last = nc.tensor.transpose(T_b[:, k * P:(k + 1) * P], phi[:, b, k * D:(k + 1) * D], ident[:])
                        last.then_inc(qkT_ps, 1)
                        if more:
                            project(u + 1, 1 - b)
                        pe.wait_ge(qx_ready, u + 1)
                        pe.wait_ge(kx_ready, u * 4 + 4)
                        for g in range(4):
                            pe.wait_ge(masked, u * 4 + (g + 1))
                            nc.tensor.matmul(s_b[g % 2][:], kx[:, b, g, :], qx[:, b].rearrange("p h t -> p (h t)"),
                                             start=True, stop=True).then_inc(s_ps, 1)
                        pe.wait_ge(qT_ready, u + 1)
                        pe.wait_ge(at_ready, u + 1)
                        pe.wait_ge(state_ready, u + 1)
                        nc.tensor.matmul(num_b[:, 0:W], qT[:, b, :], state[:, b, :], start=True, stop=True)
                        pe.wait_ge(v_ready, u + 2)
                        pe.wait_ge(upd_masked, u + 1)
                        nc.tensor.matmul(upd_b[:, 0:W], phi[:, b, D:2 * D], va[:, b, :], start=True, stop=True
                                         ).then_inc(upd_ps, 1)
                        for g in range(4):
                            pe.wait_ge(masked, u * 4 + (g + 3))
                            for h in range(4 * g, 4 * g + 4):
                                last = nc.tensor.matmul(num_b[:, h * VW:(h + 1) * VW], pr[:, g, h % 4, :],
                                                        va[:, b, h * VW:(h + 1) * VW], start=False, stop=True,
                                                        skip_group_check=True)
                        last.then_inc(num_ps, 1)
                        pe.wait_ge(at_ready, u + 2)
                        nc.tensor.transpose(T_b[:, 0:P], at[:], ident[:]).then_inc(aT_ps, 1)
                        pe.wait_ge(aT_ready, u + 1)
                        pe.wait_ge(gated, u + 2)
                        nc.tensor.matmul(o_b[:, 0:D], aT[:], wo[:], start=True, stop=True).then_inc(o_ps, 1)

                    with pe.Fori(0, J - 1) as j:
                        for b in range(B):
                            tile(j, b)
                    tile(J - 1, 0)
                    tile(J - 1, 1, more=False)

                @block.scalar
                def _(act):
                    nc.scalar.nop().then_inc(v_ready, 1)
                    nc.scalar.nop().then_inc(tanh_done, 1)
                    act.wait_ge(zeroed, 3)

                    def from_projection(u, b):
                        act.wait_ge(gate_ps, u + 3)
                        nc.scalar.activation(va[:, b, :].rearrange("p (h c) -> p h c", c=VW)[:, :, 0:AD],
                                             vg_b[:, D:2 * D].rearrange("p (h c) -> p h c", c=AD), ACT.Copy).then_inc(v_ready, 1)
                        act.wait_ge(gated, u + 1)
                        nc.scalar.activation(th[:, b, :], vg_b[:, 0:D], ACT.Tanh, scale=0.5).then_inc(tanh_done, 1)
                        act.wait_ge(floored, u + 1)
                        nc.scalar.activation(neg[:, b, :], neg[:, b, :], ACT.Exp).then_inc(exped, 1)

                    from_projection(0, 0)
                    def tile(j, b, more=True):
                        u = j * 2 + b
                        act.wait_ge(qkT_ps, u + 1)
                        nc.scalar.activation(qT[:, b, :], T_b[:, 0:P], ACT.Copy).then_inc(qT_ready, 1)
                        for g in range(4):
                            nc.scalar.activation(kx[32 * g:32 * g + 32, b, g, :], T_b[32 * g:32 * g + 32, P:2 * P], ACT.Copy
                                                 ).then_inc(kx_ready, 1)
                        if more:
                            from_projection(u + 1, 1 - b)
                        act.wait_ge(aT_ps, u + 1)
                        nc.scalar.activation(aT[:], T_b[:, 0:P], ACT.Copy).then_inc(aT_ready, 1)

                    with act.Fori(0, J - 1) as j:
                        for b in range(B):
                            tile(j, b)
                    tile(J - 1, 0)
                    tile(J - 1, 1, more=False)

                @block.vector
                def _(v):
                    nc.vector.nop().then_inc(sin_done, 2)
                    nc.vector.nop().then_inc(masked, 2)
                    nc.vector.nop().then_inc(at_ready, 1)
                    nc.vector.nop().then_inc(gated, 2)
                    nc.vector.nop().then_inc(upd_masked, 1)
                    nc.vector.nop().then_inc(state_ready, 2)
                    v.wait_ge(zeroed, 3)

                    def phis(u, j, b):
                        v.wait_ge(qkv_ps, u + 3)
                        src = qk_b[:, 0:2 * D].rearrange("p (h d) -> p h d", d=AD)
                        shape = [P, 2 * AH, AD]
                        nc.vector.tensor_tensor(rc[:, b, :].rearrange("p (h d) -> p h d", d=AD), src,
                                                rope[:, 0, bass.ds(j, 1), :].broadcast_to(shape), ALU.mult).then_inc(cos_done, 1)
                        src4 = qk_b[:, 0:2 * D].rearrange("p (h d two) -> p h d two", d=AD // 2, two=2)
                        dst4 = rs[:, b, :].rearrange("p (h d two) -> p h d two", d=AD // 2, two=2)
                        for s in range(2):
                            tab = rope[:, 1, bass.ds(j, 1), :].rearrange("p j (d two) -> p j d two", two=2)[:, :, :, s]
                            nc.vector.tensor_tensor(dst4[:, :, :, s], src4[:, :, :, 1 - s], tab.broadcast_to([P, 2 * AH, AD // 2]),
                                                    ALU.mult).then_inc(sin_done, 1)
                        v.wait_ge(sin_done, u * 2 + 4)
                        nc.vector.tensor_tensor(rc[:, b, :], rc[:, b, :], rs[:, b, :], ALU.add).then_inc(roped, 1)
                        v.wait_ge(roped, u + 1)
                        nc.vector.tensor_scalar(neg[:, b, :], rc[:, b, :], 0.0, None, ALU.min).then_inc(floored, 1)

                    def phis_end(u, b):
                        v.wait_ge(exped, u + 1)
                        nc.vector.scalar_tensor_tensor(phi[:, b, :], rc[:, b, :], 0.0, neg[:, b, :], ALU.max, ALU.add
                                                       ).then_inc(phi_ready, 1)

                    phis(0, 0, 0)
                    phis_end(0, 0)
                    def tile(j, b, more=True):
                        u = j * 2 + b
                        v.wait_ge(qkT_ps, u + 1)
                        v.wait_ge(kx_ready, u * 4 + 4)
                        nc.vector.tensor_tensor(qx[:, b], T_b[:, 0:P].unsqueeze(1).broadcast_to([P, 4, P]),
                                                head4[:].unsqueeze(2).broadcast_to([P, 4, P]), ALU.mult).then_inc(qx_ready, 1)
                        if more:
                            phis(u + 1, j + b, 1 - b)
                        for g in range(4):
                            v.wait_ge(s_ps, u * 4 + (g + 1))
                            nc.vector.tensor_tensor(pr[:, g], s_b[g % 2][:].rearrange("p (h t) -> p h t", h=4),
                                                    causal[:].unsqueeze(1).broadcast_to([P, 4, P]), ALU.mult).then_inc(masked, 1)
                        v.wait_ge(upd_ps, u + 1)
                        nc.vector.tensor_tensor(upd[:], upd_b[:, 0:W], blocks[:], ALU.mult).then_inc(upd_masked, 1)
                        v.wait_ge(upd_masked, u + 2)
                        nc.vector.tensor_tensor(state[:, b, :], state[:, b, :], upd[:], ALU.add).then_inc(state_ready, 1)
                        v.wait_ge(num_ps, u + 1)
                        n3 = num_b[:, 0:W].rearrange("p (h c) -> p h c", c=VW)
                        nc.vector.tensor_scalar(den[:], n3[:, :, AD], 1e-6, None, ALU.add).then_inc(den_ready, 1)
                        v.wait_ge(den_ready, u + 1)
                        nc.vector.reciprocal(rden[:], den[:]).then_inc(rden_ready, 1)
                        v.wait_ge(rden_ready, u + 1)
                        nc.vector.tensor_tensor(at[:].rearrange("p (h c) -> p h c", c=AD), n3[:, :, 0:AD],
                                                rden[:].unsqueeze(2).broadcast_to([P, AH, AD]), ALU.mult).then_inc(at_ready, 1)
                        if more:
                            phis_end(u + 1, 1 - b)
                        v.wait_ge(o_ps, u + 1)
                        v.wait_ge(tanh_done, u + 2)
                        nc.vector.scalar_tensor_tensor(gt[:], th[:, b, :], 1.0, o_b[:, 0:D], ALU.add, ALU.mult).then_inc(gated, 1)
                        row = x1[:, bass.ds(u, 1), :].rearrange("p n d -> p (n d)")
                        v.wait_ge(gated, u + 3)
                        v.sem_inc(waits_met)
                        nc.vector.scalar_tensor_tensor(row, gt[:], 0.5, row, ALU.mult, ALU.add).then_inc(x2_ready, 1)

                    with v.Fori(0, J - 1) as j:
                        for b in range(B):
                            tile(j, b)
                    tile(J - 1, 0)
                    tile(J - 1, 1, more=False)

        with ExitStack() as c1:
            m1 = Memory(nc, c1, "am")
            hh = m1.sb("hT_hi", [P, N_TILES * P], F32R)
            hl = m1.sb("hT_lo", [P, N_TILES * P], F32R)
            w1h = m1.sb("w1_hi", [P, AE * AF], F32R)
            w1l = m1.sb("w1_lo", [P, AE * AF], F32R)
            w2 = m1.sb("w2", [P, AE * AC, D])
            b1 = m1.sb("b1", [P, AE * AC])
            gw = m1.sb("mix", [P, N_TILES, AE])
            with ExitStack() as c3:
                m3 = Memory(nc, c3, "ah")
                h = m3.sb("h", [P, N_TILES, D])
                hT = m3.sb("hT", [P, N_TILES, P])
                gb = m3.sb("ln_g_b", [P, 2])
                w1 = m3.sb("w1", [P, AE * AF])
                wm = m3.sb("w_moe_gate", [P, AE])
                b2 = m3.sb("b2", [AE, D])
                with nc.Block() as block:
                    loaded = m3.sem("loaded")

                    @block.sync
                    def _(sp):
                        for dst, name in ((gb[:], "ln_g_b"), (w1[:], "w1"), (wm[:], "w_moe_gate"), (b2[:], "b2"),
                                          (w2[:], "w2"), (b1[:], "b1")):
                            sp.dma_start(dst, w[name]).then_inc(loaded, DMA)
                        sp.wait_ge(loaded, 6 * DMA)

                with ExitStack() as c2:
                    normalise_rows(nc, c2, "ao", x1, h, lambda n: hT[:, n, :], ident, scale=gb[:, 0:1], bias=gb[:, 1:2])

                with ExitStack() as c2, nc.Block() as block:
                    m2 = Memory(nc, c2, "as")
                    lg = m2.sb("logits", [P, N_TILES, AE])
                    mx = m2.sb("max", [P, N_TILES])
                    sm = m2.sb("sum", [P, N_TILES])
                    rm = m2.sb("inv_sum", [P, N_TILES])
                    gT = m2.sb("mixT", [AE, N_TILES, P])
                    lb = m2.bank("logits")
                    cb = [m2.bank("gT0"), m2.bank("gT1")]
                    yb = [m2.bank("y0"), m2.bank("y1")]
                    w_hi, w_lo, hi_done, lo_done, lg_ps, shifted, expd, step, mixed, gT_ps, gT_out, y_ps, y_out = (
                        m2.sem(s) for s in ("w_hi", "w_lo", "hi_done", "lo_done", "lg_ps", "shifted", "expd", "step", "mixed",
                                            "gT_ps", "gT_out", "y_ps", "y_out"))
                    shape = [P, N_TILES, AE]
                    hTf = hT[:].rearrange("p n t -> p (n t)")

                    @block.tensor
                    def _(pe):
                        for n in range(N_TILES):
                            last = nc.tensor.matmul(lb[:, n * AE:(n + 1) * AE], hT[:, n, :], wm[:], start=True, stop=True)
                        last.then_inc(lg_ps, 1)
                        pe.wait_ge(mixed, 1)
                        for g in range(GROUPS):
                            if g >= 2:
                                pe.wait_ge(gT_out, g - 1)
                                pe.wait_ge(y_out, g - 1)
                            for t in range(G4):
                                last = nc.tensor.transpose(cb[g % 2][0:AE, t * P:(t + 1) * P], gw[:, G4 * g + t, :], ident[:])
                            last.then_inc(gT_ps, 1)
                            pe.wait_ge(gT_out, g + 1)
                            for t in range(G4):
                                last = nc.tensor.matmul(yb[g % 2][:, t * D:(t + 1) * D], gT[:, G4 * g + t, :], b2[:], start=True, stop=True)
                            last.then_inc(y_ps, 1)

                    @block.scalar
                    def _(act):
                        for q in range(4):
                            sl = slice(q * 1024, (q + 1) * 1024)
                            nc.scalar.activation(hh[:, sl], hTf[:, sl], ACT.Copy).then_inc(hi_done, 1)
                        for q in range(2):
                            sl = slice(q * 1024, (q + 1) * 1024)
                            nc.scalar.activation(w1h[:, sl], w1[:, sl], ACT.Copy).then_inc(w_hi, 1)
                        act.wait_ge(shifted, 1)
                        nc.scalar.activation(gw[:], lg[:], ACT.Exp).then_inc(expd, 1)
                        for g in range(GROUPS):
                            act.wait_ge(gT_ps, g + 1)
                            nc.scalar.activation(gT[:, G4 * g:G4 * g + G4, :], cb[g % 2][0:AE, :].rearrange("p (t k) -> p t k", t=G4),
                                                 ACT.Copy).then_inc(gT_out, 1)

                    @block.vector
                    def _(v):
                        lb3 = lb[:, 0:N_TILES * AE].rearrange("p (n e) -> p n e", e=AE)
                        v.wait_ge(lg_ps, 1)
                        nc.vector.tensor_reduce(mx[:], lb3, AX.X, ALU.max).then_inc(step, 1)
                        v.wait_ge(step, 1)
                        nc.vector.tensor_tensor(lg[:], lb3, mx[:].unsqueeze(2).broadcast_to(shape), ALU.subtract).then_inc(shifted, 1)
                        for q in range(4):
                            sl = slice(q * 1024, (q + 1) * 1024)
                            v.wait_ge(hi_done, q + 1)
                            nc.vector.tensor_tensor(hl[:, sl], hTf[:, sl], hh[:, sl].bitcast(F32), ALU.subtract).then_inc(lo_done, 1)
                        for q in range(2):
                            sl = slice(q * 1024, (q + 1) * 1024)
                            v.wait_ge(w_hi, q + 1)
                            nc.vector.tensor_tensor(w1l[:, sl], w1[:, sl], w1h[:, sl].bitcast(F32), ALU.subtract).then_inc(w_lo, 1)
                        v.wait_ge(expd, 1)
                        nc.vector.tensor_reduce(sm[:], gw[:], AX.X, ALU.add).then_inc(step, 1)
                        v.wait_ge(step, 2)
                        nc.vector.reciprocal(rm[:], sm[:]).then_inc(step, 1)
                        v.wait_ge(step, 3)
                        nc.vector.tensor_tensor(gw[:], gw[:], rm[:].unsqueeze(2).broadcast_to(shape), ALU.mult).then_inc(mixed, 1)
                        for g in range(GROUPS):
                            v.wait_ge(y_ps, g + 1)
                            rows = x1[:, G4 * g:G4 * g + G4, :]
                            nc.vector.tensor_tensor(rows, yb[g % 2][:].rearrange("p (t d) -> p t d", t=G4), rows, ALU.add).then_inc(y_out, 1)

            with ExitStack() as c2, nc.Block() as block:
                m2 = Memory(nc, c2, "ax")
                hid = m2.sb("hidden", [P, 2, AC, 512])
                up = [m2.bank(f"up{i}") for i in range(4)]
                dn = [m2.bank("down0"), m2.bank("down1")]
                up_ps, hid_ready, dn_ps, added = (m2.sem(s) for s in ("up_ps", "hid_ready", "dn_ps", "added"))

                @block.tensor
                def _(pe):
                    def first(g, e):
                        for c in range(AC):
                            k = e * AC + c
                            q = g * (AE * AC) + k
                            pe.wait_ge(hid_ready, q + 1)
                            cols = bass.ds(g * 512, 512)
                            sl = slice(k * P, (k + 1) * P)
                            nc.tensor.matmul(up[c][:], w1h[:, sl], hh[:, cols], start=True, stop=False)
                            nc.tensor.matmul(up[c][:], w1l[:, sl], hh[:, cols], start=False, stop=False)
                            nc.tensor.matmul(up[c][:], w1h[:, sl], hl[:, cols], start=False, stop=True).then_inc(up_ps, 1)

                    def second(g, e):
                        q = g * AE + e
                        pe.wait_ge(hid_ready, q * AC + 8)
                        pe.wait_ge(added, q + 1)
                        for t in range(G4):
                            for c in range(AC):
                                last = nc.tensor.matmul(dn[e % 2][:, t * D:(t + 1) * D], hid[:, e % 2, c, t * P:(t + 1) * P],
                                                        w2[:, e * AC + c, :], start=(c == 0), stop=(c == AC - 1))
                        last.then_inc(dn_ps, 1)

                    with pe.Fori(0, GROUPS) as g:
                        for e in range(AE):
                            first(g, e)
                            if e:
                                second(g, e - 1)
                        second(g, AE - 1)

                @block.scalar
                def _(act):
                    nc.scalar.nop().then_inc(hid_ready, 4)
                    with act.Fori(0, GROUPS) as g:
                        for e in range(AE):
                            act.wait_ge(dn_ps, g * AE + (e + 1))
                            for c in range(AC):
                                act.wait_ge(up_ps, g * (AE * AC) + (e * AC + c + 1))
                                nc.scalar.activation(hid[:, e % 2, c, :], up[c][:], ACT.Silu,
                                                     bias=b1[:, e * AC + c:e * AC + c + 1]).then_inc(hid_ready, 1)

                @block.vector
                def _(v):
                    nc.vector.nop().then_inc(dn_ps, 2)
                    nc.vector.nop().then_inc(added, 2)
                    with v.Fori(0, GROUPS) as g:
                        for e in range(AE):
                            v.wait_ge(dn_ps, g * AE + (e + 3))
                            v.wait_ge(added, g * AE + (e + 2))
                            for t in range(G4):
                                row = x1[:, bass.ds(g * G4 + t, 1), :].rearrange("p n d -> p (n d)")
                                wt = gw[:, bass.ds(g * G4 + t, 1), e]
                                ins = nc.vector.scalar_tensor_tensor(row, dn[e % 2][:, t * D:(t + 1) * D], wt, row, ALU.mult, ALU.add)
                            ins.then_inc(added, 1)
        with ExitStack() as c2:
            add_normalised(nc, c2, "aa", x, x1)


EXPERTS = 16
FE = 256
GU = 2 * FE
CH = 1024


def fp4_experts(nc, w, x, ident):
    with ExitStack() as ctx:
        m = Memory(nc, ctx, "b")
        y = m.sb("y", [P, N_TILES, D])
        comb = m.sb("combine", [P, N_TILES, EXPERTS])
        xh = m.sb("xT_hi", [P, N_TILES * P], F32R)
        xl = m.sb("xT_lo", [P, N_TILES * P], F32R)
        wgu = m.sb("w_gu", [P, EXPERTS, GU])
        wdn = m.sb("w_down", [P, 2, EXPERTS, D])
        bgu = m.sb("bias_gu", [P, EXPERTS, 4])

        with ExitStack() as c2, nc.Block() as block:
            m2 = Memory(nc, c2, "bw")
            blk = m2.sb("blocks", [P, 2, CH], I32)
            scl = m2.sb("scales", [P, 2, CH], I32)
            nib = m2.sb("nibble", [P, CH], I32)
            cod = m2.sb("code", [P, CH], I32)
            sgn = m2.sb("sign", [P, CH], I32)
            sc = m2.sb("signed_scale", [P, CH], I32)
            mag = m2.sb("magnitude", [P, CH])
            in_dma = [m2.sem("in_dma0"), m2.sem("in_dma1")]
            step, decoded, b_dma = m2.sem("step"), m2.sem("decoded"), m2.sem("b_dma")
            n_gu = EXPERTS * GU // CH
            n_dn = EXPERTS * D // CH
            LOADS_GU, LOADS_DN = 2 + 8, 1 + 8

            @block.sync
            def _(sp):
                sp.dma_start(bgu[:], w["bias_gu"]).then_inc(b_dma, DMA)
                for i in range(n_gu + n_dn):
                    if i >= 2:
                        sp.wait_ge(decoded, i - 1)
                    if i < n_gu:
                        sl = slice(i * CH, (i + 1) * CH)
                        for half in range(2):
                            sp.dma_start(blk[64 * half:64 * half + 64, i % 2, :], w["blocks_gu"][:, sl]).then_inc(in_dma[i % 2], DMA)
                            for k in range(4):
                                p0 = 64 * half + 16 * k
                                sp.dma_start(scl[p0:p0 + 16, i % 2, :], w["scales_gu"][k:k + 1, sl].broadcast_to([16, CH])
                                             ).then_inc(in_dma[i % 2], DMA)
                    else:
                        sl = slice((i - n_gu) * CH, (i - n_gu + 1) * CH)
                        sp.dma_start(blk[:, i % 2, :], w["blocks_down"][:, sl]).then_inc(in_dma[i % 2], DMA)
                        for k in range(8):
                            sp.dma_start(scl[16 * k:16 * k + 16, i % 2, :], w["scales_down"][k:k + 1, sl].broadcast_to([16, CH])
                                         ).then_inc(in_dma[i % 2], DMA)

            @block.vector
            def _(v):
                done = 0
                loads = [0, 0]

                def decode(i, nibbles, dst, last):
                    nonlocal done
                    for lo, hi, shift in nibbles:
                        nc.vector.tensor_scalar(nib[lo:hi, :], blk[lo:hi, i % 2, :], shift, 15,
                                                ALU.logical_shift_right, ALU.bitwise_and).then_inc(step, 1)
                    done += len(nibbles)
                    v.wait_ge(step, done)
                    nc.vector.tensor_scalar(cod[:], nib[:], 7, None, ALU.bitwise_and).then_inc(step, 1)
                    nc.vector.tensor_scalar(sgn[:], nib[:], 3, 31, ALU.logical_shift_right, ALU.logical_shift_left).then_inc(step, 1)
                    nc.vector.tensor_scalar(sc[:], scl[:, i % 2, :], 23, None, ALU.logical_shift_left).then_inc(step, 1)
                    v.wait_ge(step, done + 3)
                    nc.vector.tensor_tensor(sc[:], sc[:], sgn[:], ALU.bitwise_or).then_inc(step, 1)
                    nc.vector.tensor_scalar(mag[:], cod[:], 2.0, -8.0, ALU.mult, ALU.add).then_inc(step, 1)
                    v.wait_ge(step, done + 5)
                    nc.vector.scalar_tensor_tensor(mag[:], cod[:], -2.0, mag[:], ALU.add, ALU.max).then_inc(step, 1)
                    v.wait_ge(step, done + 6)
                    nc.vector.scalar_tensor_tensor(mag[:], cod[:], 0.5, mag[:], ALU.mult, ALU.max).then_inc(step, 1)
                    v.wait_ge(step, done + 7)
                    ins = nc.vector.tensor_tensor(dst, mag[:], sc[:].bitcast(F32), ALU.mult).then_inc(step, 1)
                    done += 8
                    v.wait_ge(step, done)
                    if last:
                        nc.vector.nop().then_inc(decoded, 1)

                for i in range(n_gu + n_dn):
                    loads[i % 2] += LOADS_GU if i < n_gu else LOADS_DN
                    v.wait_ge(in_dma[i % 2], loads[i % 2] * DMA)
                    if i < n_gu:
                        dst = wgu[:].rearrange("p e o -> p (e o)")[:, i * CH:(i + 1) * CH]
                        decode(i, [(0, 64, 0), (64, 128, 4)], dst, True)
                    else:
                        k = i - n_gu
                        for c in range(2):
                            dst = wdn[:, c, :, :].rearrange("p e d -> p (e d)")[:, k * CH:(k + 1) * CH]
                            decode(i, [(0, 128, 4 * c)], dst, c == 1)
                v.wait_ge(b_dma, DMA)

        with ExitStack() as c1:
            m1 = Memory(nc, c1, "br")
            xn = m1.sb("xn", [P, N_TILES, D])
            xT = m1.sb("xT", [P, N_TILES, P])
            with ExitStack() as c2:
                normalise_rows(nc, c2, "bn", x, xn, lambda n: xT[:, n, :], ident, even_first=True)
            with ExitStack() as c2, nc.Block() as block:
                m2 = Memory(nc, c2, "bt")
                rw = m2.sb("router", [P, EXPERTS])
                bd = m2.sb("bias_down", [EXPERTS, D])
                lg = m2.sb("logits", [P, N_TILES, EXPERTS])
                top = m2.sb("top", [P, N_TILES, 8])
                idx = m2.sb("index", [P, N_TILES, 8], mybir.dt.uint32)
                idf = m2.sb("index_f", [P, N_TILES, 2])
                gap = m2.sb("gap", [P, N_TILES])
                e2 = m2.sb("exp_gap", [P, N_TILES])
                den = m2.sb("den", [P, N_TILES])
                wt = m2.sb("weights", [P, 2, N_TILES])
                iota = m2.sb("iota", [P, EXPERTS])
                hot = m2.sb("one_hot", [P, N_TILES, EXPERTS])
                cT = m2.sb("combineT", [EXPERTS, N_TILES, P])
                lb = m2.bank("logits")
                cb = [m2.bank("cT0"), m2.bank("cT1")]
                yb = [m2.bank("y0"), m2.bank("y1")]
                loaded, lg_ps, lg_out, topped, gapped, expd, step, combined, hi_done, lo_done, cT_ps, cT_out, y_ps, y_out = (
                    m2.sem(s) for s in ("loaded", "lg_ps", "lg_out", "topped", "gapped", "expd", "step", "combined",
                                        "hi_done", "lo_done", "cT_ps", "cT_out", "y_ps", "y_out"))

                @block.sync
                def _(sp):
                    sp.dma_start(rw[:], w["router"]).then_inc(loaded, DMA)
                    sp.dma_start(bd[:], w["bias_down"]).then_inc(loaded, DMA)
                    sp.dma_start(iota[:], w["iota"]).then_inc(loaded, DMA)

                @block.tensor
                def _(pe):
                    pe.wait_ge(loaded, 3 * DMA)
                    for n in range(N_TILES):
                        last = nc.tensor.matmul(lb[:, n * EXPERTS:(n + 1) * EXPERTS], xT[:, n, :], rw[:], start=True, stop=True)
                    last.then_inc(lg_ps, 1)
                    pe.wait_ge(combined, 1)
                    for g in range(GROUPS):
                        if g >= 2:
                            pe.wait_ge(cT_out, g - 1)
                        for t in range(G4):
                            last = nc.tensor.transpose(cb[g % 2][0:EXPERTS, t * P:(t + 1) * P], comb[:, G4 * g + t, :], ident[:])
                        last.then_inc(cT_ps, 1)
                        pe.wait_ge(cT_out, g + 1)
                        if g >= 2:
                            pe.wait_ge(y_out, g - 1)
                        for t in range(G4):
                            last = nc.tensor.matmul(yb[g % 2][:, t * D:(t + 1) * D], cT[:, G4 * g + t, :], bd[:], start=True, stop=True)
                        last.then_inc(y_ps, 1)

                @block.scalar
                def _(act):
                    act.wait_ge(lg_ps, 1)
                    nc.scalar.activation(lg[:].rearrange("p n e -> p (n e)"), lb[:], ACT.Copy).then_inc(lg_out, 1)
                    for q in range(4):
                        sl = slice(q * 1024, (q + 1) * 1024)
                        nc.scalar.activation(xh[:, sl], xT[:].rearrange("p n t -> p (n t)")[:, sl], ACT.Copy).then_inc(hi_done, 1)
                    act.wait_ge(gapped, 1)
                    nc.scalar.activation(e2[:], gap[:], ACT.Exp).then_inc(expd, 1)
                    for g in range(GROUPS):
                        act.wait_ge(cT_ps, g + 1)
                        nc.scalar.activation(cT[:, G4 * g:G4 * g + G4, :], cb[g % 2][0:EXPERTS, :].rearrange("p (t k) -> p t k", t=G4),
                                             ACT.Copy).then_inc(cT_out, 1)
                        act.wait_ge(y_ps, g + 1)
                        nc.scalar.activation(y[:, G4 * g:G4 * g + G4, :], yb[g % 2][:].rearrange("p (t d) -> p t d", t=G4),
                                             ACT.Copy).then_inc(y_out, 1)

                @block.vector
                def _(v):
                    v.wait_ge(lg_out, 1)
                    for n in range(N_TILES):
                        nc.vector.max(top[:, n, :], lg[:, n, :]).then_inc(topped, 1)
                    v.wait_ge(topped, N_TILES)
                    nc.vector.tensor_tensor(gap[:], top[:, :, 1], top[:, :, 0], ALU.subtract).then_inc(gapped, 1)
                    for n in range(N_TILES):
                        nc.vector.max_index(idx[:, n, :], top[:, n, :], lg[:, n, :]).then_inc(topped, 1)
                    v.wait_ge(expd, 1)
                    nc.vector.tensor_scalar(den[:], e2[:], 1.0, None, ALU.add).then_inc(step, 1)
                    v.wait_ge(step, 1)
                    nc.vector.reciprocal(wt[:, 0, :], den[:]).then_inc(step, 1)
                    v.wait_ge(step, 2)
                    nc.vector.tensor_tensor(wt[:, 1, :], wt[:, 0, :], e2[:], ALU.mult).then_inc(step, 1)
                    v.wait_ge(topped, 2 * N_TILES)
                    nc.vector.tensor_copy(idf[:], idx[:, :, 0:2]).then_inc(step, 1)
                    v.wait_ge(loaded, 3 * DMA)
                    v.wait_ge(step, 4)
                    shape = [P, N_TILES, EXPERTS]
                    for k, dst in ((0, comb), (1, hot)):
                        nc.vector.tensor_tensor(dst[:], iota[:].unsqueeze(1).broadcast_to(shape),
                                                idf[:, :, k:k + 1].broadcast_to(shape), ALU.is_equal).then_inc(step, 1)
                        v.wait_ge(step, 5 + 2 * k)
                        nc.vector.tensor_tensor(dst[:], dst[:], wt[:, k, :].unsqueeze(2).broadcast_to(shape), ALU.mult).then_inc(step, 1)
                    v.wait_ge(step, 8)
                    nc.vector.tensor_tensor(comb[:], comb[:], hot[:], ALU.add).then_inc(combined, 1)
                    for q in range(4):
                        sl = slice(q * 1024, (q + 1) * 1024)
                        v.wait_ge(hi_done, q + 1)
                        nc.vector.tensor_tensor(xl[:, sl], xT[:].rearrange("p n t -> p (n t)")[:, sl], xh[:, sl].bitcast(F32),
                                                ALU.subtract).then_inc(lo_done, 1)

        with ExitStack() as c2, nc.Block() as block:
            m2 = Memory(nc, c2, "be")
            slot = [m2.sb(f"w_slot{i}", [P, 4, P], F32R) for i in range(2)]
            bias_slot = [m2.sb(f"bias_slot{i}", [P, 4]) for i in range(2)]
            sil = m2.sb("silu", [P, 2, 512])
            h = m2.sb("h", [P, 2, 2, 512])
            gate = [m2.bank("gate0"), m2.bank("gate1")]
            up = [m2.bank("up0"), m2.bank("up1")]
            dn = [m2.bank("down0"), m2.bank("down1")]
            slot_ready, gate_ps, up_ps, silu_done, h_ready, down_ps, added = (
                m2.sem(s) for s in ("slot_ready", "gate_ps", "up_ps", "silu_done", "h_ready", "down_ps", "added"))

            @block.gpsimd
            def _(pool):
                with pool.Fori(0, EXPERTS // 2) as i:
                    for par in range(2):
                        pool.wait_ge(up_ps, (i * 2 + par) * 16 + 16)
                        for q in range(4):
                            src = wgu[:, bass.ds(i * 2 + par, 1), (q // 2) * FE:(q // 2 + 1) * FE]
                            src = src.rearrange("p e (k two) -> p (e k) two", two=2)[:, :, q % 2]
                            nc.gpsimd.tensor_copy(slot[par][:, q, :], src).then_inc(slot_ready, 1)
                        pool.wait_ge(h_ready, (i * 2 + par) * 16 + 2)
                        nc.gpsimd.tensor_copy(bias_slot[par][:], bgu[:, bass.ds(i * 2 + par, 1), :].rearrange("p e q -> p (e q)")
                                              ).then_inc(slot_ready, 1)

            @block.tensor
            def _(pe):
                def gate_up(i, par, g):
                    s = (i * 2 + par) * 8 + g
                    cols = slice(g * 512, (g + 1) * 512)
                    for c in range(2):
                        for k, banks, out_of, ready in ((0, gate, silu_done, gate_ps), (2, up, h_ready, up_ps)):
                            pe.wait_ge(out_of, s * 2 + (c + 1))
                            nc.tensor.matmul(banks[c][:], slot[par][:, k + c, :], xh[:, cols], start=True, stop=False)
                            nc.tensor.matmul(banks[c][:], slot[par][:, k + c, :], xl[:, cols], start=False, stop=True
                                             ).then_inc(ready, 1)

                def down(i, par, g):
                    s = (i * 2 + par) * 8 + g
                    pe.wait_ge(h_ready, s * 2 + 4)
                    pe.wait_ge(added, s + 1)
                    for t in range(G4):
                        for c in range(2):
                            last = nc.tensor.matmul(dn[g % 2][:, t * D:(t + 1) * D], h[:, g % 2, c, t * P:(t + 1) * P],
                                                    wdn[:, c, bass.ds(i * 2 + par, 1), :].rearrange("p e d -> p (e d)"),
                                                    start=(c == 0), stop=(c == 1))
                    last.then_inc(down_ps, 1)

                with pe.Fori(0, EXPERTS // 2) as i:
                    for par in range(2):
                        pe.wait_ge(slot_ready, (i * 2 + par) * 5 + 5)
                        for g in range(GROUPS):
                            gate_up(i, par, g)
                            if g:
                                down(i, par, g - 1)
                        down(i, par, GROUPS - 1)

            @block.scalar
            def _(act):
                nc.scalar.nop().then_inc(silu_done, 2)
                with act.Fori(0, EXPERTS // 2) as i:
                    for par in range(2):
                        for g in range(GROUPS):
                            s = (i * 2 + par) * 8 + g
                            for c in range(2):
                                act.wait_ge(gate_ps, s * 2 + (c + 1))
                                act.wait_ge(h_ready, s * 2 + (c + 1))
                                nc.scalar.activation(sil[:, c, :], gate[c][:], ACT.Silu,
                                                     bias=bias_slot[par][:, c:c + 1]).then_inc(silu_done, 1)

            @block.vector
            def _(v):
                nc.vector.nop().then_inc(h_ready, 2)
                nc.vector.nop().then_inc(added, 2)
                nc.vector.nop().then_inc(up_ps, 32)

                def hidden(i, par, g, c):
                    s = (i * 2 + par) * 8 + g
                    v.wait_ge(up_ps, s * 2 + (c + 33))
                    v.wait_ge(silu_done, s * 2 + (c + 3))
                    v.wait_ge(down_ps, s + 1)
                    nc.vector.scalar_tensor_tensor(h[:, g % 2, c, :], up[c][:], bias_slot[par][:, 2 + c:3 + c],
                                                   sil[:, c, :], ALU.add, ALU.mult).then_inc(h_ready, 1)

                def combine(i, par, g):
                    s = (i * 2 + par) * 8 + g
                    v.wait_ge(down_ps, s + 3)
                    for t in range(G4):
                        n = G4 * g + t
                        ins = nc.vector.scalar_tensor_tensor(y[:, n, :], dn[g % 2][:, t * D:(t + 1) * D],
                                                             comb[:, n, bass.ds(i * 2 + par, 1)], y[:, n, :], ALU.mult, ALU.add)
                    ins.then_inc(added, 1)

                nc.vector.nop().then_inc(down_ps, 2)
                with v.Fori(0, EXPERTS // 2) as i:
                    for par in range(2):
                        for g in range(GROUPS):
                            hidden(i, par, g, 0)
                            hidden(i, par, g, 1)
                            if g:
                                combine(i, par, g - 1)
                        combine(i, par, GROUPS - 1)

        with ExitStack() as c2:
            add_normalised(nc, c2, "ba", x, y)



def linear_attention(nc, w, x, ident):
    with ExitStack() as ctx:
        m = Memory(nc, ctx, "c")
        xn = m.sb("xn", [P, N_TILES, D])
        xT = m.sb("xT", [P, N_TILES, P])
        y = m.sb("y", [P, N_TILES, D])
        wq = m.sb("wq", [P, D])
        gram = m.sb("gram", [P, B, D])
        mix = m.sb("mix", [P, B, D])
        with ExitStack() as c2:
            normalise_rows(nc, c2, "cn", x, xn, lambda n: xT[:, n, :], ident)
        with ExitStack() as c2, nc.Block() as block:
            m2 = Memory(nc, c2, "cm")
            gb = [m2.bank(f"gram{b}") for b in range(B)]
            mb = [m2.bank(f"mix{b}") for b in range(B)]
            yb = [m2.bank(f"y{i}") for i in range(4)]
            wq_in, gram_ps, gram_out, mix_ps, mix_out, y_ps, y_out = (
                m2.sem(s) for s in ("wq_in", "gram_ps", "gram_out", "mix_ps", "mix_out", "y_ps", "y_out"))

            @block.sync
            def _(sp):
                sp.dma_start(wq[:], w["W_q"]).then_inc(wq_in, DMA)

            @block.tensor
            def _(pe):
                for b in range(B):
                    for j in range(J):
                        n = B * j + b
                        last = nc.tensor.matmul(gb[b][:, 0:D], xn[:, n, :], xn[:, n, :], start=(j == 0), stop=(j == J - 1))
                    last.then_inc(gram_ps, 1)
                pe.wait_ge(wq_in, DMA)
                for b in range(B):
                    pe.wait_ge(gram_out, b + 1)
                    nc.tensor.matmul(mb[b][:, 0:D], wq[:], gram[:, b, :], start=True, stop=True).then_inc(mix_ps, 1)
                pe.wait_ge(mix_out, B)
                for g in range(GROUPS):
                    if g >= 4:
                        pe.wait_ge(y_out, g - 3)
                    for t in range(G4):
                        n = G4 * g + t
                        last = nc.tensor.matmul(yb[g % 4][:, t * D:(t + 1) * D], xT[:, n, :], mix[:, n % B, :],
                                                start=True, stop=True)
                    last.then_inc(y_ps, 1)

            @block.scalar
            def _(act):
                for b in range(B):
                    act.wait_ge(gram_ps, b + 1)
                    nc.scalar.activation(gram[:, b, :], gb[b][:, 0:D], ACT.Copy).then_inc(gram_out, 1)
                for b in range(B):
                    act.wait_ge(mix_ps, b + 1)
                    nc.scalar.activation(mix[:, b, :], mb[b][:, 0:D], ACT.Copy).then_inc(mix_out, 1)
                for g in range(GROUPS):
                    act.wait_ge(y_ps, g + 1)
                    nc.scalar.activation(y[:, G4 * g:G4 * g + G4, :], yb[g % 4][:].rearrange("p (t d) -> p t d", t=G4),
                                         ACT.Copy).then_inc(y_out, 1)
        with ExitStack() as c2:
            add_normalised(nc, c2, "ca", x, y)


DEPTH = 6
HEADS = 16
HD = 64
INNER = HEADS * HD
WINDOW = 32
PAIRS = HEADS // 2
KEYS = WINDOW + P
FF = 341
FF_CHUNKS = [(0, 128), (128, 128), (256, FF - 256)]
MASKED = -1.0e30


def rotary_constants():
    f = np.float32
    half = np.arange(0, HD, 2, dtype=f)
    inv_freq = (f(1.0) / f(10000.0) ** (half / f(HD))).astype(f)
    t = np.arange(T, dtype=f)
    ang = (t[:, None] * inv_freq[None, :]).astype(f)
    cos, sin = np.cos(ang), np.sin(ang)
    base = ((half + f(0.4 * HD)) / f(1.4 * HD)).astype(f).astype(np.float64)
    power = ((np.arange(T) % P) - P // 2) / (WINDOW // 2)
    scale = base[None, :] ** power[:, None]
    two = lambda a: np.concatenate([a, a], -1)
    sign = np.concatenate([-np.ones(HD // 2), np.ones(HD // 2)])
    tabs = np.stack([two(cos * scale) * 8.0, two(sin * scale) * sign * 8.0,
                     two(cos / scale), two(sin / scale) * sign])
    tabs = tabs.reshape(4, J, P, HD).transpose(2, 0, 1, 3).astype(f)
    step = two((base ** (P / (WINDOW // 2)))[None, :])[0]
    decay = np.tile(step, 2).astype(f)[:, None]
    return np.ascontiguousarray(tabs), np.ascontiguousarray(decay)


def mask_constant():
    i = np.arange(P)[:, None]
    k = np.arange(KEYS)[None, :] - WINDOW
    window = np.floor_divide(i, WINDOW) * WINDOW
    seen = (k >= window - WINDOW) & (k < window + WINDOW) & (i >= k) & (i <= k + WINDOW)
    both = np.stack([seen & (k >= 0), seen])
    m = np.where(both, 0.0, MASKED).astype(np.float32).transpose(1, 0, 2)
    return np.ascontiguousarray(np.repeat(m[:, :, None, :], 2, axis=2))


def windowed_transformer(nc, w, x_outer, out):
    ctx = ExitStack()
    with ctx:
        m = Memory(nc, ctx, "d")
        xs = m.sb("xs", [P, J + 2, B, D])
        xb = m.sb("xb", [P, J, B, D // 2])
        wh = m.sb("wqkv_hi", [P, 3 * INNER], F32R)
        wl = m.sb("wqkv_lo", [P, 3 * INNER], F32R)
        wstage = m.sb("wstage", [P, 1024])
        wo = m.sb("wo", [P, PAIRS, D])
        w1raw = m.sb("w1raw", [P, 2 * FF])
        w1h = m.sb("w1_hi", [P, 2 * FF], F32R)
        w1l = m.sb("w1_lo", [P, 2 * FF], F32R)
        w2 = m.sb("w2", [P, 3, D])
        vecs = m.sb("vectors", [P, 2 + 6])
        b2row = m.sb("b2row", [1, D])
        ones1 = m.sb("ones1", [1, P])
        tabs = m.sb("tables", [P, 4, (J + 1) * HD])
        qks = m.sb("qk_scale", [P, 4, HD])
        decay = m.sb("decay", [P, 1])
        mask = m.sb("mask", [P, 2, 2 * KEYS], BF16)
        ident = m.sb("ident", [P, P])
        identb = m.sb("identb", [P, P], BF16)
        magic = m.sb("magic", [P, HEADS], I32)
        kexp = [m.sb(f"k_expanded{b}", [P, PAIRS, 2, KEYS]) for b in range(B)]
        vcur = [m.sb(f"v{b}", [P, INNER]) for b in range(B)]
        vhalo = [m.sb(f"v_before{b}", [P, INNER]) for b in range(B)]

        A = [m.bank("A0"), m.bank("A1")]
        T0, O0 = m.bank("T0"), m.bank("O0")
        S = [m.bank("S0"), m.bank("S1")]
        PT = [m.bank("PT0"), m.bank("PT1")]

        init = m.sem("init")
        waits_met = m.sem("waits_met")
        x_ln = m.sem("x_ln")

        with ExitStack() as c2, nc.Block() as block:
            m2 = Memory(nc, c2, "d0")
            maskf = m2.sb("maskf", [P, 2, 2 * KEYS])
            stats = m2.sb("stats", [P, N_TILES, 6])
            mv = m2.sb("mv", [P, N_TILES, 2])
            ve = m2.sb("ve", [P, N_TILES])
            rstd = m2.sb("rstd", [P, N_TILES])
            tmp = m2.sb("tmp", [P, N_TILES])
            magic32 = m2.sb("magic32", [P, N_TILES], I32)
            loaded, zeroed, stat, steps, mbf = (m2.sem(s) for s in ("loaded", "zeroed", "stat", "steps", "mbf"))

            @block.sync
            def _(sp):
                sp.dma_start(maskf[:], w["mask"].rearrange("p v h k -> p v (h k)")).then_inc(loaded, DMA)
                sp.dma_start(ident[:], w["ident"]).then_inc(loaded, DMA)
                sp.dma_start(decay[:], w["decay"]).then_inc(loaded, DMA)

            @block.gpsimd
            def _(pool):
                for b in range(B):
                    nc.gpsimd.memset(vcur[b][:], 0.0).then_inc(init, 1)
                    nc.gpsimd.memset(kexp[b][:], 0.0).then_inc(init, 1)
                nc.gpsimd.memset(ones1[:], 1.0).then_inc(init, 1)
                nc.gpsimd.memset(tabs[:, :, J * HD:(J + 1) * HD], 0.0).then_inc(init, 1)

            @block.vector
            def _(v):
                nc.vector.memset(xs[:].rearrange("p j b d -> p (j b d)"), 0.0).then_inc(zeroed, 1)
                nc.vector.memset(magic[:], RSQRT_MAGIC + 1).then_inc(zeroed, 1)
                for b in range(B):
                    nc.vector.memset(vhalo[b][P - WINDOW:P, :], 0.0).then_inc(init, 1)
                nc.vector.memset(magic32[:], RSQRT_MAGIC + 1).then_inc(zeroed, 1)
                for n in range(N_TILES):
                    nc.vector.bn_stats(stats[:, n, :], x_outer[:, n, :]).then_inc(stat, 1)
                v.wait_ge(stat, N_TILES)
                for n in range(N_TILES):
                    nc.vector.bn_aggr(mv[:, n, :], stats[:, n, :]).then_inc(stat, 1)
                v.wait_ge(stat, 2 * N_TILES)
                nc.vector.tensor_scalar(ve[:], mv[:, :, 1], LN_EPS, None, ALU.add).then_inc(stat, 1)
                v.wait_ge(stat, 2 * N_TILES + 1)
                v.wait_ge(zeroed, 3)
                rsqrt_steps(nc, v, ve[:], rstd[:], tmp[:], magic32[:], steps, 0, waits_met)
                v.wait_ge(steps, RSQRT_STEPS)
                for n in range(N_TILES):
                    for half, dst in ((0, xs[:, n // B, n % B, 0:64]), (1, xb[:, n // B, n % B, :])):
                        nc.vector.tensor_scalar(dst, x_outer[:, n, 64 * half:64 * half + 64], mv[:, n, 0:1],
                                                rstd[:, n:n + 1], ALU.subtract, ALU.mult).then_inc(x_ln, 1)
                v.wait_ge(loaded, 3 * DMA)
                nc.vector.tensor_copy(mask[:], maskf[:]).then_inc(mbf, 1)
                nc.vector.tensor_copy(identb[:], ident[:]).then_inc(mbf, 1)

        xcur = m.sb("x_tile", [P, D])
        xh = m.sb("xT_hi", [P, P], F32R)
        xl = m.sb("xT_lo", [P, P], F32R)
        raw = m.sb("qk", [P, 2, INNER])
        sq = m.sb("squares", [P, 2, INNER])
        sn = m.sb("sin_terms", [P, 2, INNER])
        ssq = m.sb("sum_squares", [P, 2, HEADS])
        rn = m.sb("inv_norm", [P, 2, HEADS])
        rt = m.sb("newton_tmp", [P, HEADS])
        qT = m.sb("qT", [P, PAIRS, P])
        nmax = m.sb("neg_max", [P, HEADS])
        pr = m.sb("probs", [P, 2, 2, KEYS])
        den = m.sb("den", [P, HEADS])
        rden = m.sb("inv_den", [P, HEADS])
        pT = m.sb("probsT", [P, 2, 2 * P])
        pTh = m.sb("probsT_before", [P, 2, 2 * WINDOW])
        o_n = m.sb("attn", [P, INNER])
        oT = m.sb("attnT", [P, PAIRS, P])
        fst = m.sb("ff_stats", [P, G4, 6])
        fmv = m.sb("ff_mv", [P, G4, 2])
        fve = m.sb("ff_ve", [P, G4])
        frs = m.sb("ff_rstd", [P, G4])
        frt = m.sb("ff_tmp", [P, G4])
        xn = m.sb("ff_xn", [P, G4, D])
        fx = m.sb("ff_xT", [P, G4 * P])
        fxh = m.sb("ff_xT_hi", [P, G4 * P], F32R)
        fxl = m.sb("ff_xT_lo", [P, G4 * P], F32R)
        gl = m.sb("gelu", [P, 2, G4 * P])
        act_t = m.sb("actT", [P, 3, G4 * P])

        shift_main = m.sem("shift_main")
        shift_row = m.sem("shift_row")
        w_dma = m.sem("w_dma")
        wo_dma = m.sem("wo_dma")
        small_dma = m.sem("small_dma")
        tab_dma = m.sem("tab_dma")
        w_hi, w_lo = m.sem("w_hi"), m.sem("w_lo")
        tab_ready = m.sem("tab_ready")
        w1_hi, w1_lo = m.sem("w1_hi"), m.sem("w1_lo")
        x_tile_ready = m.sem("x_tile_ready")
        xT_ps = m.sem("xT_ps")
        xh_ready, xl_ready = m.sem("xh_ready"), m.sem("xl_ready")
        proj_ps, proj_copied, proj_squared = m.sem("proj_ps"), m.sem("proj_copied"), m.sem("proj_squared")
        ssq_ready = m.sem("ssq_ready")
        ssq_floor = m.sem("ssq_floor")
        newton = m.sem("newton")
        normed = m.sem("normed")
        cos_done, sin_done, rotated = m.sem("cos_done"), m.sem("sin_done"), m.sem("rotated")
        qk_T_ps = m.sem("qk_T_ps")
        q_T_ready = m.sem("q_T_ready")
        k_T_low, k_T_high = m.sem("k_T_low"), m.sem("k_T_high")
        k_before = m.sem("k_before")
        v_before = m.sem("v_before")
        scores_ps, max_done, exp_done = m.sem("scores_ps"), m.sem("max_done"), m.sem("exp_done")
        pT_ps, pT_ready, pTh_ready = m.sem("pT_ps"), m.sem("pT_ready"), m.sem("pTh_ready")
        pv_ps = m.sem("pv_ps")
        rden_ready, attn_ready = m.sem("rden_ready"), m.sem("attn_ready")
        aT_ps, aT_ready = m.sem("aT_ps"), m.sem("aT_ready")
        wo_ps, resid_a = m.sem("wo_ps"), m.sem("resid_a")
        f_stat, f_aggr, f_ve, f_newton = m.sem("f_stat"), m.sem("f_aggr"), m.sem("f_ve"), m.sem("f_newton")
        f_xn, f_xT_ps, f_xT, f_xh, f_xl = (m.sem(s) for s in ("f_xn", "f_xT_ps", "f_xT", "f_xh", "f_xl"))
        f_gate_ps, f_a_ps, f_gelu, f_act = (m.sem(s) for s in ("f_gate_ps", "f_a_ps", "f_gelu", "f_act"))
        f_out_ps, resid_f = m.sem("f_out_ps"), m.sem("resid_f")

        U = N_TILES
        MLP_LOADS = 4
        FRONTS = U + 1

        with nc.Block() as block:

            @block.sync
            def _(sp):
                def shift(j0, nj, sem):
                    sp.dma_start(xs[1:P, bass.ds(j0, nj), :, D // 2:D], xb[0:P - 1, bass.ds(j0, nj), :, :]).then_inc(sem, DMA)

                def shift_rows():
                    sp.dma_start(xs[0:1, 1:J, :, D // 2:D], xb[P - 1:P, 0:J - 1, :, :]).then_inc(shift_row, DMA)

                shift(0, J, shift_main)
                shift_rows()
                with sp.Fori(0, DEPTH) as l:
                    with sp.Fori(0, J) as j:
                        sp.wait_ge(resid_a, (l * U + j * 2) * 2 + 6)
                        shift(j, 1, shift_main)
                    sp.wait_ge(x_tile_ready, (l + 1) * FRONTS)
                    shift_rows()
                    with sp.Fori(0, GROUPS) as g:
                        sp.wait_ge(resid_f, (l * GROUPS + g) * 2 + 2)
                        shift(g * 2, 2, shift_main)
                    shift_rows()
                sp.wait_ge(shift_main, DMA * (1 + DEPTH * (J + GROUPS)))
                sp.wait_ge(shift_row, DMA * (1 + 2 * DEPTH))

            SHIFTS = J + GROUPS

            @block.gpsimd
            def _(pool):
                def prepare_attention(l, ln):
                    for c in range(3):
                        pool.dma_start(wstage[:], w["Wqkv"][bass.ds(ln, 1), :, c * 1024:(c + 1) * 1024]
                                       .rearrange("l p n -> p (l n)")).then_inc(w_dma, DMA)
                        if c == 0:
                            pool.dma_start(wo[:], w["Wo"][bass.ds(ln, 1)].rearrange("l (c p) n -> p (l c) n", p=P)
                                           ).then_inc(wo_dma, DMA)
                            pool.dma_start(tabs[:, :, 0:J * HD], w["rotary"].rearrange("p a j d -> p a (j d)")).then_inc(tab_dma, DMA)
                            for a, name in enumerate(("q_scale", "q_swap", "k_scale", "k_swap")):
                                pool.dma_start(qks[:, a, :], w[name][bass.ds(ln, 1), :].broadcast_to([P, HD])
                                               ).then_inc(tab_dma, DMA)
                        pool.wait_ge(w_dma, (l * 3 + c + 1) * DMA)
                        sl = slice(c * 1024, (c + 1) * 1024)
                        pool.sem_inc(waits_met)
                        nc.gpsimd.tensor_copy(wh[:, sl], wstage[:]).then_inc(w_hi, 1)
                        pool.wait_ge(w_hi, upto(l, 3, c))
                        nc.gpsimd.tensor_tensor(wl[:, sl], wstage[:], wh[:, sl].bitcast(F32), ALU.subtract).then_inc(w_lo, 1)
                        pool.wait_ge(w_lo, upto(l, 3, c))
                    pool.wait_ge(tab_dma, (l + 1) * 5 * DMA)
                    for a in range(4):
                        t3 = tabs[:, a, 0:J * HD].rearrange("p (j d) -> p j d", d=HD)
                        nc.gpsimd.tensor_tensor(t3, t3, qks[:, a, :].unsqueeze(1).broadcast_to([P, J, HD]), ALU.mult
                                                ).then_inc(tab_ready, 1)

                def load_mlp(l):
                    pool.dma_start(w1raw[:], w["W1"][bass.ds(l, 1)].rearrange("l p n -> p (l n)")).then_inc(small_dma, DMA)
                    pool.dma_start(w2[:], w["W2"][bass.ds(l, 1)].rearrange("l p c n -> p (l c) n")).then_inc(small_dma, DMA)
                    pool.dma_start(vecs[:], w["vectors"][bass.ds(l, 1)].rearrange("l p n -> p (l n)")).then_inc(small_dma, DMA)
                    pool.dma_start(b2row[:], w["b2"][bass.ds(l, 1), :]).then_inc(small_dma, DMA)
                    pool.wait_ge(small_dma, (l + 1) * (MLP_LOADS * DMA))
                    pool.sem_inc(waits_met)
                    nc.gpsimd.tensor_copy(w1h[:], w1raw[:]).then_inc(w1_hi, 1)
                    pool.wait_ge(w1_hi, l + 1)
                    nc.gpsimd.tensor_tensor(w1l[:], w1raw[:], w1h[:].bitcast(F32), ALU.subtract).then_inc(w1_lo, 1)

                def rotate(f, j, k):
                    pool.wait_ge(normed, upto(f, 2, k))
                    v4 = raw[:, k, :].rearrange("p (h s d) -> p h s d", h=HEADS, s=2)
                    o4 = sn[:, k, :].rearrange("p (h s d) -> p h s d", h=HEADS, s=2)
                    tab = tabs[:, 2 * k + 1, bass.ds(j * HD, HD)]
                    for s in range(2):
                        nc.gpsimd.tensor_tensor(o4[:, :, s, :], v4[:, :, 1 - s, :],
                                                tab[:, 32 * s:32 * s + 32].unsqueeze(1).broadcast_to([P, HEADS, 32]),
                                                ALU.mult).then_inc(sin_done, 1)
                    pool.wait_ge(sin_done, (f * 2 + k) * 2 + 2)
                    pool.wait_ge(cos_done, upto(f, 2, k))
                    nc.gpsimd.tensor_tensor(raw[:, k, :], sq[:, k, :], sn[:, k, :], ALU.add).then_inc(rotated, 1)

                prepare_attention(0, 0)
                with pool.Fori(0, DEPTH) as l:
                    pool.wait_ge(shift_main, DMA * (l * SHIFTS + 1))
                    pool.wait_ge(shift_row, DMA * (2 * l + 1))
                    f0 = l * FRONTS
                    pool.sem_inc(waits_met)
                    nc.gpsimd.tensor_copy(xcur[:], xs[:, 0, 0, :]).then_inc(x_tile_ready, 1)
                    load_mlp(l)
                    pool.wait_ge(tab_ready, (l + 1) * 4)
                    rotate(f0, 0, 0)
                    rotate(f0, 0, 1)
                    with pool.Fori(0, J) as j:
                        for b in range(B):
                            f = f0 + j * 2 + (b + 1)
                            jn = j + b
                            pool.wait_ge(xT_ps, f)
                            nc.gpsimd.tensor_copy(xcur[:], xs[:, bass.ds(jn, 1), 1 - b, :].rearrange("p j d -> p (j d)")
                                                  ).then_inc(x_tile_ready, 1)
                            rotate(f, jn, 0)
                            rotate(f, jn, 1)
                    pool.wait_ge(proj_ps, (l + 1) * (FRONTS * 6))
                    pool.wait_ge(wo_ps, (l + 1) * U)
                    pool.wait_ge(cos_done, (l + 1) * (FRONTS * 2))
                    pool.wait_ge(sin_done, (l + 1) * (FRONTS * 4))
                    prepare_attention(l + 1, (l + 1) % DEPTH)
                pool.wait_ge(w_lo, 3 * (DEPTH + 1))
                pool.wait_ge(tab_ready, 4 * (DEPTH + 1))
                pool.wait_ge(wo_dma, DMA * (DEPTH + 1))

            

            @block.tensor
            def _(pe):
                def project(f, c):
                    if c == 0:
                        pe.wait_ge(xh_ready, f + 1)
                        pe.wait_ge(xl_ready, f + 1)
                    if c >= 2:
                        pe.wait_ge(proj_copied, f * 6 + (c - 1))
                        pe.wait_ge(proj_squared, f * 4 + min(c - 1, 4))
                    sl = slice(c * 512, (c + 1) * 512)
                    nc.tensor.matmul(A[c % 2][:], xh[:], wh[:, sl], start=True, stop=False)
                    nc.tensor.matmul(A[c % 2][:], xl[:], wh[:, sl], start=False, stop=False)
                    nc.tensor.matmul(A[c % 2][:], xh[:], wl[:, sl], start=False, stop=True).then_inc(proj_ps, 1)

                def qk_transposes(f, i):
                    bank = (T0, O0)[i % 2]
                    k, half = i // 2, i % 2
                    pe.wait_ge(rotated, upto(f, 2, k))
                    for p in range(4):
                        col = (4 * half + p) * P
                        last = nc.tensor.transpose(bank[:, p * P:(p + 1) * P], raw[:, k, col:col + P], ident[:])
                    last.then_inc(qk_T_ps, 1)

                def scores(a, p, b, first_tile):
                    s = S[p % 2]
                    pe.wait_ge(exp_done, a * 16 + (2 * p - 2)) if p >= 2 else None
                    nc.tensor.matmul(s[:, 0:2 * KEYS], qT[:, p, :], kexp[b][:, p, :, :].rearrange("p h k -> p (h k)"),
                                     start=True, stop=False)
                    nc.tensor.matmul(s[:, 0:2 * KEYS], identb[:], mask[:, bass.ds(first_tile, 1), :].rearrange("p v k -> p (v k)"),
                                     start=False, stop=True).then_inc(scores_ps, 1)

                def transpose_probs(a, p):
                    pe.wait_ge(exp_done, a * 16 + (2 * p + 2))
                    if p >= 2:
                        pe.wait_ge(pT_ready, a * 8 + (p - 1))
                    for h in range(2):
                        last = nc.tensor.transpose(PT[p % 2][:, h * P:(h + 1) * P], pr[:, p % 2, h, WINDOW:KEYS], ident[:])
                    last.then_inc(pT_ps, 1)

                def attend(a, p, b):
                    pe.wait_ge(pT_ready, a * 8 + (p + 1))
                    pe.wait_ge(pTh_ready, a * 8 + (p + 1))
                    bank = O0 if p < 4 else T0
                    for h in range(2):
                        col = ((p % 4) * 2 + h) * HD
                        vcol = (2 * p + h) * HD
                        nc.tensor.matmul(bank[:, col:col + HD], pT[:, p % 2, h * P:(h + 1) * P],
                                         vcur[b][:, vcol:vcol + HD], start=True, stop=True)
                        last = nc.tensor.matmul(bank[0:WINDOW, col:col + HD],
                                                pTh[P - WINDOW:P, p % 2, h * WINDOW:(h + 1) * WINDOW],
                                                vhalo[b][P - WINDOW:P, vcol:vcol + HD], start=False, stop=True,
                                                skip_group_check=True)
                    last.then_inc(pv_ps, 1)

                def transpose_attention(a, half):
                    pe.wait_ge(attn_ready, a * 2 + (half + 3))
                    if half:
                        pe.wait_ge(aT_ready, a * 2 + 1)
                    for p in range(4):
                        col = (4 * half + p) * P
                        last = nc.tensor.transpose(A[0][:, p * P:(p + 1) * P], o_n[:, col:col + P], ident[:])
                    last.then_inc(aT_ps, 1)

                def project_out(a, half):
                    pe.wait_ge(aT_ready, a * 2 + (half + 1))
                    for p in range(4 * half, 4 * half + 4):
                        last = nc.tensor.matmul(O0[:, 0:D], oT[:, p, :], wo[:, p, :], start=(p == 0), stop=(p == 7))
                    if half:
                        last.then_inc(wo_ps, 1)

                with pe.Fori(0, DEPTH) as l:
                    f0 = l * FRONTS
                    pe.wait_ge(w_hi, (l + 1) * 3)
                    pe.wait_ge(w_lo, (l + 1) * 3)
                    pe.wait_ge(wo_dma, (l + 1) * DMA)
                    pe.wait_ge(x_tile_ready, f0 + 1)
                    nc.tensor.transpose(T0[:, 0:P], xcur[:], ident[:]).then_inc(xT_ps, 1)
                    for c in range(6):
                        project(f0, c)
                    with pe.Fori(0, J) as j:
                        for b in range(B):
                            u = j * 2 + b
                            a = l * U + u
                            f = f0 + (u + 1)
                            first_tile = (j + (J - 1)) // J
                            pe.wait_ge(x_tile_ready, f + 1)
                            pe.wait_ge(xl_ready, f)
                            pe.wait_ge(proj_copied, f * 6)
                            pe.wait_ge(attn_ready, a * 2 + 2)
                            nc.tensor.transpose(T0[:, 0:P], xcur[:], ident[:]).then_inc(xT_ps, 1)
                            pe.wait_ge(resid_a, a * 2 + 2)
                            qk_transposes(f - 1, 1)
                            pe.wait_ge(xl_ready, f + 1)
                            qk_transposes(f - 1, 0)
                            pe.wait_ge(q_T_ready, a * 2 + 1)
                            qk_transposes(f - 1, 3)
                            pe.wait_ge(q_T_ready, a * 2 + 2)
                            qk_transposes(f - 1, 2)
                            pe.wait_ge(k_T_low, a * 2 + 2)
                            pe.wait_ge(k_T_high, a * 2 + 2)
                            pe.wait_ge(k_before, a + 1)
                            scores(a, 0, b, first_tile)
                            project(f, 0)
                            scores(a, 1, b, first_tile)
                            pe.wait_ge(v_before, a + 1)
                            for p in range(PAIRS):
                                transpose_probs(a, p)
                                if p + 2 < PAIRS:
                                    scores(a, p + 2, b, first_tile)
                                if p < 4:
                                    project(f, p + 1)
                                if p == 5:
                                    pe.wait_ge(proj_copied, f * 6 + 5)
                                    transpose_attention(a, 0)
                                if p == 6:
                                    project_out(a, 0)
                                if p == 7:
                                    project(f, 5)
                                attend(a, p, b)
                            transpose_attention(a, 1)
                            project_out(a, 1)
                    pe.wait_ge(w1_hi, l + 1)
                    pe.wait_ge(w1_lo, l + 1)
                    pe.wait_ge(small_dma, (l + 1) * (MLP_LOADS * DMA))

                    def transpose_group(gi):
                        pe.wait_ge(f_xn, gi * 4 + 4)
                        for t in range(G4):
                            last = nc.tensor.transpose(T0[:, t * P:(t + 1) * P], xn[:, t, :], ident[:])
                        last.then_inc(f_xT_ps, 1)

                    pe.wait_ge(attn_ready, (l + 1) * (U * 2) + 2)
                    pe.wait_ge(resid_a, (l + 1) * (U * 2) + 2)
                    m0 = l * (GROUPS + 1)
                    transpose_group(m0)
                    with pe.Fori(0, GROUPS) as g:
                        q = l * GROUPS + g
                        mg = m0 + g
                        pe.wait_ge(f_xh, mg + 1)
                        pe.wait_ge(f_xl, mg + 1)
                        for c, (o, sz) in enumerate(FF_CHUNKS):
                            for k, banks, ready in ((1, S, f_gate_ps), (0, PT, f_a_ps)):
                                bank = banks[c % 2]
                                if c == 2:
                                    pe.wait_ge(f_gelu if k else f_act, q * 3 + 1)
                                sl = slice(k * FF + o, k * FF + o + sz)
                                nc.tensor.matmul(bank[0:sz, :], w1h[:, sl], fxh[:], start=True, stop=False)
                                nc.tensor.matmul(bank[0:sz, :], w1l[:, sl], fxh[:], start=False, stop=False)
                                nc.tensor.matmul(bank[0:sz, :], w1h[:, sl], fxl[:], start=False, stop=True).then_inc(ready, 1)
                        transpose_group(mg + 1)
                        pe.wait_ge(f_act, q * 3 + 3)
                        for t in range(G4):
                            for c, (o, sz) in enumerate(FF_CHUNKS):
                                nc.tensor.matmul(O0[:, t * P:(t + 1) * P], act_t[0:sz, c, t * P:(t + 1) * P],
                                                 w2[0:sz, c, :], start=(c == 0), stop=False)
                            last = nc.tensor.matmul(O0[:, t * P:(t + 1) * P], ones1[0:1, :], b2row[0:1, :],
                                                    start=False, stop=True)
                        last.then_inc(f_out_ps, 1)
                        pe.wait_ge(resid_f, q * 2 + 2)

            @block.scalar
            def _(act):
                def split_x(f):
                    act.wait_ge(xT_ps, f + 1)
                    nc.scalar.activation(xh[:], T0[:, 0:P], ACT.Copy).then_inc(xh_ready, 1)

                def drain(f, c):
                    act.wait_ge(proj_ps, f * 6 + (c + 1))
                    if c < 4:
                        k, half = c // 2, c % 2
                        dst = raw[:, k, half * 512:half * 512 + 512]
                        nc.scalar.activation(dst, A[c % 2][:], ACT.Copy).then_inc(proj_copied, 1)
                        nc.scalar.activation(sq[:, k, half * 512:half * 512 + 512], A[c % 2][:], ACT.Square
                                             ).then_inc(proj_squared, 1)

                def drain_v(f, c, b):
                    act.wait_ge(proj_ps, f * 6 + (c + 1))
                    nc.scalar.activation(vcur[b][:, (c - 4) * 512:(c - 3) * 512], A[c % 2][:], ACT.Copy
                                         ).then_inc(proj_copied, 1)

                def exps(a, p):
                    act.wait_ge(max_done, a * 8 + (p + 1))
                    if p >= 2:
                        act.wait_ge(pT_ps, a * 8 + (p - 1))
                        act.wait_ge(pTh_ready, a * 8 + (p - 1))
                    for h in range(2):
                        nc.scalar.activation(pr[:, p % 2, h, :], S[p % 2][:, h * KEYS:(h + 1) * KEYS], ACT.Exp,
                                             bias=nmax[:, 2 * p + h:2 * p + h + 1],
                                             accum_out=den[:, 2 * p + h:2 * p + h + 1]).then_inc(exp_done, 1)

                def attn_T(a, half):
                    act.wait_ge(aT_ps, a * 2 + (half + 1))
                    nc.scalar.activation(oT[:, 4 * half:4 * half + 4, :], A[0][:], ACT.Copy).then_inc(aT_ready, 1)

                with act.Fori(0, DEPTH) as l:
                    f0 = l * FRONTS
                    split_x(f0)
                    for c in range(4):
                        drain(f0, c)
                    drain_v(f0, 4, 0)
                    drain_v(f0, 5, 0)
                    with act.Fori(0, J) as j:
                        for b in range(B):
                            a = l * U + j * 2 + b
                            f = f0 + (j * 2 + (b + 1))
                            split_x(f)
                            for half, bank in ((1, O0), (0, T0)):
                                act.wait_ge(qk_T_ps, a * 4 + (1 if half else 2))
                                nc.scalar.activation(qT[:, 4 * half:4 * half + 4, :], bank[:], ACT.Copy).then_inc(q_T_ready, 1)
                            act.wait_ge(k_before, a + 1)
                            for half, bank in ((1, O0), (0, T0)):
                                act.wait_ge(qk_T_ps, a * 4 + (3 if half else 4))
                                nc.scalar.activation(kexp[b][0:64, 4 * half:4 * half + 4, 0, WINDOW:KEYS],
                                                     bank[0:64, :].rearrange("p (c t) -> p c t", c=4), ACT.Copy
                                                     ).then_inc(k_T_low, 1)
                            exps(a, 0)
                            drain(f, 0)
                            exps(a, 1)
                            for p in range(PAIRS):
                                if p < 3:
                                    drain(f, p + 1)
                                if p == 3:
                                    act.wait_ge(v_before, a + 1)
                                    drain_v(f, 4, 1 - b)
                                if p + 2 < PAIRS:
                                    exps(a, p + 2)
                                if p == 5:
                                    attn_T(a, 0)
                                if p == 7:
                                    drain_v(f, 5, 1 - b)
                            attn_T(a, 1)
                    def split_group(mg):
                        act.wait_ge(f_xT_ps, mg + 1)
                        nc.scalar.activation(fx[:], T0[:], ACT.Identity, scale=vecs[:, 0:1], bias=vecs[:, 1:2]).then_inc(f_xT, 1)
                        act.wait_ge(f_xT, mg + 1)
                        nc.scalar.activation(fxh[:], fx[:], ACT.Copy).then_inc(f_xh, 1)

                    act.wait_ge(small_dma, (l + 1) * (MLP_LOADS * DMA))
                    m0 = l * (GROUPS + 1)
                    split_group(m0)
                    with act.Fori(0, GROUPS) as g:
                        q = l * GROUPS + g
                        for c, (o, sz) in enumerate(FF_CHUNKS):
                            act.wait_ge(f_gate_ps, q * 3 + (c + 1))
                            if c == 2:
                                act.wait_ge(f_act, q * 3 + 1)
                            nc.scalar.activation(gl[0:sz, c % 2, :], S[c % 2][0:sz, :], ACT.Gelu,
                                                 bias=vecs[0:sz, 5 + c:6 + c]).then_inc(f_gelu, 1)
                        act.wait_ge(f_a_ps, q * 3 + 3)
                        split_group(m0 + g + 1)

            @block.vector
            def _(v):
                def split_x_low(f):
                    v.wait_ge(xh_ready, f + 1)
                    nc.vector.tensor_tensor(xl[:], T0[:, 0:P], xh[:].bitcast(F32), ALU.subtract).then_inc(xl_ready, 1)

                def norms(f, k):
                    v.wait_ge(proj_squared, f * 4 + (2 * k + 2))
                    nc.vector.tensor_reduce(ssq[:, k, :], sq[:, k, :].rearrange("p (h d) -> p h d", d=HD), AX.X, ALU.add
                                            ).then_inc(ssq_ready, 1)
                    v.wait_ge(ssq_ready, f * 2 + (k + 1))
                    nc.vector.tensor_scalar(ssq[:, k, :], ssq[:, k, :], 1e-24, None, ALU.max).then_inc(ssq_floor, 1)
                    v.wait_ge(ssq_floor, f * 2 + (k + 1))
                    rsqrt_steps(nc, v, ssq[:, k, :], rn[:, k, :], rt[:], magic[:], newton, (f * 2 + k) * RSQRT_STEPS, waits_met)
                    v.wait_ge(newton, (f * 2 + k) * RSQRT_STEPS + RSQRT_STEPS)

                def normalise(f, k, j):
                    v.wait_ge(proj_copied, f * 6 + (2 * k + 2))
                    r3 = raw[:, k, :].rearrange("p (h d) -> p h d", d=HD)
                    nc.vector.tensor_tensor(r3, r3, rn[:, k, :].unsqueeze(2).broadcast_to([P, HEADS, HD]), ALU.mult
                                            ).then_inc(normed, 1)
                    v.wait_ge(normed, f * 2 + (k + 1))
                    nc.vector.tensor_tensor(sq[:, k, :].rearrange("p (h d) -> p h d", d=HD), r3,
                                            tabs[:, 2 * k, bass.ds(j * HD, HD)].unsqueeze(1).broadcast_to([P, HEADS, HD]),
                                            ALU.mult).then_inc(cos_done, 1)

                def row_max(a, p):
                    v.wait_ge(scores_ps, a * 8 + (p + 1))
                    nc.vector.tensor_reduce(nmax[:, 2 * p:2 * p + 2],
                                            S[p % 2][:, 0:2 * KEYS].rearrange("p (h k) -> p h k", h=2), AX.X, ALU.max,
                                            negate=True).then_inc(max_done, 1)

                def drain_probs(a, p):
                    v.wait_ge(exp_done, a * 16 + (2 * p + 2))
                    if p >= 2:
                        v.wait_ge(pv_ps, a * 8 + (p - 1))
                    nc.vector.transpose(pTh[P - WINDOW:P, p % 2, :].rearrange("p (h k) -> p h k", h=2),
                                        pr[0:WINDOW, p % 2, :, 0:WINDOW]).then_inc(pTh_ready, 1)
                    v.wait_ge(pT_ps, a * 8 + (p + 1))
                    nc.vector.tensor_copy(pT[:, p % 2, :], PT[p % 2][:, 0:2 * P]).then_inc(pT_ready, 1)

                def normalise_attention(a, half):
                    hs = slice(8 * half, 8 * half + 8)
                    v.wait_ge(exp_done, a * 16 + (8 * half + 8))
                    nc.vector.reciprocal(rden[:, hs], den[:, hs]).then_inc(rden_ready, 1)
                    v.wait_ge(rden_ready, a * 2 + (half + 1))
                    v.wait_ge(pv_ps, a * 8 + (4 * half + 4))
                    ins = nc.vector.tensor_tensor(o_n[:, half * 512:half * 512 + 512].rearrange("p (h d) -> p h d", d=HD),
                                                  (O0, T0)[half][:].rearrange("p (h d) -> p h d", d=HD),
                                                  rden[:, hs].unsqueeze(2).broadcast_to([P, 8, HD]), ALU.mult)
                    ins.then_inc(attn_ready, 1)
                    return ins

                def residual(a, j, b):
                    v.wait_ge(wo_ps, a + 1)
                    lo = xs[:, bass.ds(j, 1), b, 0:64].rearrange("p j d -> p (j d)")
                    hi = xb[:, bass.ds(j, 1), b, :].rearrange("p j d -> p (j d)")
                    nc.vector.tensor_tensor(lo, O0[:, 0:64], lo, ALU.add).then_inc(resid_a, 1)
                    nc.vector.tensor_tensor(hi, O0[:, 64:128], hi, ALU.add).then_inc(resid_a, 1)

                nc.vector.nop().then_inc(attn_ready, 2)
                nc.vector.nop().then_inc(resid_a, 2)
                with v.Fori(0, DEPTH) as l:
                    f0 = l * FRONTS
                    v.wait_ge(tab_ready, (l + 1) * 4)
                    split_x_low(f0)
                    norms(f0, 0)
                    normalise(f0, 0, 0)
                    norms(f0, 1)
                    normalise(f0, 1, 0)
                    with v.Fori(0, J) as j:
                        for b in range(B):
                            u = j * 2 + b
                            a = l * U + u
                            f = f0 + (u + 1)
                            jn = j + b
                            kview = kexp[b][:].rearrange("p c h k -> p (c h) k")
                            nc.vector.tensor_scalar(kview[:, :, 0:WINDOW], kview[:, :, P:KEYS], decay[:, 0:1], None,
                                                    ALU.mult).then_inc(k_before, 1)
                            split_x_low(f)
                            v.wait_ge(k_before, a + 1)
                            for half, bank in ((1, O0), (0, T0)):
                                v.wait_ge(qk_T_ps, a * 4 + (3 if half else 4))
                                nc.vector.tensor_copy(kexp[b][64:128, 4 * half:4 * half + 4, 1, WINDOW:KEYS],
                                                      bank[64:128, :].rearrange("p (c t) -> p c t", c=4)
                                                      ).then_inc(k_T_high, 1)
                            row_max(a, 0)
                            nc.vector.tensor_copy(vhalo[1 - b][P - WINDOW:P, :], vcur[1 - b][P - WINDOW:P, :]
                                                  ).then_inc(v_before, 1)
                            row_max(a, 1)
                            for p in range(PAIRS):
                                drain_probs(a, p)
                                if p + 2 < PAIRS:
                                    row_max(a, p + 2)
                                if p == 1:
                                    norms(f, 0)
                                if p == 2:
                                    normalise(f, 0, jn)
                                if p == 3:
                                    norms(f, 1)
                                    normalise_attention(a, 0)
                                if p == 4:
                                    normalise(f, 1, jn)
                            normalise_attention(a, 1)
                            residual(a, j, b)
                    def layernorm(g, mg):
                        xg = xs[:, bass.ds(g * 2, 2), :, :].rearrange("p j b d -> p (j b) d")
                        for t in range(G4):
                            nc.vector.bn_stats(fst[:, t, :], xg[:, t, :]).then_inc(f_stat, 1)
                        v.wait_ge(f_stat, mg * 4 + 4)
                        v.sem_inc(waits_met)
                        for t in range(G4):
                            nc.vector.bn_aggr(fmv[:, t, :], fst[:, t, :]).then_inc(f_aggr, 1)
                        v.wait_ge(f_aggr, mg * 4 + 4)
                        nc.vector.tensor_scalar(fve[:], fmv[:, :, 1], LN_EPS, None, ALU.add).then_inc(f_ve, 1)
                        v.wait_ge(f_ve, mg + 1)
                        rsqrt_steps(nc, v, fve[:], frs[:], frt[:], magic[:, 0:G4], f_newton, mg * RSQRT_STEPS, waits_met)
                        v.wait_ge(f_newton, mg * RSQRT_STEPS + RSQRT_STEPS)
                        for t in range(G4):
                            nc.vector.tensor_scalar(xn[:, t, :], xg[:, t, :], fmv[:, t, 0:1], frs[:, t:t + 1],
                                                    ALU.subtract, ALU.mult).then_inc(f_xn, 1)

                    def split_group_low(mg):
                        v.wait_ge(f_xh, mg + 1)
                        nc.vector.tensor_tensor(fxl[:], fx[:], fxh[:].bitcast(F32), ALU.subtract).then_inc(f_xl, 1)

                    v.wait_ge(shift_main, DMA * (l * SHIFTS + (1 + J)))
                    v.wait_ge(shift_row, DMA * (2 * l + 2))
                    m0 = l * (GROUPS + 1)
                    layernorm(0, m0)
                    split_group_low(m0)
                    with v.Fori(0, GROUPS) as g:
                        q = l * GROUPS + g
                        for c, (o, sz) in enumerate(FF_CHUNKS):
                            v.wait_ge(f_a_ps, q * 3 + (c + 1))
                            v.wait_ge(f_gelu, q * 3 + (c + 1))
                            nc.vector.scalar_tensor_tensor(act_t[0:sz, c, :], PT[c % 2][0:sz, :], vecs[0:sz, 2 + c:3 + c],
                                                           gl[0:sz, c % 2, :], ALU.add, ALU.mult).then_inc(f_act, 1)
                            if c == 0:
                                layernorm(g + 1, m0 + g + 1)
                        split_group_low(m0 + g + 1)
                        v.wait_ge(f_out_ps, q + 1)
                        o3 = O0[:].rearrange("p (t d) -> p t d", t=G4)
                        lo = xs[:, bass.ds(g * 2, 2), :, 0:64].rearrange("p j b d -> p (j b) d")
                        hi = xb[:, bass.ds(g * 2, 2), :, :].rearrange("p j b d -> p (j b) d")
                        nc.vector.tensor_tensor(lo, o3[:, :, 0:64], lo, ALU.add).then_inc(resid_f, 1)
                        nc.vector.tensor_tensor(hi, o3[:, :, 64:128], hi, ALU.add).then_inc(resid_f, 1)

        with ExitStack() as c2, nc.Block() as block:
            m2 = Memory(nc, c2, "d1")
            stats = m2.sb("stats", [P, N_TILES, 2, 6])
            mv = m2.sb("mv", [P, N_TILES, 2])
            ve = m2.sb("ve", [P, N_TILES])
            rstd = m2.sb("rstd", [P, N_TILES])
            tmp = m2.sb("tmp", [P, N_TILES])
            magic32 = m2.sb("magic32", [P, N_TILES], I32)
            zeroed, stat, steps, scaled, summed, stored = (
                m2.sem(s) for s in ("zeroed", "stat", "steps", "scaled", "summed", "stored"))

            @block.vector
            def _(v):
                nc.vector.memset(magic32[:], RSQRT_MAGIC + 1).then_inc(zeroed, 1)
                for n in range(N_TILES):
                    nc.vector.bn_stats(stats[:, n, 0, :], xs[:, n // B, n % B, 0:64]).then_inc(stat, 1)
                    nc.vector.bn_stats(stats[:, n, 1, :], xb[:, n // B, n % B, :]).then_inc(stat, 1)
                v.wait_ge(stat, 2 * N_TILES)
                for n in range(N_TILES):
                    nc.vector.bn_aggr(mv[:, n, :], stats[:, n, :, :].rearrange("p a b -> p (a b)")).then_inc(stat, 1)
                v.wait_ge(stat, 3 * N_TILES)
                nc.vector.tensor_scalar(ve[:], mv[:, :, 1], LN_EPS, None, ALU.add).then_inc(stat, 1)
                v.wait_ge(stat, 3 * N_TILES + 1)
                v.wait_ge(zeroed, 1)
                rsqrt_steps(nc, v, ve[:], rstd[:], tmp[:], magic32[:], steps, 0, waits_met)
                v.wait_ge(steps, RSQRT_STEPS)
                for n in range(N_TILES):
                    for y in (xs[:, n // B, n % B, 0:64], xb[:, n // B, n % B, :]):
                        nc.vector.tensor_scalar(y, y, mv[:, n, 0:1], rstd[:, n:n + 1], ALU.subtract, ALU.mult
                                                ).then_inc(scaled, 1)
                v.wait_ge(scaled, 2 * N_TILES)
                xo = x_outer[:].rearrange("p (j b) d -> p j b d", b=B)
                for b in range(B):
                    for q in range(4):
                        js = slice(q * J // 4, (q + 1) * J // 4)
                        nc.vector.tensor_tensor(xo[:, js, b, 0:64], xo[:, js, b, 0:64], xs[:, js, b, 0:64], ALU.add
                                                ).then_inc(summed, 1)
                        nc.vector.tensor_tensor(xo[:, js, b, 64:D], xo[:, js, b, 64:D], xb[:, js, b, :], ALU.add
                                                ).then_inc(summed, 1)

            @block.sync
            def _(sp):
                xo = x_outer[:].rearrange("p (j b) d -> p j b d", b=B)
                for b in range(B):
                    for q in range(4):
                        js = slice(q * J // 4, (q + 1) * J // 4)
                        sp.wait_ge(summed, 2 * (4 * b + q + 1))
                        sp.dma_start(out[b].rearrange("(j p) d -> p j d", p=P)[:, js, :], xo[:, js, b, :]
                                     ).then_inc(stored, DMA)
                sp.wait_ge(stored, 8 * DMA)



def sandwich_program(nc, x, out, ident_in, conv_w, experts_w, linear_w, windowed_w):
    Memory.taken.clear()
    with ExitStack() as ctx:
        m = Memory(nc, ctx, "m")
        x_tiles = m.sb("x", [P, N_TILES, D])
        with ExitStack() as c1:
            m1 = Memory(nc, c1, "m1")
            ident = m1.sb("ident", [P, P])
            with nc.Block() as block:
                loaded = m1.sem("loaded")

                @block.sync
                def _(sp):
                    x4 = x_tiles[:].rearrange("p (j b) d -> p j b d", b=B)
                    for b in range(B):
                        sp.dma_start(x4[:, :, b, :], x[b].rearrange("(j p) d -> p j d", p=P)).then_inc(loaded, DMA)
                    sp.dma_start(ident[:], ident_in).then_inc(loaded, DMA)
                    sp.wait_ge(loaded, 3 * DMA)
            conv_attention_mixture(nc, conv_w, x_tiles, ident)
            fp4_experts(nc, experts_w, x_tiles, ident)
            linear_attention(nc, linear_w, x_tiles, ident)
        release_semaphores(nc)
        windowed_transformer(nc, windowed_w, x_tiles, out)


def conv_layout(a):
    head4, causal, blocks = head_constants()
    return dict(
        w_pw=a["w_pw"].T, w_dw=a["w_dw"], w_qkv=a["w_qkv"].T, w_gate=a["w_gate"].T, w_o=a["w_o"].T,
        b_gate=a["b_gate"].reshape(1, D), rope=rope_constants(), head4=head4, causal=causal, blocks=blocks,
        ln_g_b=np.stack([a["ln_g"], a["ln_b"]], 1), w1=a["w1"].transpose(2, 0, 1).reshape(D, AE * AF),
        w_moe_gate=a["w_moe_gate"].T, b2=a["b2"], b1=a["b1"].reshape(AE * AC, P).T,
        w2=a["w2"].transpose(0, 2, 1).reshape(AE, AC, P, D).transpose(2, 0, 1, 3).reshape(P, AE * AC, D))


def experts_layout(a):
    evens_first = np.concatenate([np.arange(0, D, 2), np.arange(1, D, 2)])
    return dict(
        router=a["router_w"].T[evens_first], bias_down=a["bias_down"],
        iota=np.tile(np.arange(16, dtype=np.float32), (P, 1)),
        blocks_gu=a["blocks_gu"].transpose(2, 0, 1).reshape(64, -1),
        scales_gu=a["scales_gu"].transpose(2, 0, 1).reshape(4, -1),
        blocks_down=a["blocks_down"].transpose(2, 0, 1).reshape(128, -1),
        scales_down=a["scales_down"].transpose(2, 0, 1).reshape(8, -1),
        bias_gu=a["bias_gu"].reshape(16, 2, P, 2).transpose(2, 0, 1, 3).reshape(P, 16, 4))


def windowed_layout(a):
    rotary, decay = rotary_constants()
    w2 = np.zeros((DEPTH, 3 * P, D), np.float32)
    w2[:, :FF] = a["W2"]
    vectors = np.zeros((DEPTH, P, 2 + 6), np.float32)
    vectors[:, :, 0], vectors[:, :, 1] = a["ln_g"], a["ln_b"]
    for c, (first, size) in enumerate(FF_CHUNKS):
        for k in range(2):
            vectors[:, :size, 2 + 3 * k + c] = a["b1"][:, k * FF + first:k * FF + first + size]
    swap = lambda s: np.concatenate([s[:, HD // 2:], s[:, :HD // 2]], 1)
    return dict(
        Wqkv=a["Wqkv"], Wo=a["Wo"], W1=a["W1"], W2=w2.reshape(DEPTH, 3, P, D).transpose(0, 2, 1, 3),
        vectors=vectors, q_scale=a["q_scale"], q_swap=swap(a["q_scale"]), k_scale=a["k_scale"],
        k_swap=swap(a["k_scale"]), b2=a["b2"], rotary=rotary, decay=decay, mask=mask_constant(),
        ident=np.eye(P, dtype=np.float32))


def kernel(**inputs):
    import concourse.bacc as bacc
    from concourse.bass_utils import run_bass_kernel_spmd

    nc = bacc.Bacc("TRN2", target_bir_lowering=False, num_devices=1)
    arrays = {}

    def put(name, value):
        arrays[name] = np.ascontiguousarray(value)
        return nc.dram_tensor(name, arrays[name].shape, mybir.dt.from_np(arrays[name].dtype), kind="ExternalInput").ap()

    def stage_inputs(prefix, layout):
        mine = {n[len(prefix):]: np.asarray(v) for n, v in inputs.items() if n.startswith(prefix)}
        return {n: put(prefix + n, v) for n, v in layout(mine).items()}

    x = put("L0_attn_x", np.asarray(inputs["L0_attn_x"]))
    ident = put("identity", np.eye(P, dtype=np.float32))
    conv_w = stage_inputs("L0_attn_", conv_layout)
    experts_w = stage_inputs("L0_ffn_", experts_layout)
    linear_w = stage_inputs("L1_attn_", lambda a: a)
    windowed_w = stage_inputs("L1_ffn_", windowed_layout)
    out = nc.dram_tensor("out", (B, T, D), F32, kind="ExternalOutput").ap()
    sandwich_program(nc, x, out, ident, conv_w, experts_w, linear_w, windowed_w)
    result = run_bass_kernel_spmd(nc, [arrays], core_ids=[0])
    return result.results[0]["out"]
```

```python
from contextlib import ExitStack

import concourse.bass as bass
import numpy as np
from concourse import mybir

ALU = mybir.AluOpType
ACT = mybir.ActivationFunctionType
AX = mybir.AxisListType
F32 = mybir.dt.float32
F32R = mybir.dt.float32r
BF16 = mybir.dt.bfloat16
I32 = mybir.dt.int32

P = 128
D = 128
B = 2
T = 2048
J = T // P
N_TILES = B * J
G4 = 4
GROUPS = N_TILES // G4
LN_EPS = 1e-5
RSQRT_MAGIC = 0x5F3759DF
DMA = 16


class Memory:

    taken = []

    def __init__(self, nc, ctx, tag):
        self.nc, self.ctx, self.tag = nc, ctx, tag

    def sb(self, name, shape, dtype=F32):
        return self.ctx.enter_context(self.nc.sbuf_tensor(f"{self.tag}_{name}", list(shape), dtype))

    def bank(self, name, dtype=F32):
        return self.ctx.enter_context(self.nc.psum_tensor(f"{self.tag}_{name}_ps", [P, 512], dtype))

    def sem(self, name):
        semaphore = self.nc.alloc_semaphore(f"{self.tag}_{name}")
        self.taken.append(semaphore)
        return semaphore


def release_semaphores(nc):
    nc.clear_and_free_semaphores(Memory.taken)
    Memory.taken.clear()
    nc.all_engine_barrier()


def upto(index, per=1, k=0):
    return index * per + (k + 1)


RSQRT_STEPS = 11


def rsqrt_step(nc, vec, i, x, y, t, magic, steps, done, waits_met):
    if i:
        vec.wait_ge(steps, done + i)
    if i == 0:
        nc.vector.tensor_scalar(y.bitcast(I32), x.bitcast(I32), 1, -1, ALU.logical_shift_right,
                                ALU.bitwise_xor).then_inc(steps, 1)
    elif i == 1:
        vec.sem_inc(waits_met)
        nc.vector.tensor_tensor(t.bitcast(I32), y.bitcast(I32), magic, ALU.add).then_inc(steps, 1)
    else:
        a, b = (t, y) if (i - 2) // 3 % 2 == 0 else (y, t)
        if (i - 2) % 3 == 0:
            nc.vector.tensor_tensor(b, a, a, ALU.mult).then_inc(steps, 1)
        elif (i - 2) % 3 == 1:
            nc.vector.scalar_tensor_tensor(b, b, -0.5, x, ALU.mult, ALU.mult).then_inc(steps, 1)
        else:
            nc.vector.scalar_tensor_tensor(b, b, 1.5, a, ALU.add, ALU.mult).then_inc(steps, 1)


def rsqrt_steps(nc, vec, x, y, t, magic, steps, done, waits_met):
    for i in range(RSQRT_STEPS):
        rsqrt_step(nc, vec, i, x, y, t, magic, steps, done, waits_met)



def normalise_rows(nc, ctx, tag, x, xn, xT, ident, even_first=False, scale=None, bias=None):
    m = Memory(nc, ctx, tag)
    stats = m.sb("stats", [P, N_TILES, 6])
    mv = m.sb("mv", [P, N_TILES, 2])
    ve = m.sb("var_eps", [P, N_TILES])
    rstd = m.sb("rstd", [P, N_TILES])
    tmp = m.sb("tmp", [P, N_TILES])
    magic = m.sb("magic", [P, N_TILES], I32)
    banks = [m.bank(f"T{i}") for i in range(4)]
    magic_set, stat, steps, waits_met, rows_ready, T_ps, T_out = (
        m.sem(s) for s in ("magic_set", "stat", "steps", "waits_met", "rows_ready", "T_ps", "T_out"))

    with nc.Block() as block:
        @block.vector
        def _(v):
            nc.vector.memset(magic[:], RSQRT_MAGIC + 1).then_inc(magic_set, 1)
            for n in range(N_TILES):
                nc.vector.bn_stats(stats[:, n, :], x[:, n, :]).then_inc(stat, 1)
            v.wait_ge(stat, N_TILES)
            for n in range(N_TILES):
                nc.vector.bn_aggr(mv[:, n, :], stats[:, n, :]).then_inc(stat, 1)
            v.wait_ge(stat, 2 * N_TILES)
            nc.vector.tensor_scalar(ve[:], mv[:, :, 1], LN_EPS, None, ALU.add).then_inc(stat, 1)
            v.wait_ge(stat, 2 * N_TILES + 1)
            v.wait_ge(magic_set, 1)
            rsqrt_steps(nc, v, ve[:], rstd[:], tmp[:], magic[:], steps, 0, waits_met)
            v.wait_ge(steps, RSQRT_STEPS)
            for n in range(N_TILES):
                dst, src = xn[:, n, :], x[:, n, :]
                if even_first:
                    dst = dst.rearrange("p (two k) -> p k two", two=2)
                    src = src.rearrange("p (k two) -> p k two", two=2)
                nc.vector.tensor_scalar(dst, src, mv[:, n, 0:1], rstd[:, n:n + 1], ALU.subtract, ALU.mult
                                        ).then_inc(rows_ready, 1)

        @block.tensor
        def _(pe):
            for g in range(GROUPS):
                pe.wait_ge(rows_ready, G4 * (g + 1))
                if g >= 4:
                    pe.wait_ge(T_out, G4 * (g - 3))
                for t in range(G4):
                    last = nc.tensor.transpose(banks[g % 4][:, t * P:(t + 1) * P], xn[:, G4 * g + t, :], ident[:])
                last.then_inc(T_ps, 1)

        @block.scalar
        def _(act):
            for g in range(GROUPS):
                act.wait_ge(T_ps, g + 1)
                for t in range(G4):
                    src = banks[g % 4][:, t * P:(t + 1) * P]
                    if scale is None:
                        ins = nc.scalar.activation(xT(G4 * g + t), src, ACT.Copy)
                    else:
                        ins = nc.scalar.activation(xT(G4 * g + t), src, ACT.Identity, scale=scale, bias=bias)
                    ins.then_inc(T_out, 1)


def add_normalised(nc, ctx, tag, x, y):
    m = Memory(nc, ctx, tag)
    stats = m.sb("stats", [P, N_TILES, 6])
    mv = m.sb("mv", [P, N_TILES, 2])
    ve = m.sb("var_eps", [P, N_TILES])
    rstd = m.sb("rstd", [P, N_TILES])
    tmp = m.sb("tmp", [P, N_TILES])
    magic = m.sb("magic", [P, N_TILES], I32)
    magic_set, stat, steps, waits_met, scaled, summed = (
        m.sem(s) for s in ("magic_set", "stat", "steps", "waits_met", "scaled", "summed"))

    with nc.Block() as block:
        @block.vector
        def _(v):
            nc.vector.memset(magic[:], RSQRT_MAGIC + 1).then_inc(magic_set, 1)
            for n in range(N_TILES):
                nc.vector.bn_stats(stats[:, n, :], y[:, n, :]).then_inc(stat, 1)
            v.wait_ge(stat, N_TILES)
            for n in range(N_TILES):
                nc.vector.bn_aggr(mv[:, n, :], stats[:, n, :]).then_inc(stat, 1)
            v.wait_ge(stat, 2 * N_TILES)
            nc.vector.tensor_scalar(ve[:], mv[:, :, 1], LN_EPS, None, ALU.add).then_inc(stat, 1)
            v.wait_ge(stat, 2 * N_TILES + 1)
            v.wait_ge(magic_set, 1)
            rsqrt_steps(nc, v, ve[:], rstd[:], tmp[:], magic[:], steps, 0, waits_met)
            v.wait_ge(steps, RSQRT_STEPS)
            for n in range(N_TILES):
                nc.vector.tensor_scalar(y[:, n, :], y[:, n, :], mv[:, n, 0:1], rstd[:, n:n + 1], ALU.subtract, ALU.mult
                                        ).then_inc(scaled, 1)
            for g in range(GROUPS):
                if g % 2:
                    continue
                v.wait_ge(scaled, G4 * (g + 2))
                sl = slice(G4 * g, G4 * (g + 2))
                nc.vector.tensor_tensor(x[:, sl, :], x[:, sl, :], y[:, sl, :], ALU.add).then_inc(summed, 1)


AH = 16
AD = D // AH
VW = AD + 1
AE = 4
AF = 4 * D
AC = AF // P


def rope_constants():
    f = np.float32
    inv_freq = (f(1.0) / f(10000.0) ** (np.arange(0, AD, 2, dtype=f) / f(AD))).astype(f)
    theta = (np.arange(T, dtype=f)[:, None] * inv_freq[None, :]).astype(f)
    cos, sin = np.cos(theta), np.sin(theta)
    tabs = np.stack([np.stack([cos, cos], -1).reshape(T, AD), np.stack([-sin, sin], -1).reshape(T, AD)])
    return np.ascontiguousarray(tabs.reshape(2, J, P, AD).transpose(2, 0, 1, 3).astype(f))


def head_constants():
    p = np.arange(P)
    head4 = (((p[:, None] % 32) // AD) == np.arange(4)[None, :]).astype(np.float32)
    causal = (p[:, None] <= p[None, :]).astype(np.float32)
    blocks = np.repeat(((p[:, None] // AD) == np.arange(AH)[None, :]).astype(np.float32), VW, axis=1)
    return head4, causal, np.ascontiguousarray(blocks)


def conv_attention_mixture(nc, w, x, ident):
    with ExitStack() as ctx:
        m = Memory(nc, ctx, "a")
        x1 = m.sb("x1", [P, N_TILES, D])
        with ExitStack() as c1:
            m1 = Memory(nc, c1, "a1")
            xc = m1.sb("xT", [P, B, 2 + T])
            x1T = m1.sb("x1T", [P, B, 1 + T])
            wpw = m1.sb("w_pw", [P, D])
            wdw = m1.sb("w_dw", [P, 3])
            wqkv = m1.sb("w_qkv", [P, 3 * D])
            wg = m1.sb("w_gate", [P, D])
            wo = m1.sb("w_o", [P, D])
            bg = m1.sb("b_gate", [1, D])
            ones1 = m1.sb("ones1", [1, P])
            rope = m1.sb("rope", [P, 2, J, AD])
            head4 = m1.sb("head4", [P, 4])
            causal = m1.sb("causal", [P, P])
            blocks = m1.sb("blocks", [P, AH * VW])
            with ExitStack() as c2:
                normalise_rows(nc, c2, "an", x, x1,
                               lambda n: xc[:, n % B, 2 + (n // B) * P:2 + (n // B + 1) * P], ident)

            with ExitStack() as c2, nc.Block() as block:
                m2 = Memory(nc, c2, "av")
                cv = m2.sb("conv", [P, 2, B, 2 * P])
                db = [m2.bank("x1T0"), m2.bank("x1T1")]
                tb = [m2.bank("x1_0"), m2.bank("x1_1")]
                loaded, zeroed, conv, d_ps, t_ps, d_out, t_out, first = (
                    m2.sem(s) for s in ("loaded", "zeroed", "conv", "d_ps", "t_ps", "d_out", "t_out", "first"))

                @block.sync
                def _(sp):
                    for dst, name in ((wpw[:], "w_pw"), (wdw[:], "w_dw"), (wqkv[:], "w_qkv"), (wg[:], "w_gate"),
                                      (wo[:], "w_o"), (bg[:], "b_gate"), (rope[:], "rope"), (head4[:], "head4"),
                                      (causal[:], "causal"), (blocks[:], "blocks")):
                        sp.dma_start(dst, w[name]).then_inc(loaded, DMA)
                    sp.wait_ge(loaded, 10 * DMA)

                @block.vector
                def _(v):
                    nc.vector.memset(xc[:, :, 0:2], 0.0).then_inc(zeroed, 1)
                    nc.vector.memset(ones1[:], 1.0).then_inc(zeroed, 1)
                    v.wait_ge(loaded, 10 * DMA)
                    v.wait_ge(zeroed, 2)
                    with v.Fori(0, GROUPS // 2) as i:
                        for par in range(2):
                            g = i * 2 + par
                            v.wait_ge(t_ps, g + 1)
                            src = lambda k: xc[:, :, bass.ds(g * (2 * P) + k, 2 * P)]
                            nc.vector.tensor_scalar(cv[:, par], src(0), wdw[:, 0:1], None, ALU.mult).then_inc(conv, 1)
                            for k in (1, 2):
                                v.wait_ge(conv, g * 3 + k)
                                nc.vector.scalar_tensor_tensor(cv[:, par], src(k), wdw[:, k:k + 1], cv[:, par], ALU.mult, ALU.add
                                                               ).then_inc(conv, 1)
                            v.wait_ge(d_ps, g + 1)
                            nc.vector.tensor_tensor(x1T[:, :, bass.ds(g * (2 * P) + 1, 2 * P)],
                                                    db[par][:].rearrange("p (b t) -> p b t", b=B), src(2), ALU.add).then_inc(d_out, 1)
                            v.wait_ge(t_ps, g + 3)
                            rows = x1[:, bass.ds(g * G4, G4), :]
                            nc.vector.tensor_tensor(rows, tb[par][:].rearrange("p (t d) -> p t d", t=G4), rows, ALU.add).then_inc(t_out, 1)
                    v.wait_ge(d_out, GROUPS)
                    nc.vector.tensor_copy(x1T[:, :, 0:1], x1T[:, :, 1:2]).then_inc(first, 1)

                @block.tensor
                def _(pe):
                    nc.tensor.nop().then_inc(t_ps, 2)
                    with pe.Fori(0, GROUPS // 2) as i:
                        for par in range(2):
                            g = i * 2 + par
                            pe.wait_ge(conv, g * 3 + 3)
                            nc.tensor.matmul(db[par][:], wpw[:], cv[:, par].rearrange("p b t -> p (b t)"), start=True, stop=True
                                             ).then_inc(d_ps, 1)
                            for t in range(G4):
                                last = nc.tensor.matmul(tb[par][:, t * D:(t + 1) * D], cv[:, par, t % B, (t // B) * P:(t // B + 1) * P],
                                                        wpw[:], start=True, stop=True)
                            last.then_inc(t_ps, 1)

            with ExitStack() as c2, nc.Block() as block:
                m2 = Memory(nc, c2, "al")
                W = AH * VW
                xt = m2.sb("x_tile", [P, B, P])
                dt = m2.sb("delta_tile", [P, B, P])
                rc = m2.sb("cos_terms", [P, B, 2 * D])
                rs = m2.sb("sin_terms", [P, B, 2 * D])
                neg = m2.sb("negative", [P, B, 2 * D])
                phi = m2.sb("phi", [P, B, 2 * D])
                va = m2.sb("v_and_1", [P, B, W])
                qT = m2.sb("qT", [P, B, P])
                qx = m2.sb("q_heads", [P, B, 4, P])
                kx = m2.sb("k_groups", [P, B, 4, P])
                pr = m2.sb("products", [P, 4, 4, P])
                state = m2.sb("state", [P, B, W])
                upd = m2.sb("state_update", [P, W])
                den = m2.sb("den", [P, AH])
                rden = m2.sb("inv_den", [P, AH])
                at = m2.sb("attn", [P, D])
                aT = m2.sb("attnT", [P, P])
                th = m2.sb("gate_tanh", [P, B, D])
                gt = m2.sb("gated", [P, D])
                qk_b = m2.bank("qk")
                vg_b = m2.bank("v_gate")
                T_b = m2.bank("T")
                s_b = [m2.bank("s0"), m2.bank("s1")]
                num_b = m2.bank("num")
                upd_b = m2.bank("upd")
                o_b = m2.bank("o")
                names = ("zeroed tile_ready delta_ready qkv_ps gate_ps tanh_done cos_done sin_done roped floored exped "
                         "phi_ready v_ready qkT_ps qT_ready qx_ready kx_ready s_ps masked num_ps upd_ps upd_masked "
                         "state_ready den_ready rden_ready at_ready aT_ps aT_ready o_ps gated x2_ready waits_met")
                (zeroed, tile_ready, delta_ready, qkv_ps, gate_ps, tanh_done, cos_done, sin_done, roped, floored, exped,
                 phi_ready, v_ready, qkT_ps, qT_ready, qx_ready, kx_ready, s_ps, masked, num_ps, upd_ps, upd_masked,
                 state_ready, den_ready, rden_ready, at_ready, aT_ps, aT_ready, o_ps, gated, x2_ready, waits_met) = (
                    m2.sem(s) for s in names.split())

                @block.gpsimd
                def _(pool):
                    nc.gpsimd.memset(kx[:], 0.0).then_inc(zeroed, 1)
                    nc.gpsimd.memset(va[:], 1.0).then_inc(zeroed, 1)
                    nc.gpsimd.memset(state[:], 0.0).then_inc(zeroed, 1)
                    with pool.Fori(0, J) as j:
                        for b in range(B):
                            u = j * 2 + b
                            pool.wait_ge(qkv_ps, u + 1)
                            pool.wait_ge(gate_ps, u + 1)
                            now, before = x1T[:, b, bass.ds(j * P + 1, P)], x1T[:, b, bass.ds(j * P, P)]
                            nc.gpsimd.tensor_copy(xt[:, b, :], now).then_inc(tile_ready, 1)
                            nc.gpsimd.tensor_tensor(dt[:, b, :], now, before, ALU.subtract).then_inc(delta_ready, 1)

                @block.tensor
                def _(pe):
                    nc.tensor.nop().then_inc(qkv_ps, 2)
                    nc.tensor.nop().then_inc(gate_ps, 2)
                    pe.wait_ge(zeroed, 3)

                    def project(u, b):
                        pe.wait_ge(tile_ready, u + 1)
                        pe.wait_ge(sin_done, u * 2 + 2)
                        nc.tensor.matmul(qk_b[:, 0:2 * D], xt[:, b, :], wqkv[:, 0:2 * D], start=True, stop=True
                                         ).then_inc(qkv_ps, 1)
                        pe.wait_ge(v_ready, u + 1)
                        pe.wait_ge(tanh_done, u + 1)
                        nc.tensor.matmul(vg_b[:, D:2 * D], xt[:, b, :], wqkv[:, 2 * D:3 * D], start=True, stop=True)
                        pe.wait_ge(delta_ready, u + 1)
                        nc.tensor.matmul(vg_b[:, 0:D], dt[:, b, :], wg[:], start=True, stop=False)
                        nc.tensor.matmul(vg_b[:, 0:D], ones1[:], bg[:], start=False, stop=True).then_inc(gate_ps, 1)

                    project(0, 0)
                    def tile(j, b, more=True):
                        u = j * 2 + b
                        pe.wait_ge(phi_ready, u + 1)
                        for k in range(2):
                            last = nc.tensor.transpose(T_b[:, k * P:(k + 1) * P], phi[:, b, k * D:(k + 1) * D], ident[:])
                        last.then_inc(qkT_ps, 1)
                        if more:
                            project(u + 1, 1 - b)
                        pe.wait_ge(qx_ready, u + 1)
                        pe.wait_ge(kx_ready, u * 4 + 4)
                        for g in range(4):
                            pe.wait_ge(masked, u * 4 + (g + 1))
                            nc.tensor.matmul(s_b[g % 2][:], kx[:, b, g, :], qx[:, b].rearrange("p h t -> p (h t)"),
                                             start=True, stop=True).then_inc(s_ps, 1)
                        pe.wait_ge(qT_ready, u + 1)
                        pe.wait_ge(at_ready, u + 1)
                        pe.wait_ge(state_ready, u + 1)
                        nc.tensor.matmul(num_b[:, 0:W], qT[:, b, :], state[:, b, :], start=True, stop=True)
                        pe.wait_ge(v_ready, u + 2)
                        pe.wait_ge(upd_masked, u + 1)
                        nc.tensor.matmul(upd_b[:, 0:W], phi[:, b, D:2 * D], va[:, b, :], start=True, stop=True
                                         ).then_inc(upd_ps, 1)
                        for g in range(4):
                            pe.wait_ge(masked, u * 4 + (g + 3))
                            for h in range(4 * g, 4 * g + 4):
                                last = nc.tensor.matmul(num_b[:, h * VW:(h + 1) * VW], pr[:, g, h % 4, :],
                                                        va[:, b, h * VW:(h + 1) * VW], start=False, stop=True,
                                                        skip_group_check=True)
                        last.then_inc(num_ps, 1)
                        pe.wait_ge(at_ready, u + 2)
                        nc.tensor.transpose(T_b[:, 0:P], at[:], ident[:]).then_inc(aT_ps, 1)
                        pe.wait_ge(aT_ready, u + 1)
                        pe.wait_ge(gated, u + 2)
                        nc.tensor.matmul(o_b[:, 0:D], aT[:], wo[:], start=True, stop=True).then_inc(o_ps, 1)

                    with pe.Fori(0, J - 1) as j:
                        for b in range(B):
                            tile(j, b)
                    tile(J - 1, 0)
                    tile(J - 1, 1, more=False)

                @block.scalar
                def _(act):
                    nc.scalar.nop().then_inc(v_ready, 1)
                    nc.scalar.nop().then_inc(tanh_done, 1)
                    act.wait_ge(zeroed, 3)

                    def from_projection(u, b):
                        act.wait_ge(gate_ps, u + 3)
                        nc.scalar.activation(va[:, b, :].rearrange("p (h c) -> p h c", c=VW)[:, :, 0:AD],
                                             vg_b[:, D:2 * D].rearrange("p (h c) -> p h c", c=AD), ACT.Copy).then_inc(v_ready, 1)
                        act.wait_ge(gated, u + 1)
                        nc.scalar.activation(th[:, b, :], vg_b[:, 0:D], ACT.Tanh, scale=0.5).then_inc(tanh_done, 1)
                        act.wait_ge(floored, u + 1)
                        nc.scalar.activation(neg[:, b, :], neg[:, b, :], ACT.Exp).then_inc(exped, 1)

                    from_projection(0, 0)
                    def tile(j, b, more=True):
                        u = j * 2 + b
                        act.wait_ge(qkT_ps, u + 1)
                        nc.scalar.activation(qT[:, b, :], T_b[:, 0:P], ACT.Copy).then_inc(qT_ready, 1)
                        for g in range(4):
                            nc.scalar.activation(kx[32 * g:32 * g + 32, b, g, :], T_b[32 * g:32 * g + 32, P:2 * P], ACT.Copy
                                                 ).then_inc(kx_ready, 1)
                        if more:
                            from_projection(u + 1, 1 - b)
                        act.wait_ge(aT_ps, u + 1)
                        nc.scalar.activation(aT[:], T_b[:, 0:P], ACT.Copy).then_inc(aT_ready, 1)

                    with act.Fori(0, J - 1) as j:
                        for b in range(B):
                            tile(j, b)
                    tile(J - 1, 0)
                    tile(J - 1, 1, more=False)

                @block.vector
                def _(v):
                    nc.vector.nop().then_inc(sin_done, 2)
                    nc.vector.nop().then_inc(masked, 2)
                    nc.vector.nop().then_inc(at_ready, 1)
                    nc.vector.nop().then_inc(gated, 2)
                    nc.vector.nop().then_inc(upd_masked, 1)
                    nc.vector.nop().then_inc(state_ready, 2)
                    v.wait_ge(zeroed, 3)

                    def phis(u, j, b):
                        v.wait_ge(qkv_ps, u + 3)
                        src = qk_b[:, 0:2 * D].rearrange("p (h d) -> p h d", d=AD)
                        shape = [P, 2 * AH, AD]
                        nc.vector.tensor_tensor(rc[:, b, :].rearrange("p (h d) -> p h d", d=AD), src,
                                                rope[:, 0, bass.ds(j, 1), :].broadcast_to(shape), ALU.mult).then_inc(cos_done, 1)
                        src4 = qk_b[:, 0:2 * D].rearrange("p (h d two) -> p h d two", d=AD // 2, two=2)
                        dst4 = rs[:, b, :].rearrange("p (h d two) -> p h d two", d=AD // 2, two=2)
                        for s in range(2):
                            tab = rope[:, 1, bass.ds(j, 1), :].rearrange("p j (d two) -> p j d two", two=2)[:, :, :, s]
                            nc.vector.tensor_tensor(dst4[:, :, :, s], src4[:, :, :, 1 - s], tab.broadcast_to([P, 2 * AH, AD // 2]),
                                                    ALU.mult).then_inc(sin_done, 1)
                        v.wait_ge(sin_done, u * 2 + 4)
                        nc.vector.tensor_tensor(rc[:, b, :], rc[:, b, :], rs[:, b, :], ALU.add).then_inc(roped, 1)
                        v.wait_ge(roped, u + 1)
                        nc.vector.tensor_scalar(neg[:, b, :], rc[:, b, :], 0.0, None, ALU.min).then_inc(floored, 1)

                    def phis_end(u, b):
                        v.wait_ge(exped, u + 1)
                        nc.vector.scalar_tensor_tensor(phi[:, b, :], rc[:, b, :], 0.0, neg[:, b, :], ALU.max, ALU.add
                                                       ).then_inc(phi_ready, 1)

                    phis(0, 0, 0)
                    phis_end(0, 0)
                    def tile(j, b, more=True):
                        u = j * 2 + b
                        v.wait_ge(qkT_ps, u + 1)
                        v.wait_ge(kx_ready, u * 4 + 4)
                        nc.vector.tensor_tensor(qx[:, b], T_b[:, 0:P].unsqueeze(1).broadcast_to([P, 4, P]),
                                                head4[:].unsqueeze(2).broadcast_to([P, 4, P]), ALU.mult).then_inc(qx_ready, 1)
                        if more:
                            phis(u + 1, j + b, 1 - b)
                        for g in range(4):
                            v.wait_ge(s_ps, u * 4 + (g + 1))
                            nc.vector.tensor_tensor(pr[:, g], s_b[g % 2][:].rearrange("p (h t) -> p h t", h=4),
                                                    causal[:].unsqueeze(1).broadcast_to([P, 4, P]), ALU.mult).then_inc(masked, 1)
                        v.wait_ge(upd_ps, u + 1)
                        nc.vector.tensor_tensor(upd[:], upd_b[:, 0:W], blocks[:], ALU.mult).then_inc(upd_masked, 1)
                        v.wait_ge(upd_masked, u + 2)
                        nc.vector.tensor_tensor(state[:, b, :], state[:, b, :], upd[:], ALU.add).then_inc(state_ready, 1)
                        v.wait_ge(num_ps, u + 1)
                        n3 = num_b[:, 0:W].rearrange("p (h c) -> p h c", c=VW)
                        nc.vector.tensor_scalar(den[:], n3[:, :, AD], 1e-6, None, ALU.add).then_inc(den_ready, 1)
                        v.wait_ge(den_ready, u + 1)
                        nc.vector.reciprocal(rden[:], den[:]).then_inc(rden_ready, 1)
                        v.wait_ge(rden_ready, u + 1)
                        nc.vector.tensor_tensor(at[:].rearrange("p (h c) -> p h c", c=AD), n3[:, :, 0:AD],
                                                rden[:].unsqueeze(2).broadcast_to([P, AH, AD]), ALU.mult).then_inc(at_ready, 1)
                        if more:
                            phis_end(u + 1, 1 - b)
                        v.wait_ge(o_ps, u + 1)
                        v.wait_ge(tanh_done, u + 2)
                        nc.vector.scalar_tensor_tensor(gt[:], th[:, b, :], 1.0, o_b[:, 0:D], ALU.add, ALU.mult).then_inc(gated, 1)
                        row = x1[:, bass.ds(u, 1), :].rearrange("p n d -> p (n d)")
                        v.wait_ge(gated, u + 3)
                        v.sem_inc(waits_met)
                        nc.vector.scalar_tensor_tensor(row, gt[:], 0.5, row, ALU.mult, ALU.add).then_inc(x2_ready, 1)

                    with v.Fori(0, J - 1) as j:
                        for b in range(B):
                            tile(j, b)
                    tile(J - 1, 0)
                    tile(J - 1, 1, more=False)

        with ExitStack() as c1:
            m1 = Memory(nc, c1, "am")
            hh = m1.sb("hT_hi", [P, N_TILES * P], F32R)
            hl = m1.sb("hT_lo", [P, N_TILES * P], F32R)
            w1h = m1.sb("w1_hi", [P, AE * AF], F32R)
            w1l = m1.sb("w1_lo", [P, AE * AF], F32R)
            w2 = m1.sb("w2", [P, AE * AC, D])
            b1 = m1.sb("b1", [P, AE * AC])
            gw = m1.sb("mix", [P, N_TILES, AE])
            with ExitStack() as c3:
                m3 = Memory(nc, c3, "ah")
                h = m3.sb("h", [P, N_TILES, D])
                hT = m3.sb("hT", [P, N_TILES, P])
                gb = m3.sb("ln_g_b", [P, 2])
                w1 = m3.sb("w1", [P, AE * AF])
                wm = m3.sb("w_moe_gate", [P, AE])
                b2 = m3.sb("b2", [AE, D])
                with nc.Block() as block:
                    loaded = m3.sem("loaded")

                    @block.sync
                    def _(sp):
                        for dst, name in ((gb[:], "ln_g_b"), (w1[:], "w1"), (wm[:], "w_moe_gate"), (b2[:], "b2"),
                                          (w2[:], "w2"), (b1[:], "b1")):
                            sp.dma_start(dst, w[name]).then_inc(loaded, DMA)
                        sp.wait_ge(loaded, 6 * DMA)

                with ExitStack() as c2:
                    normalise_rows(nc, c2, "ao", x1, h, lambda n: hT[:, n, :], ident, scale=gb[:, 0:1], bias=gb[:, 1:2])

                with ExitStack() as c2, nc.Block() as block:
                    m2 = Memory(nc, c2, "as")
                    lg = m2.sb("logits", [P, N_TILES, AE])
                    mx = m2.sb("max", [P, N_TILES])
                    sm = m2.sb("sum", [P, N_TILES])
                    rm = m2.sb("inv_sum", [P, N_TILES])
                    gT = m2.sb("mixT", [AE, N_TILES, P])
                    lb = m2.bank("logits")
                    cb = [m2.bank("gT0"), m2.bank("gT1")]
                    yb = [m2.bank("y0"), m2.bank("y1")]
                    w_hi, w_lo, hi_done, lo_done, lg_ps, shifted, expd, step, mixed, gT_ps, gT_out, y_ps, y_out = (
                        m2.sem(s) for s in ("w_hi", "w_lo", "hi_done", "lo_done", "lg_ps", "shifted", "expd", "step", "mixed",
                                            "gT_ps", "gT_out", "y_ps", "y_out"))
                    shape = [P, N_TILES, AE]
                    hTf = hT[:].rearrange("p n t -> p (n t)")

                    @block.tensor
                    def _(pe):
                        for n in range(N_TILES):
                            last = nc.tensor.matmul(lb[:, n * AE:(n + 1) * AE], hT[:, n, :], wm[:], start=True, stop=True)
                        last.then_inc(lg_ps, 1)
                        pe.wait_ge(mixed, 1)
                        for g in range(GROUPS):
                            if g >= 2:
                                pe.wait_ge(gT_out, g - 1)
                                pe.wait_ge(y_out, g - 1)
                            for t in range(G4):
                                last = nc.tensor.transpose(cb[g % 2][0:AE, t * P:(t + 1) * P], gw[:, G4 * g + t, :], ident[:])
                            last.then_inc(gT_ps, 1)
                            pe.wait_ge(gT_out, g + 1)
                            for t in range(G4):
                                last = nc.tensor.matmul(yb[g % 2][:, t * D:(t + 1) * D], gT[:, G4 * g + t, :], b2[:], start=True, stop=True)
                            last.then_inc(y_ps, 1)

                    @block.scalar
                    def _(act):
                        for q in range(4):
                            sl = slice(q * 1024, (q + 1) * 1024)
                            nc.scalar.activation(hh[:, sl], hTf[:, sl], ACT.Copy).then_inc(hi_done, 1)
                        for q in range(2):
                            sl = slice(q * 1024, (q + 1) * 1024)
                            nc.scalar.activation(w1h[:, sl], w1[:, sl], ACT.Copy).then_inc(w_hi, 1)
                        act.wait_ge(shifted, 1)
                        nc.scalar.activation(gw[:], lg[:], ACT.Exp).then_inc(expd, 1)
                        for g in range(GROUPS):
                            act.wait_ge(gT_ps, g + 1)
                            nc.scalar.activation(gT[:, G4 * g:G4 * g + G4, :], cb[g % 2][0:AE, :].rearrange("p (t k) -> p t k", t=G4),
                                                 ACT.Copy).then_inc(gT_out, 1)

                    @block.vector
                    def _(v):
                        lb3 = lb[:, 0:N_TILES * AE].rearrange("p (n e) -> p n e", e=AE)
                        v.wait_ge(lg_ps, 1)
                        nc.vector.tensor_reduce(mx[:], lb3, AX.X, ALU.max).then_inc(step, 1)
                        v.wait_ge(step, 1)
                        nc.vector.tensor_tensor(lg[:], lb3, mx[:].unsqueeze(2).broadcast_to(shape), ALU.subtract).then_inc(shifted, 1)
                        for q in range(4):
                            sl = slice(q * 1024, (q + 1) * 1024)
                            v.wait_ge(hi_done, q + 1)
                            nc.vector.tensor_tensor(hl[:, sl], hTf[:, sl], hh[:, sl].bitcast(F32), ALU.subtract).then_inc(lo_done, 1)
                        for q in range(2):
                            sl = slice(q * 1024, (q + 1) * 1024)
                            v.wait_ge(w_hi, q + 1)
                            nc.vector.tensor_tensor(w1l[:, sl], w1[:, sl], w1h[:, sl].bitcast(F32), ALU.subtract).then_inc(w_lo, 1)
                        v.wait_ge(expd, 1)
                        nc.vector.tensor_reduce(sm[:], gw[:], AX.X, ALU.add).then_inc(step, 1)
                        v.wait_ge(step, 2)
                        nc.vector.reciprocal(rm[:], sm[:]).then_inc(step, 1)
                        v.wait_ge(step, 3)
                        nc.vector.tensor_tensor(gw[:], gw[:], rm[:].unsqueeze(2).broadcast_to(shape), ALU.mult).then_inc(mixed, 1)
                        for g in range(GROUPS):
                            v.wait_ge(y_ps, g + 1)
                            rows = x1[:, G4 * g:G4 * g + G4, :]
                            nc.vector.tensor_tensor(rows, yb[g % 2][:].rearrange("p (t d) -> p t d", t=G4), rows, ALU.add).then_inc(y_out, 1)

            with ExitStack() as c2, nc.Block() as block:
                m2 = Memory(nc, c2, "ax")
                hid = m2.sb("hidden", [P, 2, AC, 512])
                up = [m2.bank(f"up{i}") for i in range(4)]
                dn = [m2.bank("down0"), m2.bank("down1")]
                up_ps, hid_ready, dn_ps, added = (m2.sem(s) for s in ("up_ps", "hid_ready", "dn_ps", "added"))

                @block.tensor
                def _(pe):
                    def first(g, e):
                        for c in range(AC):
                            k = e * AC + c
                            q = g * (AE * AC) + k
                            pe.wait_ge(hid_ready, q + 1)
                            cols = bass.ds(g * 512, 512)
                            sl = slice(k * P, (k + 1) * P)
                            nc.tensor.matmul(up[c][:], w1h[:, sl], hh[:, cols], start=True, stop=False)
                            nc.tensor.matmul(up[c][:], w1l[:, sl], hh[:, cols], start=False, stop=False)
                            nc.tensor.matmul(up[c][:], w1h[:, sl], hl[:, cols], start=False, stop=True).then_inc(up_ps, 1)

                    def second(g, e):
                        q = g * AE + e
                        pe.wait_ge(hid_ready, q * AC + 8)
                        pe.wait_ge(added, q + 1)
                        for t in range(G4):
                            for c in range(AC):
                                last = nc.tensor.matmul(dn[e % 2][:, t * D:(t + 1) * D], hid[:, e % 2, c, t * P:(t + 1) * P],
                                                        w2[:, e * AC + c, :], start=(c == 0), stop=(c == AC - 1))
                        last.then_inc(dn_ps, 1)

                    with pe.Fori(0, GROUPS) as g:
                        for e in range(AE):
                            first(g, e)
                            if e:
                                second(g, e - 1)
                        second(g, AE - 1)

                @block.scalar
                def _(act):
                    nc.scalar.nop().then_inc(hid_ready, 4)
                    with act.Fori(0, GROUPS) as g:
                        for e in range(AE):
                            act.wait_ge(dn_ps, g * AE + (e + 1))
                            for c in range(AC):
                                act.wait_ge(up_ps, g * (AE * AC) + (e * AC + c + 1))
                                nc.scalar.activation(hid[:, e % 2, c, :], up[c][:], ACT.Silu,
                                                     bias=b1[:, e * AC + c:e * AC + c + 1]).then_inc(hid_ready, 1)

                @block.vector
                def _(v):
                    nc.vector.nop().then_inc(dn_ps, 2)
                    nc.vector.nop().then_inc(added, 2)
                    with v.Fori(0, GROUPS) as g:
                        for e in range(AE):
                            v.wait_ge(dn_ps, g * AE + (e + 3))
                            v.wait_ge(added, g * AE + (e + 2))
                            for t in range(G4):
                                row = x1[:, bass.ds(g * G4 + t, 1), :].rearrange("p n d -> p (n d)")
                                wt = gw[:, bass.ds(g * G4 + t, 1), e]
                                ins = nc.vector.scalar_tensor_tensor(row, dn[e % 2][:, t * D:(t + 1) * D], wt, row, ALU.mult, ALU.add)
                            ins.then_inc(added, 1)
        with ExitStack() as c2:
            add_normalised(nc, c2, "aa", x, x1)


EXPERTS = 16
FE = 256
GU = 2 * FE
CH = 1024


def fp4_experts(nc, w, x, ident):
    with ExitStack() as ctx:
        m = Memory(nc, ctx, "b")
        y = m.sb("y", [P, N_TILES, D])
        comb = m.sb("combine", [P, N_TILES, EXPERTS])
        xh = m.sb("xT_hi", [P, N_TILES * P], F32R)
        xl = m.sb("xT_lo", [P, N_TILES * P], F32R)
        wgu = m.sb("w_gu", [P, EXPERTS, GU])
        wdn = m.sb("w_down", [P, 2, EXPERTS, D])
        bgu = m.sb("bias_gu", [P, EXPERTS, 4])

        with ExitStack() as c2, nc.Block() as block:
            m2 = Memory(nc, c2, "bw")
            blk = m2.sb("blocks", [P, 2, CH], I32)
            scl = m2.sb("scales", [P, 2, CH], I32)
            nib = m2.sb("nibble", [P, CH], I32)
            cod = m2.sb("code", [P, CH], I32)
            sgn = m2.sb("sign", [P, CH], I32)
            sc = m2.sb("signed_scale", [P, CH], I32)
            mag = m2.sb("magnitude", [P, CH])
            in_dma = [m2.sem("in_dma0"), m2.sem("in_dma1")]
            step, decoded, b_dma = m2.sem("step"), m2.sem("decoded"), m2.sem("b_dma")
            n_gu = EXPERTS * GU // CH
            n_dn = EXPERTS * D // CH
            LOADS_GU, LOADS_DN = 2 + 8, 1 + 8

            @block.sync
            def _(sp):
                sp.dma_start(bgu[:], w["bias_gu"]).then_inc(b_dma, DMA)
                for i in range(n_gu + n_dn):
                    if i >= 2:
                        sp.wait_ge(decoded, i - 1)
                    if i < n_gu:
                        sl = slice(i * CH, (i + 1) * CH)
                        for half in range(2):
                            sp.dma_start(blk[64 * half:64 * half + 64, i % 2, :], w["blocks_gu"][:, sl]).then_inc(in_dma[i % 2], DMA)
                            for k in range(4):
                                p0 = 64 * half + 16 * k
                                sp.dma_start(scl[p0:p0 + 16, i % 2, :], w["scales_gu"][k:k + 1, sl].broadcast_to([16, CH])
                                             ).then_inc(in_dma[i % 2], DMA)
                    else:
                        sl = slice((i - n_gu) * CH, (i - n_gu + 1) * CH)
                        sp.dma_start(blk[:, i % 2, :], w["blocks_down"][:, sl]).then_inc(in_dma[i % 2], DMA)
                        for k in range(8):
                            sp.dma_start(scl[16 * k:16 * k + 16, i % 2, :], w["scales_down"][k:k + 1, sl].broadcast_to([16, CH])
                                         ).then_inc(in_dma[i % 2], DMA)

            @block.vector
            def _(v):
                done = 0
                loads = [0, 0]

                def decode(i, nibbles, dst, last):
                    nonlocal done
                    for lo, hi, shift in nibbles:
                        nc.vector.tensor_scalar(nib[lo:hi, :], blk[lo:hi, i % 2, :], shift, 15,
                                                ALU.logical_shift_right, ALU.bitwise_and).then_inc(step, 1)
                    done += len(nibbles)
                    v.wait_ge(step, done)
                    nc.vector.tensor_scalar(cod[:], nib[:], 7, None, ALU.bitwise_and).then_inc(step, 1)
                    nc.vector.tensor_scalar(sgn[:], nib[:], 3, 31, ALU.logical_shift_right, ALU.logical_shift_left).then_inc(step, 1)
                    nc.vector.tensor_scalar(sc[:], scl[:, i % 2, :], 23, None, ALU.logical_shift_left).then_inc(step, 1)
                    v.wait_ge(step, done + 3)
                    nc.vector.tensor_tensor(sc[:], sc[:], sgn[:], ALU.bitwise_or).then_inc(step, 1)
                    nc.vector.tensor_scalar(mag[:], cod[:], 2.0, -8.0, ALU.mult, ALU.add).then_inc(step, 1)
                    v.wait_ge(step, done + 5)
                    nc.vector.scalar_tensor_tensor(mag[:], cod[:], -2.0, mag[:], ALU.add, ALU.max).then_inc(step, 1)
                    v.wait_ge(step, done + 6)
                    nc.vector.scalar_tensor_tensor(mag[:], cod[:], 0.5, mag[:], ALU.mult, ALU.max).then_inc(step, 1)
                    v.wait_ge(step, done + 7)
                    ins = nc.vector.tensor_tensor(dst, mag[:], sc[:].bitcast(F32), ALU.mult).then_inc(step, 1)
                    done += 8
                    v.wait_ge(step, done)
                    if last:
                        nc.vector.nop().then_inc(decoded, 1)

                for i in range(n_gu + n_dn):
                    loads[i % 2] += LOADS_GU if i < n_gu else LOADS_DN
                    v.wait_ge(in_dma[i % 2], loads[i % 2] * DMA)
                    if i < n_gu:
                        dst = wgu[:].rearrange("p e o -> p (e o)")[:, i * CH:(i + 1) * CH]
                        decode(i, [(0, 64, 0), (64, 128, 4)], dst, True)
                    else:
                        k = i - n_gu
                        for c in range(2):
                            dst = wdn[:, c, :, :].rearrange("p e d -> p (e d)")[:, k * CH:(k + 1) * CH]
                            decode(i, [(0, 128, 4 * c)], dst, c == 1)
                v.wait_ge(b_dma, DMA)

        with ExitStack() as c1:
            m1 = Memory(nc, c1, "br")
            xn = m1.sb("xn", [P, N_TILES, D])
            xT = m1.sb("xT", [P, N_TILES, P])
            with ExitStack() as c2:
                normalise_rows(nc, c2, "bn", x, xn, lambda n: xT[:, n, :], ident, even_first=True)
            with ExitStack() as c2, nc.Block() as block:
                m2 = Memory(nc, c2, "bt")
                rw = m2.sb("router", [P, EXPERTS])
                bd = m2.sb("bias_down", [EXPERTS, D])
                lg = m2.sb("logits", [P, N_TILES, EXPERTS])
                top = m2.sb("top", [P, N_TILES, 8])
                idx = m2.sb("index", [P, N_TILES, 8], mybir.dt.uint32)
                idf = m2.sb("index_f", [P, N_TILES, 2])
                gap = m2.sb("gap", [P, N_TILES])
                e2 = m2.sb("exp_gap", [P, N_TILES])
                den = m2.sb("den", [P, N_TILES])
                wt = m2.sb("weights", [P, 2, N_TILES])
                iota = m2.sb("iota", [P, EXPERTS])
                hot = m2.sb("one_hot", [P, N_TILES, EXPERTS])
                cT = m2.sb("combineT", [EXPERTS, N_TILES, P])
                lb = m2.bank("logits")
                cb = [m2.bank("cT0"), m2.bank("cT1")]
                yb = [m2.bank("y0"), m2.bank("y1")]
                loaded, lg_ps, lg_out, topped, gapped, expd, step, combined, hi_done, lo_done, cT_ps, cT_out, y_ps, y_out = (
                    m2.sem(s) for s in ("loaded", "lg_ps", "lg_out", "topped", "gapped", "expd", "step", "combined",
                                        "hi_done", "lo_done", "cT_ps", "cT_out", "y_ps", "y_out"))

                @block.sync
                def _(sp):
                    sp.dma_start(rw[:], w["router"]).then_inc(loaded, DMA)
                    sp.dma_start(bd[:], w["bias_down"]).then_inc(loaded, DMA)
                    sp.dma_start(iota[:], w["iota"]).then_inc(loaded, DMA)

                @block.tensor
                def _(pe):
                    pe.wait_ge(loaded, 3 * DMA)
                    for n in range(N_TILES):
                        last = nc.tensor.matmul(lb[:, n * EXPERTS:(n + 1) * EXPERTS], xT[:, n, :], rw[:], start=True, stop=True)
                    last.then_inc(lg_ps, 1)
                    pe.wait_ge(combined, 1)
                    for g in range(GROUPS):
                        if g >= 2:
                            pe.wait_ge(cT_out, g - 1)
                        for t in range(G4):
                            last = nc.tensor.transpose(cb[g % 2][0:EXPERTS, t * P:(t + 1) * P], comb[:, G4 * g + t, :], ident[:])
                        last.then_inc(cT_ps, 1)
                        pe.wait_ge(cT_out, g + 1)
                        if g >= 2:
                            pe.wait_ge(y_out, g - 1)
                        for t in range(G4):
                            last = nc.tensor.matmul(yb[g % 2][:, t * D:(t + 1) * D], cT[:, G4 * g + t, :], bd[:], start=True, stop=True)
                        last.then_inc(y_ps, 1)

                @block.scalar
                def _(act):
                    act.wait_ge(lg_ps, 1)
                    nc.scalar.activation(lg[:].rearrange("p n e -> p (n e)"), lb[:], ACT.Copy).then_inc(lg_out, 1)
                    for q in range(4):
                        sl = slice(q * 1024, (q + 1) * 1024)
                        nc.scalar.activation(xh[:, sl], xT[:].rearrange("p n t -> p (n t)")[:, sl], ACT.Copy).then_inc(hi_done, 1)
                    act.wait_ge(gapped, 1)
                    nc.scalar.activation(e2[:], gap[:], ACT.Exp).then_inc(expd, 1)
                    for g in range(GROUPS):
                        act.wait_ge(cT_ps, g + 1)
                        nc.scalar.activation(cT[:, G4 * g:G4 * g + G4, :], cb[g % 2][0:EXPERTS, :].rearrange("p (t k) -> p t k", t=G4),
                                             ACT.Copy).then_inc(cT_out, 1)
                        act.wait_ge(y_ps, g + 1)
                        nc.scalar.activation(y[:, G4 * g:G4 * g + G4, :], yb[g % 2][:].rearrange("p (t d) -> p t d", t=G4),
                                             ACT.Copy).then_inc(y_out, 1)

                @block.vector
                def _(v):
                    v.wait_ge(lg_out, 1)
                    for n in range(N_TILES):
                        nc.vector.max(top[:, n, :], lg[:, n, :]).then_inc(topped, 1)
                    v.wait_ge(topped, N_TILES)
                    nc.vector.tensor_tensor(gap[:], top[:, :, 1], top[:, :, 0], ALU.subtract).then_inc(gapped, 1)
                    for n in range(N_TILES):
                        nc.vector.max_index(idx[:, n, :], top[:, n, :], lg[:, n, :]).then_inc(topped, 1)
                    v.wait_ge(expd, 1)
                    nc.vector.tensor_scalar(den[:], e2[:], 1.0, None, ALU.add).then_inc(step, 1)
                    v.wait_ge(step, 1)
                    nc.vector.reciprocal(wt[:, 0, :], den[:]).then_inc(step, 1)
                    v.wait_ge(step, 2)
                    nc.vector.tensor_tensor(wt[:, 1, :], wt[:, 0, :], e2[:], ALU.mult).then_inc(step, 1)
                    v.wait_ge(topped, 2 * N_TILES)
                    nc.vector.tensor_copy(idf[:], idx[:, :, 0:2]).then_inc(step, 1)
                    v.wait_ge(loaded, 3 * DMA)
                    v.wait_ge(step, 4)
                    shape = [P, N_TILES, EXPERTS]
                    for k, dst in ((0, comb), (1, hot)):
                        nc.vector.tensor_tensor(dst[:], iota[:].unsqueeze(1).broadcast_to(shape),
                                                idf[:, :, k:k + 1].broadcast_to(shape), ALU.is_equal).then_inc(step, 1)
                        v.wait_ge(step, 5 + 2 * k)
                        nc.vector.tensor_tensor(dst[:], dst[:], wt[:, k, :].unsqueeze(2).broadcast_to(shape), ALU.mult).then_inc(step, 1)
                    v.wait_ge(step, 8)
                    nc.vector.tensor_tensor(comb[:], comb[:], hot[:], ALU.add).then_inc(combined, 1)
                    for q in range(4):
                        sl = slice(q * 1024, (q + 1) * 1024)
                        v.wait_ge(hi_done, q + 1)
                        nc.vector.tensor_tensor(xl[:, sl], xT[:].rearrange("p n t -> p (n t)")[:, sl], xh[:, sl].bitcast(F32),
                                                ALU.subtract).then_inc(lo_done, 1)

        with ExitStack() as c2, nc.Block() as block:
            m2 = Memory(nc, c2, "be")
            slot = [m2.sb(f"w_slot{i}", [P, 4, P], F32R) for i in range(2)]
            bias_slot = [m2.sb(f"bias_slot{i}", [P, 4]) for i in range(2)]
            sil = m2.sb("silu", [P, 2, 512])
            h = m2.sb("h", [P, 2, 2, 512])
            gate = [m2.bank("gate0"), m2.bank("gate1")]
            up = [m2.bank("up0"), m2.bank("up1")]
            dn = [m2.bank("down0"), m2.bank("down1")]
            slot_ready, gate_ps, up_ps, silu_done, h_ready, down_ps, added = (
                m2.sem(s) for s in ("slot_ready", "gate_ps", "up_ps", "silu_done", "h_ready", "down_ps", "added"))

            @block.gpsimd
            def _(pool):
                with pool.Fori(0, EXPERTS // 2) as i:
                    for par in range(2):
                        pool.wait_ge(up_ps, (i * 2 + par) * 16 + 16)
                        for q in range(4):
                            src = wgu[:, bass.ds(i * 2 + par, 1), (q // 2) * FE:(q // 2 + 1) * FE]
                            src = src.rearrange("p e (k two) -> p (e k) two", two=2)[:, :, q % 2]
                            nc.gpsimd.tensor_copy(slot[par][:, q, :], src).then_inc(slot_ready, 1)
                        pool.wait_ge(h_ready, (i * 2 + par) * 16 + 2)
                        nc.gpsimd.tensor_copy(bias_slot[par][:], bgu[:, bass.ds(i * 2 + par, 1), :].rearrange("p e q -> p (e q)")
                                              ).then_inc(slot_ready, 1)

            @block.tensor
            def _(pe):
                def gate_up(i, par, g):
                    s = (i * 2 + par) * 8 + g
                    cols = slice(g * 512, (g + 1) * 512)
                    for c in range(2):
                        for k, banks, out_of, ready in ((0, gate, silu_done, gate_ps), (2, up, h_ready, up_ps)):
                            pe.wait_ge(out_of, s * 2 + (c + 1))
                            nc.tensor.matmul(banks[c][:], slot[par][:, k + c, :], xh[:, cols], start=True, stop=False)
                            nc.tensor.matmul(banks[c][:], slot[par][:, k + c, :], xl[:, cols], start=False, stop=True
                                             ).then_inc(ready, 1)

                def down(i, par, g):
                    s = (i * 2 + par) * 8 + g
                    pe.wait_ge(h_ready, s * 2 + 4)
                    pe.wait_ge(added, s + 1)
                    for t in range(G4):
                        for c in range(2):
                            last = nc.tensor.matmul(dn[g % 2][:, t * D:(t + 1) * D], h[:, g % 2, c, t * P:(t + 1) * P],
                                                    wdn[:, c, bass.ds(i * 2 + par, 1), :].rearrange("p e d -> p (e d)"),
                                                    start=(c == 0), stop=(c == 1))
                    last.then_inc(down_ps, 1)

                with pe.Fori(0, EXPERTS // 2) as i:
                    for par in range(2):
                        pe.wait_ge(slot_ready, (i * 2 + par) * 5 + 5)
                        for g in range(GROUPS):
                            gate_up(i, par, g)
                            if g:
                                down(i, par, g - 1)
                        down(i, par, GROUPS - 1)

            @block.scalar
            def _(act):
                nc.scalar.nop().then_inc(silu_done, 2)
                with act.Fori(0, EXPERTS // 2) as i:
                    for par in range(2):
                        for g in range(GROUPS):
                            s = (i * 2 + par) * 8 + g
                            for c in range(2):
                                act.wait_ge(gate_ps, s * 2 + (c + 1))
                                act.wait_ge(h_ready, s * 2 + (c + 1))
                                nc.scalar.activation(sil[:, c, :], gate[c][:], ACT.Silu,
                                                     bias=bias_slot[par][:, c:c + 1]).then_inc(silu_done, 1)

            @block.vector
            def _(v):
                nc.vector.nop().then_inc(h_ready, 2)
                nc.vector.nop().then_inc(added, 2)
                nc.vector.nop().then_inc(up_ps, 32)

                def hidden(i, par, g, c):
                    s = (i * 2 + par) * 8 + g
                    v.wait_ge(up_ps, s * 2 + (c + 33))
                    v.wait_ge(silu_done, s * 2 + (c + 3))
                    v.wait_ge(down_ps, s + 1)
                    nc.vector.scalar_tensor_tensor(h[:, g % 2, c, :], up[c][:], bias_slot[par][:, 2 + c:3 + c],
                                                   sil[:, c, :], ALU.add, ALU.mult).then_inc(h_ready, 1)

                def combine(i, par, g):
                    s = (i * 2 + par) * 8 + g
                    v.wait_ge(down_ps, s + 3)
                    for t in range(G4):
                        n = G4 * g + t
                        ins = nc.vector.scalar_tensor_tensor(y[:, n, :], dn[g % 2][:, t * D:(t + 1) * D],
                                                             comb[:, n, bass.ds(i * 2 + par, 1)], y[:, n, :], ALU.mult, ALU.add)
                    ins.then_inc(added, 1)

                nc.vector.nop().then_inc(down_ps, 2)
                with v.Fori(0, EXPERTS // 2) as i:
                    for par in range(2):
                        for g in range(GROUPS):
                            hidden(i, par, g, 0)
                            hidden(i, par, g, 1)
                            if g:
                                combine(i, par, g - 1)
                        combine(i, par, GROUPS - 1)

        with ExitStack() as c2:
            add_normalised(nc, c2, "ba", x, y)



def linear_attention(nc, w, x, ident):
    with ExitStack() as ctx:
        m = Memory(nc, ctx, "c")
        xn = m.sb("xn", [P, N_TILES, D])
        xT = m.sb("xT", [P, N_TILES, P])
        y = m.sb("y", [P, N_TILES, D])
        wq = m.sb("wq", [P, D])
        gram = m.sb("gram", [P, B, D])
        mix = m.sb("mix", [P, B, D])
        with ExitStack() as c2:
            normalise_rows(nc, c2, "cn", x, xn, lambda n: xT[:, n, :], ident)
        with ExitStack() as c2, nc.Block() as block:
            m2 = Memory(nc, c2, "cm")
            gb = [m2.bank(f"gram{b}") for b in range(B)]
            mb = [m2.bank(f"mix{b}") for b in range(B)]
            yb = [m2.bank(f"y{i}") for i in range(4)]
            wq_in, gram_ps, gram_out, mix_ps, mix_out, y_ps, y_out = (
                m2.sem(s) for s in ("wq_in", "gram_ps", "gram_out", "mix_ps", "mix_out", "y_ps", "y_out"))

            @block.sync
            def _(sp):
                sp.dma_start(wq[:], w["W_q"]).then_inc(wq_in, DMA)

            @block.tensor
            def _(pe):
                for b in range(B):
                    for j in range(J):
                        n = B * j + b
                        last = nc.tensor.matmul(gb[b][:, 0:D], xn[:, n, :], xn[:, n, :], start=(j == 0), stop=(j == J - 1))
                    last.then_inc(gram_ps, 1)
                pe.wait_ge(wq_in, DMA)
                for b in range(B):
                    pe.wait_ge(gram_out, b + 1)
                    nc.tensor.matmul(mb[b][:, 0:D], wq[:], gram[:, b, :], start=True, stop=True).then_inc(mix_ps, 1)
                pe.wait_ge(mix_out, B)
                for g in range(GROUPS):
                    if g >= 4:
                        pe.wait_ge(y_out, g - 3)
                    for t in range(G4):
                        n = G4 * g + t
                        last = nc.tensor.matmul(yb[g % 4][:, t * D:(t + 1) * D], xT[:, n, :], mix[:, n % B, :],
                                                start=True, stop=True)
                    last.then_inc(y_ps, 1)

            @block.scalar
            def _(act):
                for b in range(B):
                    act.wait_ge(gram_ps, b + 1)
                    nc.scalar.activation(gram[:, b, :], gb[b][:, 0:D], ACT.Copy).then_inc(gram_out, 1)
                for b in range(B):
                    act.wait_ge(mix_ps, b + 1)
                    nc.scalar.activation(mix[:, b, :], mb[b][:, 0:D], ACT.Copy).then_inc(mix_out, 1)
                for g in range(GROUPS):
                    act.wait_ge(y_ps, g + 1)
                    nc.scalar.activation(y[:, G4 * g:G4 * g + G4, :], yb[g % 4][:].rearrange("p (t d) -> p t d", t=G4),
                                         ACT.Copy).then_inc(y_out, 1)
        with ExitStack() as c2:
            add_normalised(nc, c2, "ca", x, y)


DEPTH = 6
HEADS = 16
HD = 64
INNER = HEADS * HD
WINDOW = 32
PAIRS = HEADS // 2
KEYS = WINDOW + P
FF = 341
FF_CHUNKS = [(0, 128), (128, 128), (256, FF - 256)]
MASKED = -1.0e30


def rotary_constants():
    f = np.float32
    half = np.arange(0, HD, 2, dtype=f)
    inv_freq = (f(1.0) / f(10000.0) ** (half / f(HD))).astype(f)
    t = np.arange(T, dtype=f)
    ang = (t[:, None] * inv_freq[None, :]).astype(f)
    cos, sin = np.cos(ang), np.sin(ang)
    base = ((half + f(0.4 * HD)) / f(1.4 * HD)).astype(f).astype(np.float64)
    power = ((np.arange(T) % P) - P // 2) / (WINDOW // 2)
    scale = base[None, :] ** power[:, None]
    two = lambda a: np.concatenate([a, a], -1)
    sign = np.concatenate([-np.ones(HD // 2), np.ones(HD // 2)])
    tabs = np.stack([two(cos * scale) * 8.0, two(sin * scale) * sign * 8.0,
                     two(cos / scale), two(sin / scale) * sign])
    tabs = tabs.reshape(4, J, P, HD).transpose(2, 0, 1, 3).astype(f)
    step = two((base ** (P / (WINDOW // 2)))[None, :])[0]
    decay = np.tile(step, 2).astype(f)[:, None]
    return np.ascontiguousarray(tabs), np.ascontiguousarray(decay)


def mask_constant():
    i = np.arange(P)[:, None]
    k = np.arange(KEYS)[None, :] - WINDOW
    window = np.floor_divide(i, WINDOW) * WINDOW
    seen = (k >= window - WINDOW) & (k < window + WINDOW) & (i >= k) & (i <= k + WINDOW)
    both = np.stack([seen & (k >= 0), seen])
    m = np.where(both, 0.0, MASKED).astype(np.float32).transpose(1, 0, 2)
    return np.ascontiguousarray(np.repeat(m[:, :, None, :], 2, axis=2))


def windowed_transformer(nc, w, x_outer, out):
    ctx = ExitStack()
    with ctx:
        m = Memory(nc, ctx, "d")
        xs = m.sb("xs", [P, J + 4, B, D])
        xb = m.sb("xb", [P, J, B, D // 2])
        wh = m.sb("wqkv_hi", [P, 3 * INNER], F32R)
        wl = m.sb("wqkv_lo", [P, 3 * INNER], F32R)
        wstage = m.sb("wstage", [P, 1024])
        wo = m.sb("wo", [P, PAIRS, D])
        w1raw = m.sb("w1raw", [P, 2 * FF])
        w1h = m.sb("w1_hi", [P, 2 * FF], F32R)
        w1l = m.sb("w1_lo", [P, 2 * FF], F32R)
        w2 = m.sb("w2", [P, 3, D])
        vecs = m.sb("vectors", [P, 2 + 6])
        tabs = m.sb("tables", [P, 4, (J + 1) * HD])
        qks = m.sb("qk_scale", [P, 4, HD])
        decay = m.sb("decay", [P, 1])
        mask = m.sb("mask", [P, 2, 2 * KEYS], BF16)
        ident = m.sb("ident", [P, P])
        identb = m.sb("identb", [P, P], BF16)
        magic = m.sb("magic", [P, 2 * HEADS], I32)
        kexp = [m.sb(f"k_expanded{b}", [P, PAIRS, 2, KEYS]) for b in range(B)]
        vals = [m.sb(f"v{b}", [P, 2, INNER]) for b in range(B)]

        act_t = m.sb("actT", [P, 2, 3, G4 * P])
        A = [m.bank("A0"), m.bank("A1")]
        T0, O0 = m.bank("T0"), m.bank("O0")
        S = [m.bank("S0"), m.bank("S1")]
        PT = [m.bank("PT0"), m.bank("PT1")]

        init = m.sem("init")
        waits_met = m.sem("waits_met")
        x_ln = m.sem("x_ln")

        with ExitStack() as c2, nc.Block() as block:
            m2 = Memory(nc, c2, "d0")
            maskf = m2.sb("maskf", [P, 2, 2 * KEYS])
            stats = m2.sb("stats", [P, N_TILES, 6])
            mv = m2.sb("mv", [P, N_TILES, 2])
            ve = m2.sb("ve", [P, N_TILES])
            rstd = m2.sb("rstd", [P, N_TILES])
            tmp = m2.sb("tmp", [P, N_TILES])
            magic32 = m2.sb("magic32", [P, N_TILES], I32)
            loaded, zeroed, stat, steps, mbf = (m2.sem(s) for s in ("loaded", "zeroed", "stat", "steps", "mbf"))

            @block.sync
            def _(sp):
                sp.dma_start(maskf[:], w["mask"].rearrange("p v h k -> p v (h k)")).then_inc(loaded, DMA)
                sp.dma_start(ident[:], w["ident"]).then_inc(loaded, DMA)
                sp.dma_start(decay[:], w["decay"]).then_inc(loaded, DMA)

            @block.gpsimd
            def _(pool):
                for b in range(B):
                    nc.gpsimd.memset(kexp[b][:], 0.0).then_inc(init, 1)
                nc.gpsimd.memset(tabs[:, :, J * HD:(J + 1) * HD], 0.0).then_inc(init, 1)

            @block.vector
            def _(v):
                nc.vector.memset(xs[:].rearrange("p j b d -> p (j b d)"), 0.0).then_inc(zeroed, 1)
                nc.vector.memset(magic[:], RSQRT_MAGIC + 1).then_inc(zeroed, 1)
                for b in range(B):
                    nc.vector.memset(vals[b][:], 0.0).then_inc(init, 1)
                nc.vector.memset(act_t[64:P, :, 2, :], 1.0).then_inc(init, 1)
                nc.vector.memset(magic32[:], RSQRT_MAGIC + 1).then_inc(zeroed, 1)
                for n in range(N_TILES):
                    nc.vector.bn_stats(stats[:, n, :], x_outer[:, n, :]).then_inc(stat, 1)
                v.wait_ge(stat, N_TILES)
                for n in range(N_TILES):
                    nc.vector.bn_aggr(mv[:, n, :], stats[:, n, :]).then_inc(stat, 1)
                v.wait_ge(stat, 2 * N_TILES)
                nc.vector.tensor_scalar(ve[:], mv[:, :, 1], LN_EPS, None, ALU.add).then_inc(stat, 1)
                v.wait_ge(stat, 2 * N_TILES + 1)
                v.wait_ge(zeroed, 3)
                rsqrt_steps(nc, v, ve[:], rstd[:], tmp[:], magic32[:], steps, 0, waits_met)
                v.wait_ge(steps, RSQRT_STEPS)
                for n in range(N_TILES):
                    for half, dst in ((0, xs[:, n // B, n % B, 0:64]), (1, xb[:, n // B, n % B, :])):
                        nc.vector.tensor_scalar(dst, x_outer[:, n, 64 * half:64 * half + 64], mv[:, n, 0:1],
                                                rstd[:, n:n + 1], ALU.subtract, ALU.mult).then_inc(x_ln, 1)
                v.wait_ge(loaded, 3 * DMA)
                nc.vector.tensor_copy(mask[:], maskf[:]).then_inc(mbf, 1)
                nc.vector.tensor_copy(identb[:], ident[:]).then_inc(mbf, 1)

        xcur = m.sb("x_tile", [P, D])
        xh = m.sb("xT_hi", [P, P], F32R)
        xl = m.sb("xT_lo", [P, P], F32R)
        raw = m.sb("qk", [P, 2, INNER])
        sq = m.sb("squares", [P, 2, INNER])
        sn = m.sb("sin_terms", [P, 2, INNER])
        ssq = m.sb("sum_squares", [P, 2, HEADS])
        rn = m.sb("inv_norm", [P, 2, 2, HEADS])
        rt = m.sb("newton_tmp", [P, 2 * HEADS])
        qT = m.sb("qT", [P, PAIRS, P])
        nmax = m.sb("neg_max", [P, HEADS])
        nmx = m.sb("neg_max_scaled", [P, HEADS])
        pr = m.sb("probs", [P, 2, 2, KEYS])
        den = m.sb("den", [P, HEADS])
        rden = m.sb("inv_den", [P, HEADS])
        pT = m.sb("probsT", [P, 2, 2 * P])
        pTh = m.sb("probsT_before", [P, 2, 2 * WINDOW])
        o_n = m.sb("attn", [P, INNER])
        oT = m.sb("attnT", [P, PAIRS, P])
        fst = m.sb("ff_stats", [P, G4, 6])
        fmv = m.sb("ff_mv", [P, 2, G4, 2])
        fve = m.sb("ff_ve", [P, G4])
        frs = m.sb("ff_rstd", [P, 2, G4])
        frt = m.sb("ff_tmp", [P, G4])
        xn = m.sb("ff_xn", [P, G4, D])
        fx = m.sb("ff_xT", [P, G4 * P])
        fxh = m.sb("ff_xT_hi", [P, G4 * P], F32R)
        fxl = m.sb("ff_xT_lo", [P, G4 * P], F32R)
        gl = o_n[:].rearrange("p (c t) -> p c t", c=2)
        table_probe = m.sb("table_probe", [1, 1])
        probed = m.sem("probed")

        shift_main = m.sem("shift_main")
        shift_row = m.sem("shift_row")
        w_dma = m.sem("w_dma")
        wo_dma = m.sem("wo_dma")
        small_dma = m.sem("small_dma")
        tab_dma = m.sem("tab_dma")
        w_hi, w_lo = m.sem("w_hi"), m.sem("w_lo")
        tab_ready = m.sem("tab_ready")
        w1_hi, w1_lo = m.sem("w1_hi"), m.sem("w1_lo")
        x_tile_ready = m.sem("x_tile_ready")
        xT_ps = m.sem("xT_ps")
        xh_ready, xl_ready = m.sem("xh_ready"), m.sem("xl_ready")
        proj_ps, proj_copied, proj_squared = m.sem("proj_ps"), m.sem("proj_copied"), m.sem("proj_squared")
        ssq_ready = m.sem("ssq_ready")
        ssq_floor = m.sem("ssq_floor")
        newton = m.sem("newton")
        k_cos_done, q_cos_done, sin_done, rotated = (m.sem(s) for s in ("k_cos_done", "q_cos_done", "sin_done", "rotated"))
        k_scaled = m.sem("k_scaled")
        max_found = m.sem("max_found")
        qk_T_ps = m.sem("qk_T_ps")
        q_T_ready = m.sem("q_T_ready")
        k_T_low, k_T_high = m.sem("k_T_low"), m.sem("k_T_high")
        k_before = m.sem("k_before")
        scores_ps, max_done, exp_done = m.sem("scores_ps"), m.sem("max_done"), m.sem("exp_done")
        pT_ps, pTh_ready = m.sem("pT_ps"), m.sem("pTh_ready")
        pT_first, pT_second = m.sem("pT_first"), m.sem("pT_second")
        pv_ps = m.sem("pv_ps")
        rden_ready, attn_ready = m.sem("rden_ready"), m.sem("attn_ready")
        aT_ps, aT_ready = m.sem("aT_ps"), m.sem("aT_ready")
        wo_ps, resid_a = m.sem("wo_ps"), m.sem("resid_a")
        f_stat, f_aggr, f_ve, f_newton = m.sem("f_stat"), m.sem("f_aggr"), m.sem("f_ve"), m.sem("f_newton")
        f_xn, f_xT_ps, f_xT, f_xh, f_xl = (m.sem(s) for s in ("f_xn", "f_xT_ps", "f_xT", "f_xh", "f_xl"))
        f_gate_ps, f_a_ps, f_gelu, f_act = (m.sem(s) for s in ("f_gate_ps", "f_a_ps", "f_gelu", "f_act"))
        f_out_ps, resid_f = m.sem("f_out_ps"), m.sem("resid_f")

        U = N_TILES
        MLP_LOADS = 3
        FRONTS = U + 1
        CHUNKS = (2, 3, 0, 1, 4, 5)
        XS = U + 2

        with nc.Block() as block:

            @block.sync
            def _(sp):
                def shift(j0, nj, sem):
                    sp.dma_start(xs[1:P, bass.ds(j0, nj), :, D // 2:D], xb[0:P - 1, bass.ds(j0, nj), :, :]).then_inc(sem, DMA)

                def shift_rows():
                    sp.dma_start(xs[0:1, 1:J, :, D // 2:D], xb[P - 1:P, 0:J - 1, :, :]).then_inc(shift_row, DMA)

                shift(0, J, shift_main)
                shift_rows()
                with sp.Fori(0, DEPTH) as l:
                    with sp.Fori(0, J) as j:
                        sp.wait_ge(resid_a, (l * U + j * 2) * 2 + 6)
                        shift(j, 1, shift_main)
                    sp.wait_ge(x_tile_ready, (l + 1) * XS)
                    shift_rows()
                    with sp.Fori(0, GROUPS) as g:
                        sp.wait_ge(resid_f, (l * GROUPS + g) * 2 + 6)
                        shift(g * 2, 2, shift_main)
                    shift_rows()
                sp.wait_ge(shift_main, DMA * (1 + DEPTH * (J + GROUPS)))
                sp.wait_ge(shift_row, DMA * (1 + 2 * DEPTH))

            SHIFTS = J + GROUPS

            @block.gpsimd
            def _(pool):
                def prepare_attention(l, ln):
                    for c in range(3):
                        pool.dma_start(wstage[:], w["Wqkv"][bass.ds(ln, 1), :, c * 1024:(c + 1) * 1024]
                                       .rearrange("l p n -> p (l n)")).then_inc(w_dma, DMA)
                        if c == 0:
                            pool.dma_start(wo[:], w["Wo"][bass.ds(ln, 1)].rearrange("l (c p) n -> p (l c) n", p=P)
                                           ).then_inc(wo_dma, DMA)
                            pool.dma_start(tabs[:, :, 0:J * HD], w["rotary"].rearrange("p a j d -> p a (j d)")).then_inc(tab_dma, DMA)
                            for a, name in enumerate(("q_scale", "q_swap", "k_scale", "k_swap")):
                                pool.dma_start(qks[:, a, :], w[name][bass.ds(ln, 1), :].broadcast_to([P, HD])
                                               ).then_inc(tab_dma, DMA)
                        pool.wait_ge(w_dma, (l * 3 + c + 1) * DMA)
                        sl = slice(c * 1024, (c + 1) * 1024)
                        pool.sem_inc(waits_met)
                        nc.gpsimd.tensor_copy(wh[:, sl], wstage[:]).then_inc(w_hi, 1)
                        pool.wait_ge(w_hi, upto(l, 3, c))
                        nc.gpsimd.tensor_tensor(wl[:, sl], wstage[:], wh[:, sl].bitcast(F32), ALU.subtract).then_inc(w_lo, 1)
                        pool.wait_ge(w_lo, upto(l, 3, c))
                    pool.wait_ge(tab_dma, (l + 1) * 5 * DMA)
                    for a in range(4):
                        t3 = tabs[:, a, 0:J * HD].rearrange("p (j d) -> p j d", d=HD)
                        nc.gpsimd.tensor_tensor(t3, t3, qks[:, a, :].unsqueeze(1).broadcast_to([P, J, HD]), ALU.mult
                                                ).then_inc(tab_ready, 1)

                def load_mlp(l):
                    pool.dma_start(w1raw[:], w["W1"][bass.ds(l, 1)].rearrange("l p n -> p (l n)")).then_inc(small_dma, DMA)
                    pool.dma_start(w2[:], w["W2"][bass.ds(l, 1)].rearrange("l p c n -> p (l c) n")).then_inc(small_dma, DMA)
                    pool.dma_start(vecs[:], w["vectors"][bass.ds(l, 1)].rearrange("l p n -> p (l n)")).then_inc(small_dma, DMA)

                def split_w1(l):
                    pool.wait_ge(small_dma, (l + 1) * (MLP_LOADS * DMA))
                    pool.sem_inc(waits_met)
                    nc.gpsimd.tensor_copy(w1h[:], w1raw[:]).then_inc(w1_hi, 1)
                    pool.wait_ge(w1_hi, l + 1)
                    nc.gpsimd.tensor_tensor(w1l[:], w1raw[:], w1h[:].bitcast(F32), ALU.subtract).then_inc(w1_lo, 1)

                def sin_terms(f, j, k):
                    pool.wait_ge(proj_copied, f * 6 + (l + (4 - 2 * k)))
                    pool.sem_inc(waits_met)
                    v4 = raw[:, k, :].rearrange("p (h s d) -> p h s d", h=HEADS, s=2)
                    o4 = sn[:, k, :].rearrange("p (h s d) -> p h s d", h=HEADS, s=2)
                    tab = tabs[:, 2 * k + 1, bass.ds(j * HD, HD)]
                    for s in range(2):
                        nc.gpsimd.tensor_tensor(o4[:, :, s, :], v4[:, :, 1 - s, :],
                                                tab[:, 32 * s:32 * s + 32].unsqueeze(1).broadcast_to([P, HEADS, 32]),
                                                ALU.mult).then_inc(sin_done, 1)

                def rotate(f, k):
                    pool.wait_ge(sin_done, (f * 2 + (1 - k)) * 2 + 2)
                    pool.wait_ge(k_cos_done if k else q_cos_done, f + 1)
                    nc.gpsimd.tensor_tensor(raw[:, k, :], sq[:, k, :], sn[:, k, :], ALU.add).then_inc(rotated, 1)

                def q_cos_terms(f, j):
                    pool.wait_ge(ssq_ready, f * 2 + 2)
                    pool.sem_inc(waits_met)
                    nc.gpsimd.tensor_tensor(sq[:, 0, :].rearrange("p (h d) -> p h d", d=HD),
                                            raw[:, 0, :].rearrange("p (h d) -> p h d", d=HD),
                                            tabs[:, 0, bass.ds(j * HD, HD)].unsqueeze(1).broadcast_to([P, HEADS, HD]),
                                            ALU.mult).then_inc(q_cos_done, 1)

                prepare_attention(0, 0)
                with pool.Fori(0, DEPTH) as l:
                    pool.wait_ge(shift_main, DMA * (l * SHIFTS + 1))
                    pool.wait_ge(shift_row, DMA * (2 * l + 1))
                    f0 = l * FRONTS
                    pool.sem_inc(waits_met)
                    nc.gpsimd.tensor_copy(xcur[:], xs[:, 0, 0, :]).then_inc(x_tile_ready, 1)
                    pool.wait_ge(xT_ps, l * XS + 1)
                    pool.sem_inc(waits_met)
                    nc.gpsimd.tensor_copy(xcur[:], xs[:, 0, 1, :]).then_inc(x_tile_ready, 1)
                    load_mlp(l)
                    pool.wait_ge(tab_ready, (l + 1) * 4)
                    sin_terms(f0, 0, 1)
                    sin_terms(f0, 0, 0)
                    q_cos_terms(f0, 0)
                    rotate(f0, 1)
                    rotate(f0, 0)
                    split_w1(l)
                    with pool.Fori(0, J // 2) as i:
                        for jj in range(2):
                            for b in range(B):
                                j = i * 2 + jj
                                u = j * 2 + b
                                f = f0 + (u + 1)
                                pool.wait_ge(xT_ps, l * XS + (u + 2))
                                nc.gpsimd.tensor_copy(xcur[:], xs[:, bass.ds(j + 1, 1), b, :].rearrange("p j d -> p (j d)")
                                                      ).then_inc(x_tile_ready, 1)
                                sin_terms(f, j + b, 1)
                                sin_terms(f, j + b, 0)
                                rotate(f, 1)
                                q_cos_terms(f, j + b)
                                rotate(f, 0)
                    pool.wait_ge(proj_ps, (l + 1) * (FRONTS * 6 + 1))
                    pool.wait_ge(wo_ps, (l + 1) * U)
                    pool.wait_ge(k_cos_done, (l + 1) * FRONTS)
                    pool.wait_ge(q_cos_done, (l + 1) * FRONTS)
                    pool.wait_ge(sin_done, (l + 1) * (FRONTS * 4))
                    prepare_attention(l + 1, (l + 1) % DEPTH)
                pool.wait_ge(w_lo, 3 * (DEPTH + 1))
                pool.wait_ge(tab_ready, 4 * (DEPTH + 1))
                pool.wait_ge(wo_dma, DMA * (DEPTH + 1))

            

            @block.tensor
            def _(pe):
                def transpose_x(n):
                    pe.wait_ge(x_tile_ready, n + 1)
                    nc.tensor.transpose(A[1][:, 0:P], xcur[:], ident[:]).then_inc(xT_ps, 1)

                def project(f, c, n):
                    if c == 0:
                        pe.wait_ge(xh_ready, n + 1)
                        pe.wait_ge(xl_ready, n + 1)
                    if c >= 2:
                        pe.wait_ge(proj_copied, f * 6 + (l + (c - 1)))
                        pe.wait_ge(proj_squared, f * 4 + (l + min(c - 1, 4)))
                    sl = slice(CHUNKS[c] * 512, (CHUNKS[c] + 1) * 512)
                    bank = A[(c + 1) % 2]
                    nc.tensor.matmul(bank[:], xh[:], wh[:, sl], start=True, stop=False)
                    nc.tensor.matmul(bank[:], xl[:], wh[:, sl], start=False, stop=False)
                    nc.tensor.matmul(bank[:], xh[:], wl[:, sl], start=False, stop=True).then_inc(proj_ps, 1)

                def transpose_four(bank, k, half):
                    for p in range(4):
                        col = (4 * half + p) * P
                        last = nc.tensor.transpose(bank[:, p * P:(p + 1) * P], raw[:, k, col:col + P], ident[:])
                    last.then_inc(qk_T_ps, 1)

                def transpose_q0(f):
                    pe.wait_ge(rotated, f * 2 + 2)
                    transpose_four(O0, 0, 0)

                def transpose_k0(f):
                    pe.wait_ge(q_T_ready, f * 2 + 1)
                    pe.wait_ge(k_scaled, f + 1)
                    transpose_four(O0, 1, 0)

                def transpose_q1(f):
                    transpose_four(PT[0], 0, 1)

                def transpose_k1(f):
                    transpose_four(PT[1], 1, 1)

                def scores(a, f, p, b, first_tile):
                    s = S[p % 2]
                    if p == 0:
                        pe.wait_ge(k_before, f + (l + 1))
                    if p % 4 == 0:
                        pe.wait_ge(q_T_ready, f * 2 + (1 + p // 4))
                        pe.wait_ge(k_T_low, f * 2 + (5 + p // 4))
                        pe.wait_ge(k_T_high, f * 2 + (5 + p // 4))
                    if p >= 2:
                        pe.wait_ge(exp_done, a * 16 + (2 * p - 2))
                    nc.tensor.matmul(s[:, 0:2 * KEYS], qT[:, p, :], kexp[b][:, p, :, :].rearrange("p h k -> p (h k)"),
                                     start=True, stop=False)
                    nc.tensor.matmul(s[:, 0:2 * KEYS], identb[:], mask[:, bass.ds(first_tile, 1), :].rearrange("p v k -> p (v k)"),
                                     start=False, stop=True).then_inc(scores_ps, 1)

                def wait_for_pT(a, p):
                    if p < 4:
                        pe.wait_ge(pT_first, a * 4 + (p + 1))
                    else:
                        pe.wait_ge(pT_second, a * 4 + (p - 3))

                def transpose_probs(a, f, p):
                    pe.wait_ge(exp_done, a * 16 + (2 * p + 2))
                    if p == 0:
                        pe.wait_ge(q_T_ready, f * 2 + 2)
                    if p == 1:
                        pe.wait_ge(k_T_low, f * 2 + 6)
                        pe.wait_ge(k_T_high, f * 2 + 6)
                    if p >= 2:
                        wait_for_pT(a, p - 2)
                    for h in range(2):
                        last = nc.tensor.transpose(PT[p % 2][:, h * P:(h + 1) * P], pr[:, p % 2, h, WINDOW:KEYS], ident[:])
                    last.then_inc(pT_ps, 1)

                def attend(a, p, b, jj):
                    wait_for_pT(a, p)
                    pe.wait_ge(pTh_ready, a * 8 + (p + 1))
                    if p == 4:
                        pe.wait_ge(resid_a, a * 2 + 2)
                    bank = O0 if p < 4 else T0
                    for h in range(2):
                        col = ((p % 4) * 2 + h) * HD
                        vcol = (2 * p + h) * HD
                        nc.tensor.matmul(bank[:, col:col + HD], pT[:, p % 2, h * P:(h + 1) * P],
                                         vals[b][:, jj, vcol:vcol + HD], start=True, stop=True)
                        last = nc.tensor.matmul(bank[0:WINDOW, col:col + HD],
                                                pTh[P - WINDOW:P, p % 2, h * WINDOW:(h + 1) * WINDOW],
                                                vals[b][P - WINDOW:P, 1 - jj, vcol:vcol + HD], start=False, stop=True,
                                                skip_group_check=True)
                    last.then_inc(pv_ps, 1)

                def transpose_attention(a, half):
                    pe.wait_ge(attn_ready, a * 2 + (half + 3))
                    for p in range(4):
                        col = (4 * half + p) * P
                        last = nc.tensor.transpose(A[1 - half][:, p * P:(p + 1) * P], o_n[:, col:col + P], ident[:])
                    last.then_inc(aT_ps, 1)

                def project_out(a, half):
                    pe.wait_ge(aT_ready, a * 2 + (half + 3))
                    for p in range(4 * half, 4 * half + 4):
                        last = nc.tensor.matmul(T0[:, 0:D], oT[:, p, :], wo[:, p, :], start=(p == 0), stop=(p == 7))
                    if half:
                        last.then_inc(wo_ps, 1)

                with pe.Fori(0, DEPTH) as l:
                    f0 = l * FRONTS
                    pe.wait_ge(w_hi, (l + 1) * 3)
                    pe.wait_ge(w_lo, (l + 1) * 3)
                    pe.wait_ge(wo_dma, (l + 1) * DMA)
                    transpose_x(l * XS)
                    for c in range(6):
                        project(f0, c, l * XS)
                    pe.wait_ge(proj_copied, f0 * 6 + (l + 5))
                    transpose_x(l * XS + 1)
                    transpose_q0(f0)
                    transpose_q1(f0)
                    transpose_k0(f0)
                    transpose_k1(f0)
                    project(f0 + 1, 0, l * XS + 1)
                    with pe.Fori(0, J // 2) as i:
                        for jj in range(2):
                            for b in range(B):
                                j = i * 2 + jj
                                u = j * 2 + b
                                a = l * U + u
                                f = f0 + (u + 1)
                                n = l * XS + (u + 1)
                                first_tile = (j + (J - 1)) // J
                                scores(a, f - 1, 0, b, first_tile)
                                scores(a, f - 1, 1, b, first_tile)
                                pe.wait_ge(aT_ready, a * 2 + 2)
                                project(f, 1, n)
                                for p in range(PAIRS):
                                    transpose_probs(a, f - 1, p)
                                    if p + 2 < PAIRS:
                                        scores(a, f - 1, p + 2, b, first_tile)
                                    if p < 4:
                                        project(f, p + 2, n)
                                    if p == 5:
                                        pe.wait_ge(proj_copied, f * 6 + (l + 5))
                                        transpose_x(n + 1)
                                    if p == 7:
                                        pe.wait_ge(xh_ready, n + 2)
                                        pe.wait_ge(xl_ready, n + 2)
                                        transpose_attention(a, 0)
                                    if p:
                                        attend(a, p - 1, b, jj)
                                attend(a, PAIRS - 1, b, jj)
                                transpose_q0(f)
                                transpose_q1(f)
                                pe.wait_ge(proj_copied, f * 6 + (l + 6))
                                transpose_attention(a, 1)
                                transpose_k0(f)
                                transpose_k1(f)
                                pe.wait_ge(aT_ready, a * 2 + 3)
                                project(f + 1, 0, n + 1)
                                project_out(a, 0)
                                project_out(a, 1)
                    pe.wait_ge(w1_hi, l + 1)
                    pe.wait_ge(w1_lo, l + 1)
                    pe.wait_ge(small_dma, (l + 1) * (MLP_LOADS * DMA))

                    def transpose_group(gi):
                        pe.wait_ge(f_xn, gi * 4 + 4)
                        for t in range(G4):
                            last = nc.tensor.transpose(T0[:, t * P:(t + 1) * P], xn[:, t, :], ident[:])
                        last.then_inc(f_xT_ps, 1)

                    pe.wait_ge(resid_a, (l + 1) * (U * 2) + 2)
                    pe.wait_ge(q_T_ready, (l + 1) * (FRONTS * 2))
                    pe.wait_ge(k_T_low, (l + 1) * (FRONTS * 2) + 4)
                    pe.wait_ge(k_T_high, (l + 1) * (FRONTS * 2) + 4)
                    pe.wait_ge(proj_copied, (l + 1) * (FRONTS * 6 + 1))
                    pe.wait_ge(proj_squared, (l + 1) * (FRONTS * 4 + 1))
                    m0 = l * (GROUPS + 1)
                    transpose_group(m0)

                    def hidden_units(g, gp):
                        q, mg = l * GROUPS + g, m0 + g
                        pe.wait_ge(f_xh, mg + 1)
                        pe.wait_ge(f_xl, mg + 1)
                        for c, (o, sz) in enumerate(FF_CHUNKS):
                            for k, banks, ready in ((1, S, f_gate_ps), (0, PT, f_a_ps)):
                                bank = banks[c % 2]
                                if c == 2:
                                    pe.wait_ge(f_gelu if k else f_act, q * 3 + (1 if k else 4))
                                elif k == 0 and c == 0:
                                    pe.wait_ge(f_act, q * 3 + 3)
                                sl = slice(k * FF + o, k * FF + o + sz)
                                nc.tensor.matmul(bank[0:sz, :], w1h[:, sl], fxh[:], start=True, stop=False)
                                nc.tensor.matmul(bank[0:sz, :], w1l[:, sl], fxh[:], start=False, stop=False)
                                nc.tensor.matmul(bank[0:sz, :], w1h[:, sl], fxl[:], start=False, stop=True).then_inc(ready, 1)
                        transpose_group(mg + 1)

                    def outputs(g, gp):
                        q = l * GROUPS + g
                        out_bank = (O0, A[0])[gp]
                        pe.wait_ge(resid_f, q * 2 + 2)
                        pe.wait_ge(f_act, q * 3 + 6)
                        for t in range(G4):
                            for c, (o, sz) in enumerate(FF_CHUNKS):
                                rows = sz + (c == 2)
                                last = nc.tensor.matmul(out_bank[:, t * P:(t + 1) * P], act_t[0:rows, gp, c, t * P:(t + 1) * P],
                                                        w2[0:rows, c, :], start=(c == 0), stop=(c == 2))
                        last.then_inc(f_out_ps, 1)

                    hidden_units(0, 0)
                    with pe.Fori(0, GROUPS // 2 - 1) as i:
                        for gp in range(2):
                            g = i * 2 + gp
                            hidden_units(g + 1, 1 - gp)
                            outputs(g, gp)
                    hidden_units(GROUPS - 1, 1)
                    outputs(GROUPS - 2, 0)
                    outputs(GROUPS - 1, 1)
                    pe.wait_ge(resid_f, (l + 1) * (GROUPS * 2) + 4)

            @block.scalar
            def _(act):
                def split_x(n):
                    act.wait_ge(xT_ps, n + 1)
                    nc.scalar.activation(xh[:], A[1][:, 0:P], ACT.Copy).then_inc(xh_ready, 1)

                def drain(f, c):
                    act.wait_ge(proj_ps, f * 6 + (l + (c + 1)))
                    k, half = CHUNKS[c] // 2, c % 2
                    dst = raw[:, k, half * 512:half * 512 + 512]
                    nc.scalar.activation(dst, A[(c + 1) % 2][:], ACT.Copy).then_inc(proj_copied, 1)
                    nc.scalar.activation(sq[:, k, half * 512:half * 512 + 512], A[(c + 1) % 2][:], ACT.Square
                                         ).then_inc(proj_squared, 1)

                def drain_v(f, c, b, jj):
                    act.wait_ge(proj_ps, f * 6 + (l + (c + 1)))
                    nc.scalar.activation(vals[b][:, jj, (c - 4) * 512:(c - 3) * 512], A[(c + 1) % 2][:], ACT.Copy
                                         ).then_inc(proj_copied, 1)

                def drain_q_T(f, half):
                    act.wait_ge(qk_T_ps, f * 4 + (half + 1))
                    nc.scalar.activation(qT[:, 4 * half:4 * half + 4, :], (O0, PT[0])[half][:], ACT.Copy).then_inc(q_T_ready, 1)

                def drain_k_T(f, half, b):
                    act.wait_ge(k_before, f + (l + 1))
                    act.wait_ge(qk_T_ps, f * 4 + (half + 3))
                    nc.scalar.activation(kexp[b][0:64, 4 * half:4 * half + 4, 0, WINDOW:KEYS],
                                         (O0, PT[1])[half][0:64, :].rearrange("p (c t) -> p c t", c=4), ACT.Copy
                                         ).then_inc(k_T_low, 1)

                def exps(a, p, b):
                    act.wait_ge(max_done, a * 8 + (p + 1))
                    if p >= 2:
                        act.wait_ge(pT_ps, a * 8 + (p - 1))
                        act.wait_ge(pTh_ready, a * 8 + (p - 1))
                    for h in range(2):
                        head = slice(2 * p + h, 2 * p + h + 1)
                        nc.scalar.activation(pr[:, p % 2, h, :], S[p % 2][:, h * KEYS:(h + 1) * KEYS], ACT.Exp,
                                             scale=rn[:, b, 0, head], bias=nmx[:, head], accum_out=den[:, head]
                                             ).then_inc(exp_done, 1)

                def drain_probs(a, p):
                    act.wait_ge(pT_ps, a * 8 + (p + 1))
                    act.wait_ge(pv_ps, a * 8 + (p - 1))
                    nc.scalar.activation(pT[:, p % 2, :], PT[p % 2][:, 0:2 * P], ACT.Copy).then_inc(pT_second, 1)

                def attn_T(a, half):
                    act.wait_ge(aT_ps, a * 2 + (half + 1))
                    nc.scalar.activation(oT[:, 4 * half:4 * half + 4, :], A[1 - half][:], ACT.Copy).then_inc(aT_ready, 1)

                nc.scalar.nop().then_inc(aT_ready, 2)
                nc.scalar.nop().then_inc(k_T_low, 4)
                with act.Fori(0, DEPTH) as l:
                    f0 = l * FRONTS
                    split_x(l * XS)
                    for c in range(4):
                        drain(f0, c)
                    drain_v(f0, 4, 0, 0)
                    drain_v(f0, 5, 0, 0)
                    split_x(l * XS + 1)
                    drain_q_T(f0, 0)
                    drain_q_T(f0, 1)
                    drain_k_T(f0, 0, 0)
                    drain_k_T(f0, 1, 0)
                    drain(f0 + 1, 0)
                    with act.Fori(0, J // 2) as i:
                        for jj in range(2):
                            for b in range(B):
                                u = (i * 2 + jj) * 2 + b
                                a = l * U + u
                                f = f0 + (u + 1)
                                exps(a, 0, b)
                                drain(f, 1)
                                exps(a, 1, b)
                                for p in range(PAIRS):
                                    if p >= 4:
                                        drain_probs(a, p)
                                    if p == 5:
                                        split_x(l * XS + (u + 2))
                                    if p + 2 < PAIRS:
                                        exps(a, p + 2, b)
                                    if p < 2:
                                        drain(f, p + 2)
                                    if p in (2, 3):
                                        drain_v(f, p + 2, 1 - b, (jj + b) % 2)
                                    if p == 7:
                                        attn_T(a, 0)
                                drain_q_T(f, 0)
                                drain_q_T(f, 1)
                                attn_T(a, 1)
                                drain_k_T(f, 0, 1 - b)
                                drain_k_T(f, 1, 1 - b)
                                drain(f + 1, 0)
                    def split_group(mg):
                        act.wait_ge(f_xT_ps, mg + 1)
                        nc.scalar.activation(fx[:], T0[:], ACT.Identity, scale=vecs[:, 0:1], bias=vecs[:, 1:2]).then_inc(f_xT, 1)
                        act.wait_ge(f_xT, mg + 1)
                        nc.scalar.activation(fxh[:], fx[:], ACT.Copy).then_inc(f_xh, 1)

                    act.wait_ge(small_dma, (l + 1) * (MLP_LOADS * DMA))
                    m0 = l * (GROUPS + 1)
                    split_group(m0)
                    act.wait_ge(f_xh, m0 + 1)
                    nc.scalar.activation(table_probe[:], fx[0:1, 0:1], ACT.Gelu).then_inc(probed, 1)
                    with act.Fori(0, GROUPS) as g:
                        q = l * GROUPS + g
                        for c, (o, sz) in enumerate(FF_CHUNKS):
                            act.wait_ge(f_gate_ps, q * 3 + (c + 1))
                            if c == 0:
                                act.wait_ge(f_act, q * 3 + 3)
                            if c == 2:
                                act.wait_ge(f_act, q * 3 + 4)
                            nc.scalar.activation(gl[0:sz, c % 2, :], S[c % 2][0:sz, :], ACT.Gelu,
                                                 bias=vecs[0:sz, 5 + c:6 + c]).then_inc(f_gelu, 1)
                        act.wait_ge(f_a_ps, q * 3 + 3)
                        split_group(m0 + g + 1)

            @block.vector
            def _(v):
                def split_x_low(n):
                    v.wait_ge(xh_ready, n + 1)
                    nc.vector.tensor_tensor(xl[:], A[1][:, 0:P], xh[:].bitcast(F32), ALU.subtract).then_inc(xl_ready, 1)

                def sum_squares(f, k):
                    v.wait_ge(proj_squared, f * 4 + (l + (4 - 2 * k)))
                    nc.vector.tensor_reduce(ssq[:, k, :], sq[:, k, :].rearrange("p (h d) -> p h d", d=HD), AX.X, ALU.add
                                            ).then_inc(ssq_ready, 1)

                def k_cos_terms(f, j):
                    v.wait_ge(proj_copied, f * 6 + (l + 2))
                    v.wait_ge(ssq_ready, f * 2 + 1)
                    nc.vector.tensor_tensor(sq[:, 1, :].rearrange("p (h d) -> p h d", d=HD),
                                            raw[:, 1, :].rearrange("p (h d) -> p h d", d=HD),
                                            tabs[:, 2, bass.ds(j * HD, HD)].unsqueeze(1).broadcast_to([P, HEADS, HD]),
                                            ALU.mult).then_inc(k_cos_done, 1)

                def newton_step(f, b, i):
                    sums = ssq[:].rearrange("p k h -> p (k h)")
                    if i == 0:
                        v.wait_ge(ssq_ready, f * 2 + 2)
                        nc.vector.tensor_scalar(sums, sums, 1e-24, None, ALU.max).then_inc(ssq_floor, 1)
                        return
                    if i == 1:
                        v.wait_ge(ssq_floor, f + 1)
                    rsqrt_step(nc, v, i - 1, sums, rn[:, b, :, :].rearrange("p k h -> p (k h)"), rt[:], magic[:], newton,
                               f * RSQRT_STEPS, waits_met)

                def scale_k(f, b):
                    v.wait_ge(newton, f * RSQRT_STEPS + RSQRT_STEPS)
                    v.wait_ge(rotated, f * 2 + 1)
                    r3 = raw[:, 1, :].rearrange("p (h d) -> p h d", d=HD)
                    nc.vector.tensor_tensor(r3, r3, rn[:, b, 1, :].unsqueeze(2).broadcast_to([P, HEADS, HD]), ALU.mult
                                            ).then_inc(k_scaled, 1)

                def keys_before(f, b, since):
                    v.wait_ge(k_T_low, f * 2 + since)
                    v.wait_ge(k_T_high, f * 2 + since)
                    kview = kexp[b][:].rearrange("p c h k -> p (c h) k")
                    nc.vector.tensor_scalar(kview[:, :, 0:WINDOW], kview[:, :, P:KEYS], decay[:, 0:1], None,
                                            ALU.mult).then_inc(k_before, 1)

                def drain_k_T_high(f, half, b):
                    v.wait_ge(k_before, f + (l + 1))
                    v.wait_ge(qk_T_ps, f * 4 + (half + 3))
                    nc.vector.tensor_copy(kexp[b][64:128, 4 * half:4 * half + 4, 1, WINDOW:KEYS],
                                          (O0, PT[1])[half][64:128, :].rearrange("p (c t) -> p c t", c=4)
                                          ).then_inc(k_T_high, 1)

                def find_max(a, p):
                    v.wait_ge(scores_ps, a * 8 + (p + 1))
                    nc.vector.tensor_reduce(nmax[:, 2 * p:2 * p + 2], S[p % 2][:, 0:2 * KEYS].rearrange("p (h k) -> p h k", h=2),
                                            AX.X, ALU.max, negate=True).then_inc(max_found, 1)

                def scale_max(a, p, b):
                    hs = slice(2 * p, 2 * p + 2)
                    v.wait_ge(max_found, a * 8 + (p + 1))
                    nc.vector.tensor_tensor(nmx[:, hs], nmax[:, hs], rn[:, b, 0, hs], ALU.mult).then_inc(max_done, 1)

                def drain_probs_before(a, p):
                    v.wait_ge(exp_done, a * 16 + (2 * p + 2))
                    if p >= 2:
                        v.wait_ge(pv_ps, a * 8 + (p - 1))
                    nc.vector.transpose(pTh[P - WINDOW:P, p % 2, :].rearrange("p (h k) -> p h k", h=2),
                                        pr[0:WINDOW, p % 2, :, 0:WINDOW]).then_inc(pTh_ready, 1)

                def drain_probs(a, p):
                    v.wait_ge(pT_ps, a * 8 + (p + 1))
                    nc.vector.tensor_copy(pT[:, p % 2, :], PT[p % 2][:, 0:2 * P]).then_inc(pT_first, 1)

                def normalise_attention(a, half):
                    hs = slice(8 * half, 8 * half + 8)
                    v.wait_ge(exp_done, a * 16 + (8 * half + 8))
                    nc.vector.reciprocal(rden[:, hs], den[:, hs]).then_inc(rden_ready, 1)
                    v.wait_ge(rden_ready, a * 2 + (half + 1))
                    v.wait_ge(pv_ps, a * 8 + (4 * half + 4))
                    ins = nc.vector.tensor_tensor(o_n[:, half * 512:half * 512 + 512].rearrange("p (h d) -> p h d", d=HD),
                                                  (O0, T0)[half][:].rearrange("p (h d) -> p h d", d=HD),
                                                  rden[:, hs].unsqueeze(2).broadcast_to([P, 8, HD]), ALU.mult)
                    ins.then_inc(attn_ready, 1)
                    return ins

                def residual(a, j, b):
                    v.wait_ge(wo_ps, a + 1)
                    lo = xs[:, bass.ds(j, 1), b, 0:64].rearrange("p j d -> p (j d)")
                    hi = xb[:, bass.ds(j, 1), b, :].rearrange("p j d -> p (j d)")
                    nc.vector.tensor_tensor(lo, T0[:, 0:64], lo, ALU.add).then_inc(resid_a, 1)
                    nc.vector.tensor_tensor(hi, T0[:, 64:128], hi, ALU.add).then_inc(resid_a, 1)

                nc.vector.nop().then_inc(attn_ready, 2)
                nc.vector.nop().then_inc(resid_a, 2)
                nc.vector.nop().then_inc(k_T_high, 4)
                nc.vector.nop().then_inc(resid_f, 4)
                nc.vector.nop().then_inc(f_act, 3)
                with v.Fori(0, DEPTH) as l:
                    f0 = l * FRONTS
                    v.wait_ge(tab_ready, (l + 1) * 4)
                    split_x_low(l * XS)
                    sum_squares(f0, 1)
                    k_cos_terms(f0, 0)
                    sum_squares(f0, 0)
                    for i in range(12):
                        newton_step(f0, 0, i)
                    keys_before(f0, 0, 4)
                    keys_before(f0 + 1, 1, 2)
                    split_x_low(l * XS + 1)
                    scale_k(f0, 0)
                    drain_k_T_high(f0, 0, 0)
                    drain_k_T_high(f0, 1, 0)
                    with v.Fori(0, J // 2) as i:
                        for jj in range(2):
                            for b in range(B):
                                j = i * 2 + jj
                                u = j * 2 + b
                                a = l * U + u
                                f = f0 + (u + 1)
                                for p in range(2):
                                    find_max(a, p)
                                    scale_max(a, p, b)
                                for p in range(PAIRS):
                                    step = 4 * (p - 3) if 3 <= p < 6 else None
                                    drain_probs_before(a, p)
                                    if step is not None:
                                        newton_step(f, 1 - b, step)
                                    if p < 4:
                                        drain_probs(a, p)
                                    if step is not None:
                                        newton_step(f, 1 - b, step + 1)
                                    if p + 2 < PAIRS:
                                        find_max(a, p + 2)
                                    if step is not None:
                                        newton_step(f, 1 - b, step + 2)
                                    if p + 2 < PAIRS:
                                        scale_max(a, p + 2, b)
                                    if p == 0:
                                        sum_squares(f, 1)
                                    if p == 1:
                                        k_cos_terms(f, j + b)
                                    if p == 2:
                                        sum_squares(f, 0)
                                    if p == 5:
                                        split_x_low(l * XS + (u + 2))
                                    if step is not None:
                                        newton_step(f, 1 - b, step + 3)
                                    if p == 5:
                                        normalise_attention(a, 0)
                                    if p == 7:
                                        scale_k(f, 1 - b)
                                normalise_attention(a, 1)
                                keys_before(f + 1, b, 2)
                                for half in range(2):
                                    drain_k_T_high(f, half, 1 - b)
                                residual(a, j, b)
                    def rows_of(g):
                        return xs[:, bass.ds(g * 2, 2), :, :].rearrange("p j b d -> p (j b) d")

                    def group_stats(g, ms):
                        xg = rows_of(g)
                        for t in range(G4):
                            nc.vector.bn_stats(fst[:, t, :], xg[:, t, :]).then_inc(f_stat, 1)

                    def group_variance(ms, gp):
                        v.wait_ge(f_stat, ms * 4 + 4)
                        v.sem_inc(waits_met)
                        for t in range(G4):
                            nc.vector.bn_aggr(fmv[:, gp, t, :], fst[:, t, :]).then_inc(f_aggr, 1)
                        v.wait_ge(f_aggr, ms * 4 + 4)
                        nc.vector.tensor_scalar(fve[:], fmv[:, gp, :, 1], LN_EPS, None, ALU.add).then_inc(f_ve, 1)

                    def group_rstd(ms, gp, i):
                        if i == 0:
                            v.wait_ge(f_ve, ms + 1)
                        rsqrt_step(nc, v, i, fve[:], frs[:, gp, :], frt[:], magic[:, 0:G4], f_newton, ms * RSQRT_STEPS, waits_met)

                    def group_normalise(g, ms, gp):
                        v.wait_ge(f_newton, ms * RSQRT_STEPS + RSQRT_STEPS)
                        xg = rows_of(g)
                        for t in range(G4):
                            nc.vector.tensor_scalar(xn[:, t, :], xg[:, t, :], fmv[:, gp, t, 0:1], frs[:, gp, t:t + 1],
                                                    ALU.subtract, ALU.mult).then_inc(f_xn, 1)

                    def split_group_low(mg):
                        v.wait_ge(f_xh, mg + 1)
                        nc.vector.tensor_tensor(fxl[:], fx[:], fxh[:].bitcast(F32), ALU.subtract).then_inc(f_xl, 1)

                    def gate(q, gp, c):
                        sz = FF_CHUNKS[c][1]
                        v.wait_ge(f_a_ps, q * 3 + (c + 1))
                        v.wait_ge(f_gelu, q * 3 + (c + 1))
                        nc.vector.scalar_tensor_tensor(act_t[0:sz, gp, c, :], PT[c % 2][0:sz, :], vecs[0:sz, 2 + c:3 + c],
                                                       gl[0:sz, c % 2, :], ALU.add, ALU.mult).then_inc(f_act, 1)

                    v.wait_ge(shift_main, DMA * (l * SHIFTS + (1 + J)))
                    v.wait_ge(shift_row, DMA * (2 * l + 2))
                    m0 = l * (GROUPS + 1)
                    s0 = l * (GROUPS + 2)
                    for gp in range(2):
                        group_stats(gp, s0 + gp)
                        group_variance(s0 + gp, gp)
                        for i in range(6 if gp else RSQRT_STEPS):
                            group_rstd(s0 + gp, gp, i)
                        if gp == 0:
                            group_normalise(0, s0, 0)
                    split_group_low(m0)

                    def group(g, gp, residual=True):
                        q = l * GROUPS + g
                        s1, s2 = s0 + (g + 1), s0 + (g + 2)
                        for half in range(2):
                            if residual:
                                add_outputs(g - 2, gp, half)
                            group_rstd(s1, 1 - gp, 6 + half)
                        gate(q, gp, 0)
                        for i in range(8, RSQRT_STEPS):
                            group_rstd(s1, 1 - gp, i)
                        v.wait_ge(f_xT_ps, m0 + (g + 1))
                        group_normalise(g + 1, s1, 1 - gp)
                        gate(q, gp, 1)
                        gate(q, gp, 2)
                        group_stats(g + 2, s2)
                        split_group_low(m0 + (g + 1))
                        group_variance(s2, gp)
                        for i in range(6):
                            group_rstd(s2, gp, i)

                    def add_outputs(g, gp, half):
                        v.wait_ge(f_out_ps, l * GROUPS + (g + 1))
                        o3 = (O0, A[0])[gp][:].rearrange("p (t d) -> p t d", t=G4)
                        rows = xb[:, bass.ds(g * 2, 2), :, :] if half else xs[:, bass.ds(g * 2, 2), :, 0:64]
                        rows = rows.rearrange("p j b d -> p (j b) d")
                        nc.vector.tensor_tensor(rows, o3[:, :, 64 * half:64 * half + 64], rows, ALU.add).then_inc(resid_f, 1)

                    for gp in range(2):
                        group(gp, gp, residual=False)
                    with v.Fori(1, GROUPS // 2) as i2:
                        for gp in range(2):
                            group(i2 * 2 + gp, gp)
                    for gp in range(2):
                        for half in range(2):
                            add_outputs(GROUPS - 2 + gp, gp, half)
                    for i in range(6, RSQRT_STEPS):
                        group_rstd(s0 + (GROUPS + 1), 1, i)

        with ExitStack() as c2, nc.Block() as block:
            m2 = Memory(nc, c2, "d1")
            stats = m2.sb("stats", [P, N_TILES, 2, 6])
            mv = m2.sb("mv", [P, N_TILES, 2])
            ve = m2.sb("ve", [P, N_TILES])
            rstd = m2.sb("rstd", [P, N_TILES])
            tmp = m2.sb("tmp", [P, N_TILES])
            magic32 = m2.sb("magic32", [P, N_TILES], I32)
            zeroed, stat, steps, scaled, summed, stored = (
                m2.sem(s) for s in ("zeroed", "stat", "steps", "scaled", "summed", "stored"))

            @block.vector
            def _(v):
                nc.vector.memset(magic32[:], RSQRT_MAGIC + 1).then_inc(zeroed, 1)
                for n in range(N_TILES):
                    nc.vector.bn_stats(stats[:, n, 0, :], xs[:, n // B, n % B, 0:64]).then_inc(stat, 1)
                    nc.vector.bn_stats(stats[:, n, 1, :], xb[:, n // B, n % B, :]).then_inc(stat, 1)
                v.wait_ge(stat, 2 * N_TILES)
                for n in range(N_TILES):
                    nc.vector.bn_aggr(mv[:, n, :], stats[:, n, :, :].rearrange("p a b -> p (a b)")).then_inc(stat, 1)
                v.wait_ge(stat, 3 * N_TILES)
                nc.vector.tensor_scalar(ve[:], mv[:, :, 1], LN_EPS, None, ALU.add).then_inc(stat, 1)
                v.wait_ge(stat, 3 * N_TILES + 1)
                v.wait_ge(zeroed, 1)
                rsqrt_steps(nc, v, ve[:], rstd[:], tmp[:], magic32[:], steps, 0, waits_met)
                v.wait_ge(steps, RSQRT_STEPS)
                for n in range(N_TILES):
                    for y in (xs[:, n // B, n % B, 0:64], xb[:, n // B, n % B, :]):
                        nc.vector.tensor_scalar(y, y, mv[:, n, 0:1], rstd[:, n:n + 1], ALU.subtract, ALU.mult
                                                ).then_inc(scaled, 1)
                v.wait_ge(scaled, 2 * N_TILES)
                xo = x_outer[:].rearrange("p (j b) d -> p j b d", b=B)
                for b in range(B):
                    for q in range(4):
                        js = slice(q * J // 4, (q + 1) * J // 4)
                        nc.vector.tensor_tensor(xo[:, js, b, 0:64], xo[:, js, b, 0:64], xs[:, js, b, 0:64], ALU.add
                                                ).then_inc(summed, 1)
                        nc.vector.tensor_tensor(xo[:, js, b, 64:D], xo[:, js, b, 64:D], xb[:, js, b, :], ALU.add
                                                ).then_inc(summed, 1)

            @block.sync
            def _(sp):
                xo = x_outer[:].rearrange("p (j b) d -> p j b d", b=B)
                for b in range(B):
                    for q in range(4):
                        js = slice(q * J // 4, (q + 1) * J // 4)
                        sp.wait_ge(summed, 2 * (4 * b + q + 1))
                        sp.dma_start(out[b].rearrange("(j p) d -> p j d", p=P)[:, js, :], xo[:, js, b, :]
                                     ).then_inc(stored, DMA)
                sp.wait_ge(stored, 8 * DMA)



def sandwich_program(nc, x, out, ident_in, conv_w, experts_w, linear_w, windowed_w):
    Memory.taken.clear()
    with ExitStack() as ctx:
        m = Memory(nc, ctx, "m")
        x_tiles = m.sb("x", [P, N_TILES, D])
        with ExitStack() as c1:
            m1 = Memory(nc, c1, "m1")
            ident = m1.sb("ident", [P, P])
            with nc.Block() as block:
                loaded = m1.sem("loaded")

                @block.sync
                def _(sp):
                    x4 = x_tiles[:].rearrange("p (j b) d -> p j b d", b=B)
                    for b in range(B):
                        sp.dma_start(x4[:, :, b, :], x[b].rearrange("(j p) d -> p j d", p=P)).then_inc(loaded, DMA)
                    sp.dma_start(ident[:], ident_in).then_inc(loaded, DMA)
                    sp.wait_ge(loaded, 3 * DMA)
            conv_attention_mixture(nc, conv_w, x_tiles, ident)
            fp4_experts(nc, experts_w, x_tiles, ident)
            linear_attention(nc, linear_w, x_tiles, ident)
        release_semaphores(nc)
        windowed_transformer(nc, windowed_w, x_tiles, out)


def conv_layout(a):
    head4, causal, blocks = head_constants()
    return dict(
        w_pw=a["w_pw"].T, w_dw=a["w_dw"], w_qkv=a["w_qkv"].T, w_gate=a["w_gate"].T, w_o=a["w_o"].T,
        b_gate=a["b_gate"].reshape(1, D), rope=rope_constants(), head4=head4, causal=causal, blocks=blocks,
        ln_g_b=np.stack([a["ln_g"], a["ln_b"]], 1), w1=a["w1"].transpose(2, 0, 1).reshape(D, AE * AF),
        w_moe_gate=a["w_moe_gate"].T, b2=a["b2"], b1=a["b1"].reshape(AE * AC, P).T,
        w2=a["w2"].transpose(0, 2, 1).reshape(AE, AC, P, D).transpose(2, 0, 1, 3).reshape(P, AE * AC, D))


def experts_layout(a):
    evens_first = np.concatenate([np.arange(0, D, 2), np.arange(1, D, 2)])
    return dict(
        router=a["router_w"].T[evens_first], bias_down=a["bias_down"],
        iota=np.tile(np.arange(16, dtype=np.float32), (P, 1)),
        blocks_gu=a["blocks_gu"].transpose(2, 0, 1).reshape(64, -1),
        scales_gu=a["scales_gu"].transpose(2, 0, 1).reshape(4, -1),
        blocks_down=a["blocks_down"].transpose(2, 0, 1).reshape(128, -1),
        scales_down=a["scales_down"].transpose(2, 0, 1).reshape(8, -1),
        bias_gu=a["bias_gu"].reshape(16, 2, P, 2).transpose(2, 0, 1, 3).reshape(P, 16, 4))


def windowed_layout(a):
    rotary, decay = rotary_constants()
    w2 = np.zeros((DEPTH, 3 * P, D), np.float32)
    w2[:, :FF], w2[:, FF] = a["W2"], a["b2"]
    vectors = np.zeros((DEPTH, P, 2 + 6), np.float32)
    vectors[:, :, 0], vectors[:, :, 1] = a["ln_g"], a["ln_b"]
    for c, (first, size) in enumerate(FF_CHUNKS):
        for k in range(2):
            vectors[:, :size, 2 + 3 * k + c] = a["b1"][:, k * FF + first:k * FF + first + size]
    swap = lambda s: np.concatenate([s[:, HD // 2:], s[:, :HD // 2]], 1)
    return dict(
        Wqkv=a["Wqkv"], Wo=a["Wo"], W1=a["W1"], W2=w2.reshape(DEPTH, 3, P, D).transpose(0, 2, 1, 3),
        vectors=vectors, q_scale=a["q_scale"], q_swap=swap(a["q_scale"]), k_scale=a["k_scale"],
        k_swap=swap(a["k_scale"]), rotary=rotary, decay=decay, mask=mask_constant(),
        ident=np.eye(P, dtype=np.float32))


def kernel(**inputs):
    import concourse.bacc as bacc
    from concourse.bass_utils import run_bass_kernel_spmd

    nc = bacc.Bacc("TRN2", target_bir_lowering=False, num_devices=1)
    arrays = {}

    def put(name, value):
        arrays[name] = np.ascontiguousarray(value)
        return nc.dram_tensor(name, arrays[name].shape, mybir.dt.from_np(arrays[name].dtype), kind="ExternalInput").ap()

    def stage_inputs(prefix, layout):
        mine = {n[len(prefix):]: np.asarray(v) for n, v in inputs.items() if n.startswith(prefix)}
        return {n: put(prefix + n, v) for n, v in layout(mine).items()}

    x = put("L0_attn_x", np.asarray(inputs["L0_attn_x"]))
    ident = put("identity", np.eye(P, dtype=np.float32))
    conv_w = stage_inputs("L0_attn_", conv_layout)
    experts_w = stage_inputs("L0_ffn_", experts_layout)
    linear_w = stage_inputs("L1_attn_", lambda a: a)
    windowed_w = stage_inputs("L1_ffn_", windowed_layout)
    out = nc.dram_tensor("out", (B, T, D), F32, kind="ExternalOutput").ap()
    sandwich_program(nc, x, out, ident, conv_w, experts_w, linear_w, windowed_w)
    result = run_bass_kernel_spmd(nc, [arrays], core_ids=[0])
    return result.results[0]["out"]
```
